# Optimizing a Trainium2 kernel written in Bass

```python
import numpy as np
import jax
import jax.numpy as jnp

def _softmax(x, axis=-1):
    return jax.nn.softmax(x, axis=axis)

def _gelu(x):
    return jax.nn.gelu(x, approximate=True)

def _silu(x):
    return jax.nn.silu(x)

def _sigmoid(x):
    return jax.nn.sigmoid(x)

def _layernorm(x, axis=-1, eps=1e-05):
    m = jnp.mean(x, axis=axis, keepdims=True)
    v = jnp.var(x, axis=axis, keepdims=True)
    return (x - m) / jnp.sqrt(v + eps)

def _scatter_add(tgt, idx, src, axis=0):
    return tgt.at[idx].add(src)

def _segment_sum(src, seg, n):
    return jax.ops.segment_sum(src, seg, n)
kernel_name = 'mk_gnn_preln_d4_gnn_r32_ae0229'

def setup_inputs(seed: int=0):
    np.random.seed(seed)
    _w = jnp.asarray

    def _rec_inputs():
        import jax
        import jax.numpy as jnp
        _gk = jax.random.key(seed)
        x = -0.000202 + 1 * jax.random.normal(jax.random.fold_in(_gk, 1), (3125, 128), jnp.float32)
        src = jax.random.randint(jax.random.fold_in(_gk, 2), (50000,), 0, 3125, jnp.int32)
        dst = jnp.minimum((3125 * jax.random.uniform(jax.random.fold_in(_gk, 3), (50000,)) ** 2.0).astype(jnp.int32), 99999)
        _o = jnp.argsort(dst, stable=True)
        src = src[_o]
        dst = dst[_o]
        return (x, src, dst)
    x, src, dst = _rec_inputs()

    def _L0_gnn_setup():
        import jax, jax.numpy as jnp
        import numpy as np
        N_NODES = 50000
        N_EDGES = 25000
        CHANNELS = 128
        EPS = 0.1
        key = jax.random.key(seed)
        k1, k2, k3 = jax.random.split(key, 3)
        x = jax.random.normal(k1, (N_NODES, CHANNELS), dtype=jnp.float32)
        edge_index = jax.random.randint(k2, (2, N_EDGES), 0, N_NODES, dtype=jnp.int32)
        gate_w = jax.random.normal(k3, (2 * CHANNELS, 1), dtype=jnp.float32) * (1.0 / np.sqrt(2 * CHANNELS))
        gate_b = jnp.zeros((1,), dtype=jnp.float32)
        return {'x': x, 'edge_index': edge_index, 'gate_w': gate_w, 'gate_b': gate_b}
    _L0_gnn_all = _L0_gnn_setup()
    _L0_gnn_in = {k: v for k, v in _L0_gnn_all.items() if k in ('gate_w', 'gate_b')}
    del _L0_gnn_all

    def _L1_gnn_setup():
        import jax, jax.numpy as jnp
        import numpy as np
        N_NODES = 10000
        N_EDGES = 10000
        D = 128
        H = 4
        C = 128
        L = 2
        NEG_SLOPE = 0.2
        LN_EPS = 1e-05

        def _gatv2_layer(x, src, dst, Wl, bl, Wr, br, att, b):
            n = x.shape[0]
            xl = (x @ Wl + bl).reshape(n, H, C)
            xr = (x @ Wr + br).reshape(n, H, C)
            s = jax.nn.leaky_relu(xl[src] + xr[dst], NEG_SLOPE)
            e = jnp.einsum('ehc,hc->eh', s, att)
            m = jax.ops.segment_max(e, dst, num_segments=n)
            ex = jnp.exp(e - m[dst])
            denom = jax.ops.segment_sum(ex, dst, num_segments=n)
            alpha = ex / denom[dst]
            out = jax.ops.segment_sum(alpha[:, :, None] * xl[src], dst, num_segments=n)
            return out.mean(axis=1) + b

        def _layer_norm(h, g, b):
            mu = h.mean(-1, keepdims=True)
            var = ((h - mu) ** 2).mean(-1, keepdims=True)
            return (h - mu) * jax.lax.rsqrt(var + LN_EPS) * g + b
        key = jax.random.key(seed)
        ks = jax.random.split(key, 8)
        x = jax.random.normal(ks[0], (N_NODES, D), dtype=jnp.float32)
        edge_index = jax.random.randint(ks[1], (2, N_EDGES), 0, N_NODES, dtype=jnp.int64)
        Wl = jax.random.normal(ks[2], (L, D, H * C), dtype=jnp.float32) * 0.1
        Wr = jax.random.normal(ks[3], (L, D, H * C), dtype=jnp.float32) * 0.1
        att = jax.random.normal(ks[4], (L, H, C), dtype=jnp.float32) * 0.1
        return {'x': x, 'edge_index': edge_index, 'Wl': Wl, 'bl': jnp.zeros((L, H * C), jnp.float32), 'Wr': Wr, 'br': jnp.zeros((L, H * C), jnp.float32), 'att': att, 'bias': jnp.zeros((L, D), jnp.float32), 'ln_g': jnp.ones((L, D), jnp.float32), 'ln_b': jnp.zeros((L, D), jnp.float32)}
    _L1_gnn_all = _L1_gnn_setup()
    _L1_gnn_in = {k: v for k, v in _L1_gnn_all.items() if k in ('Wl', 'bl', 'Wr', 'br', 'att', 'bias', 'ln_g', 'ln_b')}
    del _L1_gnn_all

    def _L2_gnn_setup():
        import jax, jax.numpy as jnp
        import numpy as np
        N_NODES = 10000
        N_EDGES = 20000
        D_FEAT = 128
        key = jax.random.key(seed)
        k1, k2 = jax.random.split(key)
        x = jax.random.normal(k1, (N_NODES, D_FEAT), dtype=jnp.float32)
        edge_index = jax.random.randint(k2, (2, N_EDGES), 0, N_NODES, dtype=jnp.int64)
        counts = jax.ops.segment_sum(jnp.ones((N_EDGES,), jnp.float32), edge_index[1], num_segments=N_NODES)
        deg = jnp.maximum(counts, 1.0)
        return {'x': x, 'edge_index': edge_index, 'deg': deg}
    _L2_gnn_all = _L2_gnn_setup()
    _L2_gnn_in = {k: v for k, v in _L2_gnn_all.items() if k in ()}
    del _L2_gnn_all

    def _L3_gnn_setup():
        import jax, jax.numpy as jnp
        import numpy as np
        N_NODES = 3125
        N_EDGES = 50000
        D_IN = 128
        D_H = 128

        def _sage_conv(x, src, dst, inv_deg, W_self, W_neigh, b):
            msg = jnp.take(x, src, axis=0)
            agg = jax.ops.segment_sum(msg, dst, num_segments=x.shape[0])
            agg = agg * inv_deg[:, None]
            return x @ W_self + agg @ W_neigh + b
        key = jax.random.key(seed)
        ks = jax.random.split(key, 10)
        in_feat = jax.random.normal(ks[0], (N_NODES, D_IN), dtype=jnp.float32)
        src = jax.random.randint(ks[1], (N_EDGES,), 0, N_NODES, dtype=jnp.int32)
        dst = jax.random.randint(ks[2], (N_EDGES,), 0, N_NODES, dtype=jnp.int32)
        s_in = 1.0 / np.sqrt(D_IN)
        s_h = 1.0 / np.sqrt(D_H)
        W_self1 = jax.random.normal(ks[3], (D_IN, D_H), dtype=jnp.float32) * s_in
        W_neigh1 = jax.random.normal(ks[4], (D_IN, D_H), dtype=jnp.float32) * s_in
        b1 = jnp.zeros((D_H,), dtype=jnp.float32)
        W_self2 = jax.random.normal(ks[5], (D_H, D_H), dtype=jnp.float32) * s_h
        W_neigh2 = jax.random.normal(ks[6], (D_H, D_H), dtype=jnp.float32) * s_h
        b2 = jnp.zeros((D_H,), dtype=jnp.float32)
        return {'in_feat': in_feat, 'src': src, 'dst': dst, 'W_self1': W_self1, 'W_neigh1': W_neigh1, 'b1': b1, 'W_self2': W_self2, 'W_neigh2': W_neigh2, 'b2': b2}
    _L3_gnn_all = _L3_gnn_setup()
    _L3_gnn_in = {k: v for k, v in _L3_gnn_all.items() if k in ('W_self1', 'W_neigh1', 'b1', 'W_self2', 'W_neigh2', 'b2')}
    del _L3_gnn_all
    return {'x': x, 'src': src, 'dst': dst, 'L0_gnn_gate_w': _L0_gnn_in['gate_w'], 'L0_gnn_gate_b': _L0_gnn_in['gate_b'], 'L1_gnn_Wl': _L1_gnn_in['Wl'], 'L1_gnn_bl': _L1_gnn_in['bl'], 'L1_gnn_Wr': _L1_gnn_in['Wr'], 'L1_gnn_br': _L1_gnn_in['br'], 'L1_gnn_att': _L1_gnn_in['att'], 'L1_gnn_bias': _L1_gnn_in['bias'], 'L1_gnn_ln_g': _L1_gnn_in['ln_g'], 'L1_gnn_ln_b': _L1_gnn_in['ln_b'], 'L3_gnn_W_self1': _L3_gnn_in['W_self1'], 'L3_gnn_W_neigh1': _L3_gnn_in['W_neigh1'], 'L3_gnn_b1': _L3_gnn_in['b1'], 'L3_gnn_W_self2': _L3_gnn_in['W_self2'], 'L3_gnn_W_neigh2': _L3_gnn_in['W_neigh2'], 'L3_gnn_b2': _L3_gnn_in['b2']}

def reference(x, src, dst, L0_gnn_gate_w, L0_gnn_gate_b, L1_gnn_Wl, L1_gnn_bl, L1_gnn_Wr, L1_gnn_br, L1_gnn_att, L1_gnn_bias, L1_gnn_ln_g, L1_gnn_ln_b, L3_gnn_W_self1, L3_gnn_W_neigh1, L3_gnn_b1, L3_gnn_W_self2, L3_gnn_W_neigh2, L3_gnn_b2):
    import jax
    import jax.numpy as jnp

    def _L0_gnn_ref(x, edge_index, gate_w, gate_b):
        import jax, jax.numpy as jnp
        import numpy as np
        N_NODES = 50000
        N_EDGES = 25000
        CHANNELS = 128
        EPS = 0.1
        row, col = (edge_index[0], edge_index[1])
        n = x.shape[0]
        x_row = x[row]
        x_col = x[col]
        pair = jnp.concatenate([x_row, x_col], axis=-1)
        scores = jnp.tanh(pair @ gate_w + gate_b)[:, 0]
        seg_max = jax.ops.segment_max(scores, col, num_segments=n)
        ex = jnp.exp(scores - seg_max[col])
        seg_sum = jax.ops.segment_sum(ex, col, num_segments=n)
        weights = ex / seg_sum[col]
        propagated = jax.ops.segment_sum(x_row * weights[:, None], col, num_segments=n)
        return (1.0 - EPS) * propagated + EPS * x

    def _L1_gnn_ref(x, edge_index, Wl, bl, Wr, br, att, bias, ln_g, ln_b):
        import jax, jax.numpy as jnp
        import numpy as np
        N_NODES = 10000
        N_EDGES = 10000
        D = 128
        H = 4
        C = 128
        L = 2
        NEG_SLOPE = 0.2
        LN_EPS = 1e-05

        def _gatv2_layer(x, src, dst, Wl, bl, Wr, br, att, b):
            n = x.shape[0]
            xl = (x @ Wl + bl).reshape(n, H, C)
            xr = (x @ Wr + br).reshape(n, H, C)
            s = jax.nn.leaky_relu(xl[src] + xr[dst], NEG_SLOPE)
            e = jnp.einsum('ehc,hc->eh', s, att)
            m = jax.ops.segment_max(e, dst, num_segments=n)
            ex = jnp.exp(e - m[dst])
            denom = jax.ops.segment_sum(ex, dst, num_segments=n)
            alpha = ex / denom[dst]
            out = jax.ops.segment_sum(alpha[:, :, None] * xl[src], dst, num_segments=n)
            return out.mean(axis=1) + b

        def _layer_norm(h, g, b):
            mu = h.mean(-1, keepdims=True)
            var = ((h - mu) ** 2).mean(-1, keepdims=True)
            return (h - mu) * jax.lax.rsqrt(var + LN_EPS) * g + b
        n = x.shape[0]
        loop = jnp.arange(n, dtype=edge_index.dtype)
        src = jnp.concatenate([edge_index[0], loop])
        dst = jnp.concatenate([edge_index[1], loop])
        for i in range(L):
            h = _gatv2_layer(x, src, dst, Wl[i], bl[i], Wr[i], br[i], att[i], bias[i])
            x = h + x
            x = jax.nn.relu(_layer_norm(x, ln_g[i], ln_b[i]))
        return x

    def _L2_gnn_ref(x, edge_index, deg):
        import jax, jax.numpy as jnp
        import numpy as np
        N_NODES = 10000
        N_EDGES = 20000
        D_FEAT = 128
        src, dst = (edge_index[0], edge_index[1])
        out = jax.ops.segment_sum(x[src], dst, num_segments=x.shape[0])
        return out / deg[:, None].astype(x.dtype)

    def _L3_gnn_ref(in_feat, src, dst, W_self1, W_neigh1, b1, W_self2, W_neigh2, b2):
        import jax, jax.numpy as jnp
        import numpy as np
        N_NODES = 3125
        N_EDGES = 50000
        D_IN = 128
        D_H = 128

        def _sage_conv(x, src, dst, inv_deg, W_self, W_neigh, b):
            msg = jnp.take(x, src, axis=0)
            agg = jax.ops.segment_sum(msg, dst, num_segments=x.shape[0])
            agg = agg * inv_deg[:, None]
            return x @ W_self + agg @ W_neigh + b
        n = in_feat.shape[0]
        deg = jax.ops.segment_sum(jnp.ones_like(dst, dtype=jnp.float32), dst, num_segments=n)
        inv_deg = jnp.where(deg > 0, 1.0 / jnp.maximum(deg, 1.0), 0.0)
        h = _sage_conv(in_feat, src, dst, inv_deg, W_self1, W_neigh1, b1)
        h = jax.nn.relu(h)
        h = _sage_conv(h, src, dst, inv_deg, W_self2, W_neigh2, b2)
        return h
    edge_index = jnp.stack([src, dst])
    deg = jnp.maximum(jax.ops.segment_sum(jnp.ones(dst.shape, jnp.float32), dst, num_segments=3125), 1.0)
    h = jnp.maximum(_layernorm(x, axis=-1), 0.0)
    x = x + _L0_gnn_ref(h, edge_index, L0_gnn_gate_w, L0_gnn_gate_b)
    h = jnp.maximum(_layernorm(x, axis=-1), 0.0)
    x = x + _L1_gnn_ref(h, edge_index, L1_gnn_Wl, L1_gnn_bl, L1_gnn_Wr, L1_gnn_br, L1_gnn_att, L1_gnn_bias, L1_gnn_ln_g, L1_gnn_ln_b)
    h = jnp.maximum(_layernorm(x, axis=-1), 0.0)
    x = x + _L2_gnn_ref(h, edge_index, deg)
    h = jnp.maximum(_layernorm(x, axis=-1), 0.0)
    x = x + _L3_gnn_ref(h, src, dst, L3_gnn_W_self1, L3_gnn_W_neigh1, L3_gnn_b1, L3_gnn_W_self2, L3_gnn_W_neigh2, L3_gnn_b2)
    return x

_drawn_inputs = setup_inputs


def setup_inputs(seed=0):
    import zlib

    import numpy as np

    out = dict(_drawn_inputs(seed))
    spreads = {'L1_gnn_bl': (0.0, 0.1),
     'L1_gnn_br': (0.0, 0.8),
     'L1_gnn_bias': (0.0, 0.1),
     'L1_gnn_ln_g': (1.0, 0.2),
     'L1_gnn_ln_b': (0.0, 0.1),
     'L3_gnn_b1': (0.0, 0.1),
     'L3_gnn_b2': (0.0, 0.1)}
    factors = {'L1_gnn_Wr': 3.511}
    for name, (base, spread) in spreads.items():
        noise = np.random.default_rng([zlib.crc32(name.encode()), seed]).standard_normal(out[name].shape)
        drawn = base * np.exp(spread * noise) if base else spread * noise
        out[name] = jnp.asarray(drawn.astype(out[name].dtype))
    for name, factor in factors.items():
        out[name] = (out[name] * factor).astype(out[name].dtype)
    return out
```

```python
from contextlib import ExitStack, contextmanager

import concourse.bass as bass
from concourse import mybir

F32 = mybir.dt.float32
BF16 = mybir.dt.bfloat16
I32 = mybir.dt.int32
ALU = mybir.AluOpType
ACT = mybir.ActivationFunctionType
AX = mybir.AxisListType

P = 128
N = 3125
E = 50000
C = 128
H = 4
LAYERS = 2
NODE_TILES = -(-N // P)
NODES_FULL = N // P
NODES_REST = N - NODES_FULL * P
EDGE_TILES = -(-E // P)
EDGES_FULL = E // P
EDGES_REST = E - EDGES_FULL * P
EDGE_BLOCKS = -(-EDGE_TILES // P)
SLOT_BLOCKS = 4
GROUP = 8
HALF = GROUP // 2
SLOTS = -(-(EDGE_TILES + NODE_TILES - 1) // (GROUP * SLOT_BLOCKS)) * GROUP * SLOT_BLOCKS
SB = SLOTS // SLOT_BLOCKS
ITERS = SLOTS // GROUP
HC = H * C
XLW = HC + H
XRW = HC + 2 * H
SIDE = NODE_TILES * C
BANK = 512
BANKS = 8
ACC_BANKS = -(-(SIDE + NODE_TILES * H) // BANK)
GATE = 7 * BANK
NEG = -1e30
LN_EPS = 1e-5
SLOPE = 0.2
L0_EPS = 0.1

assert SB <= P and ACC_BANKS < BANKS and SLOTS >= EDGE_TILES + NODE_TILES - 1
assert SIDE % BANK + NODE_TILES * H <= BANK


def rows_of(ap, offset, n):
    return bass.AP(ap.tensor, ap.offset + offset, [[0, P], [1, n]])


def fresh(nc, name):
    return f"{name}_{nc.next_id()}"


def linker(engine, sem):
    count = [0]

    def link(ins):
        count[0] += 1
        ins.then_inc(sem, 1)
        engine.wait_ge(sem, count[0])

    return link


@contextmanager
def phase(nc, **counts):
    s, every = {}, []
    for name, n in counts.items():
        handles = [nc.alloc_semaphore(name=fresh(nc, name)) for _ in range(n or 1)]
        every += handles
        s[name] = handles if n else handles[0]
    with nc.Block() as block:
        yield block, s
    nc.clear_and_free_semaphores(every)
    nc.all_engine_barrier()


def make_slots(nc, c, src, dst, rel_rows, dst_line):
    with ExitStack() as ctx:
        def sb(name, shape, dt=F32):
            return ctx.enter_context(nc.sbuf_tensor(fresh(nc, name), shape, dt))

        dst_i = sb("dst_i", [P, EDGE_BLOCKS, P], I32)
        src_i = sb("src_i", [P, EDGE_BLOCKS, P], I32)
        dst_f = sb("dst_f", [P, EDGE_BLOCKS, P])
        src_f = sb("src_f", [P, EDGE_BLOCKS, P])
        span_i = sb("span_i", [P, EDGE_BLOCKS, 2], I32)
        span = sb("span", [P, EDGE_BLOCKS, 2])
        tile_id = sb("tile_id", [P, EDGE_BLOCKS])
        real = sb("real", [P, EDGE_BLOCKS])
        n_slots = sb("n_slots", [P, EDGE_BLOCKS])
        n_before = sb("n_before", [P, EDGE_BLOCKS])
        first = sb("first", [P, EDGE_BLOCKS])
        end = sb("end", [P, EDGE_BLOCKS])
        shift = sb("shift", [P, EDGE_BLOCKS])
        shift_w = sb("shift_w", [P, EDGE_BLOCKS, P])
        later = sb("later", [P, P])
        from_first = sb("from_first", [P, EDGE_BLOCKS, SLOTS])
        pick = sb("pick", [P, EDGE_BLOCKS, SLOTS])
        slot_no = sb("slot_no", [P, SLOTS])
        tile_f = sb("tile_f", [P, SLOTS])
        used_off = sb("used_off", [P, SLOTS])
        dst_slot = sb("dst_slot", [P, SLOTS])
        part_1 = sb("part_1", [P, SLOTS])
        rel_row = sb("rel_row", [SB, SLOT_BLOCKS, P], BF16)
        dst_row = sb("dst_row", [SB, SLOT_BLOCKS, P])
        dst_prev = sb("dst_prev", [SB, SLOT_BLOCKS, P])
        dst_next = sb("dst_next", [SB, SLOT_BLOCKS, P])
        outside = sb("outside", [1, 1])
        any_break = sb("any_break", [SB, 2, SLOT_BLOCKS, H])
        ps = ctx.enter_context(nc.psum_tensor(fresh(nc, "slot_ps"), [P, BANKS * BANK], F32))
        PRE, SRC, DST, TIL, USE, REL, ROW, BRK = (k * BANK for k in range(BANKS))

        with phase(nc, pads=0, loads=0, iotas=0, vec=0, pe=0, row_parts=0, rows_out=0, rows_back=0) as (block, s):

            @block.gpsimd
            def _(pool):
                link = linker(pool, s["iotas"])
                link(nc.gpsimd.iota(slot_no[:, :], [[1, SLOTS]], base=0, channel_multiplier=0,
                                    allow_small_or_imprecise_dtypes=True))
                link(nc.gpsimd.iota(c.part[:, :], [[1, 1]], base=0, channel_multiplier=1,
                                    allow_small_or_imprecise_dtypes=True))
                link(nc.gpsimd.iota(tile_id[:, :], [[P, EDGE_BLOCKS]], base=0, channel_multiplier=1,
                                    allow_small_or_imprecise_dtypes=True))
                link(nc.gpsimd.memset(c.ones[:, :], 1.0))
                link(nc.gpsimd.memset(c.zeros[:, :], 0.0))
                link(nc.gpsimd.memset(outside[:, :], -5.0))

            @block.sync
            def _(sp):
                sp.wait_ge(s["pads"], 2)
                whole = EDGES_FULL // P * P
                for ap, to in ((dst, dst_i), (src, src_i)):
                    sp.dma_start(to[:, 0:whole // P, :],
                                 ap[0:whole * P].rearrange("(b p e) -> p b e", p=P, e=P)).then_inc(s["loads"], 16)
                    sp.dma_start(to[0:EDGES_FULL - whole, whole // P, :],
                                 ap[whole * P:EDGES_FULL * P].rearrange("(p e) -> p e", e=P)).then_inc(s["loads"], 16)
                    sp.dma_start(to[EDGES_FULL - whole:EDGES_FULL - whole + 1, whole // P, 0:EDGES_REST],
                                 ap[EDGES_FULL * P:E].rearrange("(a e) -> a e", a=1)).then_inc(s["loads"], 16)
                sp.wait_ge(s["row_parts"], 2)
                sp.dma_start(rel_rows[0:SLOTS * P].rearrange("(b r e) -> r b e", r=SB, e=P),
                             rel_row[:, :, :]).then_inc(s["rows_out"], 16)
                sp.dma_start(rel_rows[SLOTS * P:(SLOTS + GROUP) * P].rearrange("(r e) -> r e", e=P),
                             rel_row[0:GROUP, 0, :]).then_inc(s["rows_out"], 16)
                sp.dma_start(dst_line[1:1 + SLOTS * P].rearrange("(b r e) -> r b e", r=SB, e=P),
                             dst_row[:, :, :]).then_inc(s["rows_out"], 16)
                for at in (0, 1 + SLOTS * P):
                    sp.dma_start(dst_line[at:at + 1].rearrange("(a e) -> a e", a=1),
                                 outside[:, :]).then_inc(s["rows_out"], 16)
                sp.wait_ge(s["rows_out"], 5 * 16)
                for to, at in ((dst_prev, 0), (dst_next, 2)):
                    sp.dma_start(to[:, :, :], dst_line[at:at + SLOTS * P].rearrange("(b r e) -> r b e", r=SB, e=P))\
                      .then_inc(s["rows_back"], 16)

            @block.vector
            def _(dve):
                nc.vector.memset(dst_i[:, :, :], NODE_TILES * P - 1).then_inc(s["pads"], 1)
                nc.vector.memset(src_i[:, :, :], 0).then_inc(s["pads"], 1)
                link = linker(dve, s["vec"])
                dve.wait_ge(s["iotas"], 6)
                link(nc.vector.tensor_copy(c.iota[:, :], slot_no[:, 0:P]))
                link(nc.vector.tensor_scalar(later[:, :], slot_no[:, 0:P], c.part[:, 0:1], None, ALU.is_gt))
                link(nc.vector.tensor_scalar(c.ident[:, :], slot_no[:, 0:P], c.part[:, 0:1], None, ALU.is_equal))
                link(nc.vector.tensor_scalar(real[:, :], tile_id[:, :], float(EDGE_TILES), None, ALU.is_lt))
                dve.wait_ge(s["loads"], 6 * 16)
                link(nc.vector.tensor_copy(dst_f[:, :, :], dst_i[:, :, :]))
                link(nc.vector.tensor_copy(src_f[:, :, :], src_i[:, :, :]))
                link(nc.vector.tensor_single_scalar(span_i[:, :, :], dst_i[:, :, 0:P:P - 1], 7,
                                                    op=ALU.arith_shift_right))
                link(nc.vector.tensor_copy(span[:, :, :], span_i[:, :, :]))
                link(nc.vector.tensor_tensor(out=n_slots[:, :], in0=span[:, :, 1], in1=span[:, :, 0], op=ALU.subtract))
                link(nc.vector.scalar_tensor_tensor(out=n_slots[:, :], in0=n_slots[:, :], scalar=1.0, in1=real[:, :],
                                                    op0=ALU.add, op1=ALU.mult))
                link(nc.vector.memset(n_before[:, 0:1], 0.0))
                for b in range(1, EDGE_BLOCKS):
                    link(nc.vector.tensor_tensor(out=n_before[:, b:b + 1], in0=n_before[:, b - 1:b],
                                                 in1=n_slots[:, b - 1:b], op=ALU.add))
                dve.wait_ge(s["pe"], 1)
                link(nc.vector.tensor_copy(first[:, :], ps[:, PRE:PRE + EDGE_BLOCKS]))
                link(nc.vector.tensor_tensor(out=end[:, :], in0=first[:, :], in1=n_slots[:, :], op=ALU.add))
                link(nc.vector.tensor_tensor(out=shift[:, :], in0=span[:, :, 0], in1=first[:, :], op=ALU.subtract))
                for b in range(EDGE_BLOCKS):
                    nc.vector.tensor_scalar(shift_w[:, b, :], c.ones[:, :], shift[:, b:b + 1], None, ALU.mult)
                    link(nc.vector.tensor_scalar(from_first[:, b, :], slot_no[:, :], first[:, b:b + 1], None, ALU.is_ge))
                    link(nc.vector.scalar_tensor_tensor(out=pick[:, b, :], in0=slot_no[:, :], scalar=end[:, b:b + 1],
                                                        in1=from_first[:, b, :], op0=ALU.is_lt, op1=ALU.mult))
                dve.wait_ge(s["pe"], 2)
                link(nc.vector.tensor_tensor(out=tile_f[:, :], in0=ps[:, TIL:TIL + SLOTS], in1=slot_no[:, :], op=ALU.add))
                link(nc.vector.tensor_tensor(out=tile_f[:, :], in0=ps[:, USE:USE + SLOTS], in1=tile_f[:, :], op=ALU.mult))
                link(nc.vector.tensor_copy(c.slot_tile[0:1, :], tile_f[0:1, :]))
                link(nc.vector.memset(c.idx[:, :], 0))
                link(nc.vector.tensor_copy(c.idx[:, 0:SLOTS], ps[:, SRC:SRC + SLOTS]))
                link(nc.vector.tensor_copy(dst_slot[:, :], ps[:, DST:DST + SLOTS]))
                link(nc.vector.tensor_scalar(used_off[:, :], ps[:, USE:USE + SLOTS], 1000.0, -1000.0, ALU.mult, ALU.add))
                link(nc.vector.scalar_tensor_tensor(out=c.rel[:, :], in0=tile_f[:, :], scalar=-float(P),
                                                    in1=dst_slot[:, :], op0=ALU.mult, op1=ALU.add))
                link(nc.vector.tensor_tensor(out=c.rel[:, :], in0=c.rel[:, :], in1=used_off[:, :], op=ALU.add))
                link(nc.vector.tensor_scalar(part_1[:, :], c.rel[:, :], 0.0, None, ALU.is_ge))
                link(nc.vector.scalar_tensor_tensor(out=c.valid[:, :], in0=c.rel[:, :], scalar=float(P),
                                                    in1=part_1[:, :], op0=ALU.is_lt, op1=ALU.mult))
                link(nc.vector.tensor_scalar(c.invalid_neg[:, :], c.valid[:, :], -1.0, -NEG, ALU.add, ALU.mult))
                dve.wait_ge(s["pe"], 3)
                nc.vector.tensor_copy(rel_row[:, :, :], ps[0:SB, REL:REL + BANK].rearrange("r (b e) -> r b e", e=P))\
                  .then_inc(s["row_parts"], 1)
                nc.vector.tensor_copy(dst_row[:, :, :], ps[0:SB, ROW:ROW + BANK].rearrange("r (b e) -> r b e", e=P))\
                  .then_inc(s["row_parts"], 1)
                dve.wait_ge(s["row_parts"], 2)
                dve.wait_ge(s["rows_back"], 32)
                for k, other, own, through in ((0, dst_prev, c.brk_before, c.open_from_start),
                                               (1, dst_next, c.brk_after, c.open_to_end)):
                    link(nc.vector.tensor_tensor(out=own[:, :, :], in0=dst_row[:, :, :], in1=other[:, :, :],
                                                 op=ALU.is_equal))
                    link(nc.vector.tensor_scalar(own[:, :, :], own[:, :, :], -1.0, -NEG, ALU.add, ALU.mult))
                    for b in range(SLOT_BLOCKS):
                        step = 1 if k == 0 else -1
                        link(nc.vector.tensor_tensor_scan(out=through[:, b, ::step], data0=own[:, b, ::step],
                                                          data1=own[:, b, ::step], initial=0.0,
                                                          op0=ALU.min, op1=ALU.min))
                    edge = P - 1 if k == 0 else 0
                    for h in range(H):
                        link(nc.vector.tensor_copy(any_break[:, k, :, h], through[:, :, edge]))
                    link(nc.vector.memset(own[:, :, P - 1 - edge:P - edge], NEG))
                dve.wait_ge(s["pe"], 4)
                link(nc.vector.tensor_copy(c.slot_brk[:, 0, :], ps[0:H, BRK:BRK + SLOTS]))
                link(nc.vector.tensor_copy(c.slot_brk[:, 1, :], ps[0:H, PRE:PRE + SLOTS]))

            @block.tensor
            def _(pe):
                V = 4 + 7 + EDGE_BLOCKS - 1
                pe.wait_ge(s["vec"], V)
                nc.tensor.matmul(ps[:, PRE:PRE + EDGE_BLOCKS], later[:, :], n_slots[:, :], start=True, stop=False)
                nc.tensor.matmul(ps[:, PRE:PRE + EDGE_BLOCKS], c.ones[:, :], n_before[:, :], start=False, stop=True)\
                  .then_inc(s["pe"], 1)
                V += 3 + 2 * EDGE_BLOCKS
                pe.wait_ge(s["vec"], V)
                for b in range(EDGE_BLOCKS):
                    for at, left in ((SRC, src_f[:, b, :]), (DST, dst_f[:, b, :]), (TIL, shift_w[:, b, :]),
                                     (USE, c.ones[:, :])):
                        last = nc.tensor.matmul(ps[:, at:at + SLOTS], left, pick[:, b, :], start=b == 0,
                                                stop=b == EDGE_BLOCKS - 1)
                last.then_inc(s["pe"], 1)
                V += 12
                pe.wait_ge(s["vec"], V)
                for b in range(SLOT_BLOCKS):
                    nc.tensor.transpose(ps[0:SB, REL + b * P:REL + (b + 1) * P], c.rel[:, b * SB:(b + 1) * SB],
                                        c.ident[:, :])
                    last = nc.tensor.transpose(ps[0:SB, ROW + b * P:ROW + (b + 1) * P],
                                               dst_slot[:, b * SB:(b + 1) * SB], c.ident[:, :])
                last.then_inc(s["pe"], 1)
                pe.wait_ge(s["vec"], V + 2 * (2 + SLOT_BLOCKS + H + 1))
                for k, at in ((0, BRK), (1, PRE)):
                    for b in range(SLOT_BLOCKS):
                        last = nc.tensor.transpose(ps[0:H, at + b * SB:at + (b + 1) * SB], any_break[:, k, b, :],
                                                   c.ident[0:SB, 0:SB])
                last.then_inc(s["pe"], 1)


def norm_relu(nc, c, x, out, table=None, gain=None, shift=None, dot=None):
    ACT_TILES = 0 if gain is not None else 10
    with ExitStack() as ctx:
        stats = ctx.enter_context(nc.sbuf_tensor(fresh(nc, "stats"), [P, NODE_TILES, 6], F32))
        mean_var = ctx.enter_context(nc.sbuf_tensor(fresh(nc, "mean_var"), [P, NODE_TILES, 2], F32))
        std = ctx.enter_context(nc.sbuf_tensor(fresh(nc, "std"), [P, NODE_TILES], F32))
        rstd = ctx.enter_context(nc.sbuf_tensor(fresh(nc, "rstd"), [P, NODE_TILES], F32))
        bias = ctx.enter_context(nc.sbuf_tensor(fresh(nc, "norm_bias"), [P, NODE_TILES], F32))
        if dot is not None:
            prod = ctx.enter_context(nc.sbuf_tensor(fresh(nc, "prod"), [P, C], F32))

        with phase(nc, stats=0, var=0, std=0, scaled=0, rows=0, vec=0, dots=0, out=0) as (block, s):

            @block.vector
            def _(dve):
                link = linker(dve, s["vec"])
                for t in range(NODE_TILES):
                    nc.vector.bn_stats(stats[:, t, :], x[:, t, :]).then_inc(s["stats"], 1)
                for t in range(NODE_TILES):
                    dve.wait_ge(s["stats"], t + 1)
                    nc.vector.bn_aggr(mean_var[:, t, :], stats[:, t, :]).then_inc(s["var"], 1)
                dve.wait_ge(s["var"], NODE_TILES)
                link(nc.vector.tensor_scalar(std[:, :], mean_var[:, :, 1], LN_EPS, None, ALU.add))
                dve.wait_ge(s["std"], 1)
                link(nc.vector.reciprocal(rstd[:, :], std[:, :]))
                link(nc.vector.scalar_tensor_tensor(out=bias[:, :], in0=mean_var[:, :, 0], scalar=-1.0,
                                                    in1=rstd[:, :], op0=ALU.mult, op1=ALU.mult))
                for t in range(ACT_TILES, NODE_TILES):
                    nc.vector.tensor_scalar(out[:, t, :], x[:, t, :], rstd[:, t:t + 1], bias[:, t:t + 1],
                                            ALU.mult, ALU.add).then_inc(s["scaled"], 1)
                dve.wait_ge(s["scaled"], NODE_TILES - ACT_TILES)
                mine = out[:, ACT_TILES:NODE_TILES, :]
                if gain is not None:
                    each = [P, NODE_TILES, C]
                    link(nc.vector.tensor_tensor(out=mine, in0=mine, in1=gain.unsqueeze(1).to_broadcast(each), op=ALU.mult))
                    link(nc.vector.tensor_tensor(out=mine, in0=mine, in1=shift.unsqueeze(1).to_broadcast(each), op=ALU.add))
                nc.vector.tensor_scalar(mine, mine, 0.0, None, ALU.max).then_inc(s["rows"], 1)
                if dot is not None:
                    dve.wait_ge(s["rows"], 1 + ACT_TILES)
                    for k in range(2):
                        for t in range(NODE_TILES):
                            link(nc.vector.scalar_tensor_tensor(
                                out=prod[:, :], in0=out[:, t, :], scalar=1.0, in1=dot[0][:, k * C:(k + 1) * C],
                                op0=ALU.mult, op1=ALU.mult,
                                accum_out=dot[2][:, t:t + 1] if k else dot[1][:, t, C:C + 1]))
                        dve.sem_inc(s["dots"], 1)

            @block.scalar
            def _(act):
                act.wait_ge(s["vec"], 1)
                nc.scalar.activation(std[:, :], std[:, :], ACT.Sqrt).then_inc(s["std"], 1)
                act.wait_ge(s["vec"], 3)
                for t in range(ACT_TILES):
                    nc.scalar.activation(out[:, t, :], x[:, t, :], ACT.Relu, bias=bias[:, t:t + 1],
                                         scale=rstd[:, t:t + 1]).then_inc(s["rows"], 1)

            @block.sync
            def _(sp):
                if dot is not None:
                    sp.wait_ge(s["dots"], 1)
                    sp.dma_start(table.rearrange("(t p) c -> p t c", p=P), dot[1][:, :, :]).then_inc(s["out"], 16)
                    sp.wait_ge(s["out"], 16)
                elif table is not None:
                    sp.wait_ge(s["rows"], 1 + ACT_TILES)
                    sp.dma_start(table.rearrange("(t p) c -> p t c", p=P), out[:, :, :]).then_inc(s["out"], 16)
                    sp.wait_ge(s["out"], 16)


def first_indices(nc, c, idx_ready):
    for half in range(2):
        nc.vector.tensor_copy(c.idx_now[:, half * HALF:(half + 1) * HALF],
                              c.idx[:, half * HALF:(half + 1) * HALF]).then_inc(idx_ready[half], 1)


def gather_rows(nc, c, pool, table, width, s, filled=None):
    with pool.Fori(0, ITERS) as i:
        for u in range(GROUP):
            half = u // HALF
            if u % HALF == 0:
                pool.wait_ge(s["idx_ready"][half], i + 1)
                pool.wait_ge(s["used"], GROUP * i + (half + 1) * HALF)
            if filled is not None:
                pool.wait_ge(filled, GROUP * i + u + 1 + HALF)
            if filled is not None or u % HALF == 0:
                pool.sem_inc(s["let_go"], 1)
            nc.gpsimd.indirect_dma_start(
                out=c.rows[:, u, 0:width], out_offset=None, in_=table,
                in_offset=bass.IndirectOffsetOnAxis(ap=c.idx_now[:, u:u + 1], axis=0),
                compute_op=ALU.bypass if filled is None else ALU.add).then_inc(s["gathered"][u], 16)


def next_indices(nc, c, engine, copy, i, half, idx_ready):
    copy(c.idx_now[:, half * HALF:(half + 1) * HALF],
         c.idx[:, bass.ds((i + 1) * GROUP + half * HALF, HALF)]).then_inc(idx_ready[half], 1)


def load_tiles(nc, c, i):
    return nc.values_load_multi_w_load_instructions(
        c.slot_tile[0:1, bass.ds(i * GROUP, GROUP)], engines=[mybir.EngineType.PE], min_val=0,
        max_val=NODE_TILES - 1, skip_runtime_bounds_check_because="slots hold node tiles by construction")[1]


def clear_sums(nc, c, acc):
    for b in range(ACC_BANKS):
        last = nc.tensor.matmul(acc[:, b * BANK:(b + 1) * BANK], c.zeros[:, 0:P], c.zeros[:, :], start=True, stop=True)
    return last


def spread_rows(sp, c, rel_rows, spread, s):
    def load(first_slot, half):
        sp.dma_start(spread[:, half, :], bass.AP(rel_rows.tensor, (first_slot + half * HALF) * P,
                                                 [[0, P], [1, HALF * P]])).then_inc(s["spread"][half], 16)
    for half in range(2):
        load(0, half)
    with sp.Fori(0, ITERS) as i:
        for half in range(2):
            sp.wait_ge(s["hot_t"], 2 * i + 1 + half)
            load((i + 1) * GROUP, half)
    for half in range(2):
        sp.wait_ge(s["spread"][half], 16 * (ITERS + 1))


def gated_pass(nc, c, rel_rows, table, node_gate, gate_b, x, h):
    with ExitStack() as ctx:
        def sb(name, shape, dt=F32):
            return ctx.enter_context(nc.sbuf_tensor(fresh(nc, name), shape, dt))

        hot_t = sb("hot_t", [P, 2, HALF * P])
        spread = sb("spread", [P, 2, HALF * P], BF16)
        score = sb("score", [P, 2, HALF])
        weight = sb("weight", [P, 2, HALF])
        hot = sb("hot", [P, HALF, P])
        inv = sb("inv", [P, NODE_TILES])
        acc = ctx.enter_context(nc.psum_tensor(fresh(nc, "acc0"), [P, BANKS * BANK], F32))

        with phase(nc, idx_ready=2, used=0, let_go=0, gathered=GROUP, spread=2, hot_t=0, gate_dst=0, score=0, tanh=0,
                   weight=0, hot=0, cleared=0) as (block, s):

            @block.gpsimd
            def _(pool):
                gather_rows(nc, c, pool, table, C + 1, s)

            @block.sync
            def _(sp):
                spread_rows(sp, c, rel_rows, spread, s)

            @block.scalar
            def _(act):
                with act.Fori(0, ITERS) as i:
                    for half in range(2):
                        act.wait_ge(s["score"], 2 * i + 1 + half)
                        nc.scalar.activation(score[:, half, :], score[:, half, :], ACT.Tanh, bias=gate_b)\
                          .then_inc(s["tanh"], 1)
                        act.wait_ge(s["tanh"], 2 * i + 1 + half)
                        nc.scalar.activation(weight[:, half, :], score[:, half, :], ACT.Exp).then_inc(s["weight"], 1)

            @block.vector
            def _(dve):
                first_indices(nc, c, s["idx_ready"])
                dve.sem_inc(s["used"], GROUP)
                with dve.Fori(0, ITERS) as i:
                    for half in range(2):
                        dve.wait_ge(s["spread"][half], 16 * i + 16)
                        nc.vector.tensor_scalar(hot_t[:, half, :], spread[:, half, :], c.part[:, 0:1], None,
                                                ALU.is_equal).then_inc(s["hot_t"], 1)
                    for half in range(2):
                        q = half * HALF
                        dve.wait_ge(s["gate_dst"], 2 * i + 1 + half)
                        for u in range(q, q + HALF):
                            dve.wait_ge(s["gathered"][u], 16 * i + 16)
                        nc.vector.tensor_tensor(out=score[:, half, :], in0=acc[:, GATE + q:GATE + q + HALF],
                                                in1=c.rows[:, q:q + HALF, C], op=ALU.add).then_inc(s["score"], 1)
                        next_indices(nc, c, dve, nc.vector.tensor_copy, i, half, s["idx_ready"])
                        dve.wait_ge(s["weight"], 2 * i + 1 + half)
                        for u in range(q, q + HALF):
                            dve.wait_ge(s["used"], GROUP * i + u + 1 + GROUP - HALF)
                            nc.vector.tensor_scalar(hot[:, u % HALF, :], c.iota[:, :],
                                                    c.rel[:, bass.ds(i * GROUP + u, 1)],
                                                    weight[:, half, u % HALF:u % HALF + 1],
                                                    ALU.is_equal, ALU.mult).then_inc(s["hot"], 1)

            @block.tensor
            def _(pe):
                clear_sums(nc, c, acc).then_inc(s["cleared"], 1)
                pe.wait_ge(s["cleared"], 1)
                with pe.Fori(0, ITERS) as i:
                    tiles = load_tiles(nc, c, i)
                    for half in range(2):
                        pe.wait_ge(s["hot_t"], 2 * i + 1 + half)
                        if half:
                            pe.wait_ge(s["score"], 2 * i + 1)
                        for u in range(half * HALF, (half + 1) * HALF):
                            last = nc.tensor.matmul(acc[:, GATE + u:GATE + u + 1],
                                                    hot_t[:, half, u % HALF * P:(u % HALF + 1) * P],
                                                    node_gate[:, bass.ds(tiles[u], 1)], start=True, stop=True)
                        last.then_inc(s["gate_dst"], 1)
                    for u in range(GROUP):
                        pe.wait_ge(s["hot"], GROUP * i + u + 1)
                        nc.tensor.matmul(acc[:, bass.ds(tiles[u] * C, C)], hot[:, u % HALF, :],
                                         c.rows[:, u, 0:C], start=False, stop=False, skip_group_check=True)
                        nc.tensor.matmul(acc[:, bass.ds(tiles[u] + SIDE, 1)], hot[:, u % HALF, :],
                                         c.ones[:, 0:1], start=False, stop=False, skip_group_check=True)\
                          .then_inc(s["used"], 1)

        with phase(nc, vec=0, tile=0) as (block, s):

            @block.vector
            def _(dve):
                link = linker(dve, s["vec"])
                link(nc.vector.tensor_scalar(inv[:, :], acc[:, SIDE:SIDE + NODE_TILES], 1e-30, None, ALU.max))
                link(nc.vector.reciprocal(inv[:, :], inv[:, :]))
                link(nc.vector.tensor_scalar(inv[:, :], inv[:, :], 1.0 - L0_EPS, None, ALU.mult))
                link(nc.vector.scalar_tensor_tensor(out=x[:, :, :], in0=h[:, :, :], scalar=L0_EPS, in1=x[:, :, :],
                                                    op0=ALU.mult, op1=ALU.add))
                for t in range(NODE_TILES):
                    nc.vector.scalar_tensor_tensor(out=x[:, t, :], in0=acc[:, t * C:(t + 1) * C],
                                                   scalar=inv[:, t:t + 1], in1=x[:, t, :],
                                                   op0=ALU.mult, op1=ALU.add).then_inc(s["tile"], 1)


def neighbour_pass(nc, c, table, acc, count_edges):
    with nc.sbuf_tensor(fresh(nc, "hot_n"), [P, HALF, P], F32) as hot:
        with phase(nc, idx_ready=2, used=0, let_go=0, gathered=GROUP, hot=0, cleared=0) as (block, s):

            @block.gpsimd
            def _(pool):
                gather_rows(nc, c, pool, table, C, s)

            @block.scalar
            def _(act):
                with act.Fori(0, ITERS) as i:
                    for half in range(2):
                        for u in range(half * HALF, (half + 1) * HALF):
                            act.wait_ge(s["gathered"][u], 16 * i + 16)
                        next_indices(nc, c, act, nc.scalar.copy, i, half, s["idx_ready"])

            @block.vector
            def _(dve):
                first_indices(nc, c, s["idx_ready"])
                dve.sem_inc(s["used"], GROUP)
                with dve.Fori(0, ITERS) as i:
                    for u in range(GROUP):
                        dve.wait_ge(s["used"], GROUP * i + u + 1 + GROUP - HALF)
                        nc.vector.tensor_scalar(hot[:, u % HALF, :], c.iota[:, :],
                                                c.rel[:, bass.ds(i * GROUP + u, 1)], None,
                                                ALU.is_equal).then_inc(s["hot"], 1)

            @block.tensor
            def _(pe):
                clear_sums(nc, c, acc).then_inc(s["cleared"], 1)
                pe.wait_ge(s["cleared"], 1)
                with pe.Fori(0, ITERS) as i:
                    tiles = load_tiles(nc, c, i)
                    for u in range(GROUP):
                        pe.wait_ge(s["hot"], GROUP * i + u + 1)
                        if count_edges:
                            nc.tensor.matmul(acc[:, bass.ds(tiles[u] + SIDE, 1)], hot[:, u % HALF, :],
                                             c.ones[:, 0:1], start=False, stop=False, skip_group_check=True)
                        pe.wait_ge(s["gathered"][u], 16 * i + 16)
                        nc.tensor.matmul(acc[:, bass.ds(tiles[u] * C, C)], hot[:, u % HALF, :],
                                         c.rows[:, u, 0:C], start=False, stop=False, skip_group_check=True)\
                          .then_inc(s["used"], 1)


def gat_weights(nc, c, g, layer, Wl, Wr, bl, br, att, bias, ln_g, ln_b):
    with nc.sbuf_tensor(fresh(nc, "prod_w"), [P, C], F32) as prod, nc.sbuf_tensor(fresh(nc, "bl_all"), [P, HC], F32) as bl_all:
        with phase(nc, loads=0, vec=0) as (block, s):

            @block.sync
            def _(sp):
                sp.dma_start(g.w[0][:, 0:HC], Wl[layer, :, :]).then_inc(s["loads"], 16)
                sp.dma_start(g.w[1][:, 0:HC], Wr[layer, :, :]).then_inc(s["loads"], 16)
                sp.dma_start(g.att[:, :], rows_of(att, layer * HC, HC)).then_inc(s["loads"], 16)
                sp.dma_start(bl_all[:, :], rows_of(bl, layer * HC, HC)).then_inc(s["loads"], 16)
                sp.dma_start(g.b_sum[:, 0:HC], rows_of(br, layer * HC, HC)).then_inc(s["loads"], 16)
                sp.dma_start(g.b_out[:, :], rows_of(bias, layer * C, C)).then_inc(s["loads"], 16)
                sp.dma_start(g.gain[:, :], rows_of(ln_g, layer * C, C)).then_inc(s["loads"], 16)
                sp.dma_start(g.shift[:, :], rows_of(ln_b, layer * C, C)).then_inc(s["loads"], 16)

            @block.vector
            def _(dve):
                link = linker(dve, s["vec"])
                dve.wait_ge(s["loads"], 8 * 16)
                link(nc.vector.tensor_tensor(out=g.b_sum[:, 0:HC], in0=g.b_sum[:, 0:HC], in1=bl_all[:, :], op=ALU.add))
                for m in (g.w[0], g.w[1], g.b_sum):
                    for h in range(H):
                        link(nc.vector.scalar_tensor_tensor(
                            out=prod[:, :], in0=m[:, h * C:(h + 1) * C], scalar=SLOPE, in1=g.att[:, h * C:(h + 1) * C],
                            op0=ALU.mult, op1=ALU.mult, accum_out=m[:, HC + h:HC + h + 1]))
                for h in range(H):
                    link(nc.vector.scalar_tensor_tensor(out=g.b_out[:, :], in0=bl_all[:, h * C:(h + 1) * C],
                                                        scalar=1.0 / H, in1=g.b_out[:, :], op0=ALU.mult, op1=ALU.add))


def gat_tables(nc, c, g, h, xl_table):
    U = 5
    with ExitStack() as ctx:
        h_t = ctx.enter_context(nc.sbuf_tensor(fresh(nc, "h_t"), [P, 2, P], F32))
        part = ctx.enter_context(nc.sbuf_tensor(fresh(nc, "self_part"), [P, U, H], F32))
        ps = ctx.enter_context(nc.psum_tensor(fresh(nc, "tab_ps"), [P, BANKS * BANK], F32))
        assert NODE_TILES % U == 0
        pairs = [[(u % 2 * 4 + 2 * k) * BANK for k in range(2)] for u in range(U)]

        with phase(nc, turned=0, h_t=0, proj=0, xl=0, xr=0, z=0, parts=0, z_used=0, stored=0) as (block, s):

            @block.tensor
            def _(pe):
                for t in range(NODE_TILES):
                    u = t % U
                    at = pairs[u]
                    pe.wait_ge(s["xl"], t + 1 + (u == 0))
                    pe.wait_ge(s["xr"], t + 1 + (u == 0))
                    nc.tensor.transpose(ps[:, at[0] + BANK + P:at[0] + BANK + 2 * P], h[:, t, :],
                                        c.ident[:, :]).then_inc(s["turned"], 1)
                    pe.wait_ge(s["h_t"], t + 1)
                    for k in range(2):
                        nc.tensor.matmul(ps[:, at[k]:at[k] + BANK], h_t[:, u % 2, :], g.w[k][:, 0:HC],
                                         start=True, stop=True)
                        last = nc.tensor.matmul(ps[:, at[k] + BANK:at[k] + BANK + H], h_t[:, u % 2, :],
                                                g.w[k][:, HC:XLW], start=True, stop=True)
                    last.then_inc(s["proj"], 1)

            @block.scalar
            def _(act):
                act.sem_inc(s["xl"], 2)
                with act.Fori(0, NODE_TILES // U) as i:
                    for u in range(U):
                        t = i * U + u
                        at = pairs[u]
                        act.wait_ge(s["turned"], t + 1)
                        nc.scalar.copy(h_t[:, u % 2, :], ps[:, at[0] + BANK + P:at[0] + BANK + 2 * P])\
                          .then_inc(s["h_t"], 1)
                        act.wait_ge(s["proj"], t + 1)
                        nc.scalar.copy(g.xl[:, bass.ds(t, 1), :].rearrange("p a c -> p (a c)"),
                                       ps[:, at[0]:at[0] + XLW]).then_inc(s["xl"], 1)

            @block.gpsimd
            def _(pool):
                with pool.Fori(0, NODE_TILES // U) as i:
                    for u in range(U):
                        t = i * U + u
                        pool.wait_ge(s["xl"], t + 3)
                        pool.wait_ge(s["xr"], t + 3)
                        pool.wait_ge(s["z_used"], t + 1)
                        nc.gpsimd.tensor_tensor(out=c.rows[:, u, 0:XLW],
                                                in0=g.xl[:, bass.ds(t, 1), :].rearrange("p a c -> p (a c)"),
                                                in1=g.xr[:, bass.ds(t, 1), 0:XLW].rearrange("p a c -> p (a c)"),
                                                op=ALU.add).then_inc(s["z"], 1)

            @block.vector
            def _(dve):
                dve.sem_inc(s["xr"], 2)
                dve.sem_inc(s["z_used"], U)
                with dve.Fori(0, NODE_TILES // U) as i:
                    for u in range(U):
                        t = i * U + u
                        dve.wait_ge(s["proj"], t + 1)
                        nc.vector.tensor_tensor(out=g.xr[:, bass.ds(t, 1), 0:XLW].rearrange("p a c -> p (a c)"),
                                                in0=ps[:, pairs[u][1]:pairs[u][1] + XLW], in1=g.b_sum[:, :],
                                                op=ALU.add).then_inc(s["xr"], 1)
                    for u in range(U):
                        t = i * U + u
                        dve.wait_ge(s["z"], t + 1)
                        relu_scores(nc, g, c.rows[:, u, :], part[:, u, :]).then_inc(s["parts"], 1)
                    for u in range(U):
                        t = i * U + u
                        dve.wait_ge(s["parts"], t + 1)
                        nc.vector.scalar_tensor_tensor(
                            out=g.xr[:, bass.ds(t, 1), XLW:XRW].rearrange("p a c -> p (a c)"), in0=part[:, u, :],
                            scalar=1.0 - SLOPE, in1=c.rows[:, u, HC:XLW],
                            op0=ALU.mult, op1=ALU.add).then_inc(s["z_used"], 1)

            @block.sync
            def _(sp):
                with sp.Fori(0, NODE_TILES) as t:
                    sp.wait_ge(s["xl"], t + 3)
                    sp.dma_start(xl_table[bass.ds(t * P, P), :],
                                 g.xl[:, bass.ds(t, 1), :].rearrange("p a c -> p (a c)")).then_inc(s["stored"], 16)
                sp.wait_ge(s["stored"], 16 * NODE_TILES)


def relu_scores(nc, g, z, part):
    for h in range(H):
        last = nc.vector.scalar_tensor_tensor(out=z[:, h * C:(h + 1) * C], in0=z[:, h * C:(h + 1) * C], scalar=0.0,
                                              in1=g.att[:, h * C:(h + 1) * C], op0=ALU.max, op1=ALU.mult,
                                              accum_out=part[:, h:h + 1])
    return last


def gat_scores(nc, c, g, rel_rows, xl_table):
    PSB = 4
    with ExitStack() as ctx:
        hot_t = ctx.enter_context(nc.sbuf_tensor(fresh(nc, "hot_ta"), [P, 2, HALF * P], F32))
        spread = ctx.enter_context(nc.sbuf_tensor(fresh(nc, "spread_a"), [P, 2, HALF * P], BF16))
        part = ctx.enter_context(nc.sbuf_tensor(fresh(nc, "edge_part"), [P, 2, HALF, H], F32))
        ps = ctx.enter_context(nc.psum_tensor(fresh(nc, "xr_ps"), [P, PSB, 2 * BANK], F32))
        assert PSB == HALF

        with phase(nc, idx_ready=2, used=0, let_go=0, gathered=GROUP, spread=2, hot_t=0, xr=0, placed=0, parts=0) as (block, s):

            @block.gpsimd
            def _(pool):
                gather_rows(nc, c, pool, xl_table, XLW, s, filled=s["placed"])

            @block.sync
            def _(sp):
                spread_rows(sp, c, rel_rows, spread, s)

            @block.tensor
            def _(pe):
                with pe.Fori(0, ITERS) as i:
                    tiles = load_tiles(nc, c, i)
                    for u in range(GROUP):
                        if u % HALF == 0:
                            pe.wait_ge(s["hot_t"], 2 * i + 1 + u // HALF)
                        pe.wait_ge(s["placed"], GROUP * i + u + 1)
                        left = hot_t[:, u // HALF, u % HALF * P:(u % HALF + 1) * P]
                        xr = g.xr[:, bass.ds(tiles[u], 1), :].rearrange("p a c -> p (a c)")
                        nc.tensor.matmul(ps[:, u % PSB, 0:BANK], left, xr[:, 0:BANK], start=True, stop=True)
                        nc.tensor.matmul(ps[:, u % PSB, BANK:XRW], left, xr[:, BANK:XRW], start=True, stop=True)\
                          .then_inc(s["xr"], 1)

            @block.scalar
            def _(act):
                act.sem_inc(s["placed"], PSB)
                with act.Fori(0, ITERS) as i:
                    for u in range(GROUP):
                        if u % HALF == 0:
                            act.wait_ge(s["used"], GROUP * i + u + HALF)
                        act.wait_ge(s["xr"], GROUP * i + u + 1)
                        nc.scalar.copy(c.rows[:, u, 0:XRW], ps[:, u % PSB, 0:XRW]).then_inc(s["placed"], 1)

            @block.vector
            def _(dve):
                def one_hot(spread_count, half):
                    dve.wait_ge(s["spread"][half], spread_count)
                    nc.vector.tensor_scalar(hot_t[:, half, :], spread[:, half, :], c.part[:, 0:1], None,
                                            ALU.is_equal).then_inc(s["hot_t"], 1)

                first_indices(nc, c, s["idx_ready"])
                dve.sem_inc(s["used"], GROUP)
                for half in range(2):
                    one_hot(16, half)
                with dve.Fori(0, ITERS) as i:
                    for half in range(2):
                        q = half * HALF
                        dve.wait_ge(s["used"], GROUP * i + q + HALF)
                        for u in range(q, q + HALF):
                            dve.wait_ge(s["gathered"][u], 16 * i + 16)
                            relu_scores(nc, g, c.rows[:, u, :], part[:, half, u % HALF, :]).then_inc(s["parts"], 1)
                        next_indices(nc, c, dve, nc.vector.tensor_copy, i, half, s["idx_ready"])
                        one_hot(16 * i + 32, half)
                        at = bass.ds(i * GROUP + q, HALF)
                        nc.vector.tensor_copy(c.e_self[:, at, :], c.rows[:, q:q + HALF, XLW:XRW])
                        dve.wait_ge(s["parts"], GROUP * i + q + HALF)
                        nc.vector.scalar_tensor_tensor(out=c.e[:, at, :], in0=part[:, half, :, :], scalar=1.0 - SLOPE,
                                                       in1=c.rows[:, q:q + HALF, HC:XLW], op0=ALU.mult,
                                                       op1=ALU.add).then_inc(s["used"], HALF)


def gat_softmax(nc, c, scratch):
    ROWS = SLOT_BLOCKS * H * P
    flat = scratch.rearrange("p t c -> p (t c)")

    def part(k):
        return flat[0:SB, k * ROWS:(k + 1) * ROWS]

    def split(ap):
        return ap.rearrange("r (b h e) -> r b h e", b=SLOT_BLOCKS, h=H)

    def over_heads(brk):
        return brk.unsqueeze(2).to_broadcast([SB, SLOT_BLOCKS, H, P])

    er, es, run, more, brk_f, brk_b = (part(k) for k in range(6))
    with ExitStack() as ctx:
        carry = ctx.enter_context(nc.sbuf_tensor(fresh(nc, "carry"), [SB, SLOT_BLOCKS * H], F32))
        ends = ctx.enter_context(nc.sbuf_tensor(fresh(nc, "ends"), [SB, SLOT_BLOCKS * H], F32))
        over = ctx.enter_context(nc.sbuf_tensor(fresh(nc, "over"), [H, SLOTS + 2], F32))
        slot_keep = ctx.enter_context(nc.sbuf_tensor(fresh(nc, "slot_keep"), [H, SLOTS], F32))
        ps = ctx.enter_context(nc.psum_tensor(fresh(nc, "soft_ps"), [P, BANKS * BANK], F32))

        with phase(nc, masked=0, turned=0, rows=0, ends=0, slots=0, over=0, carried=0, pick=0, ex=0, vec=0, breaks=0,
                   alpha=0, back=0) as (block, s):

            @block.tensor
            def _(pe):
                for n, e in enumerate((c.e, c.e_self)):
                    if n == 0:
                        pe.wait_ge(s["masked"], 1)
                    for b in range(SLOT_BLOCKS):
                        for h in range(H):
                            at = n * ROWS + (b * H + h) * P
                            last = nc.tensor.transpose(ps[0:SB, at:at + P], e[:, b * SB:(b + 1) * SB, h], c.ident[:, :])
                    last.then_inc(s["turned"], 1)
                pe.wait_ge(s["rows"], 2)
                for n in range(4):
                    pe.wait_ge(s["ends"], n + 1)
                    for b in range(SLOT_BLOCKS):
                        last = nc.tensor.transpose(ps[0:H, b * SB:(b + 1) * SB], ends[:, b * H:(b + 1) * H],
                                                   c.ident[0:SB, 0:SB])
                    last.then_inc(s["slots"], 1)
                    pe.wait_ge(s["over"], n + 1)
                    back = n % 2 * 2
                    for b in range(SLOT_BLOCKS):
                        last = nc.tensor.transpose(ps[0:SB, BANK + b * H:BANK + (b + 1) * H],
                                                   over[:, back + b * SB:back + (b + 1) * SB], c.ident[0:H, 0:H])
                    last.then_inc(s["carried"], 1)
                pe.wait_ge(s["alpha"], 1)
                for h in range(H):
                    for b in range(SLOT_BLOCKS):
                        at = (2 + h) * BANK + b * SB
                        last = nc.tensor.transpose(ps[:, at:at + SB], part(1)[:, (b * H + h) * P:(b * H + h + 1) * P],
                                                   c.ident[0:SB, 0:SB])
                last.then_inc(s["back"], 1)

            @block.scalar
            def _(act):
                for n, to in enumerate((er, es)):
                    act.wait_ge(s["turned"], n + 1)
                    nc.scalar.copy(to, ps[0:SB, n * ROWS:(n + 1) * ROWS]).then_inc(s["rows"], 1)
                for n, x in enumerate((er, es)):
                    act.wait_ge(s["pick"], n + 1)
                    nc.scalar.activation(x, x, ACT.Exp).then_inc(s["ex"], 1)
                act.wait_ge(s["back"], 1)
                for h in range(H):
                    nc.scalar.copy(c.e[:, 0:SLOTS, h], ps[:, (2 + h) * BANK:(2 + h) * BANK + SLOTS])

            @block.gpsimd
            def _(pool):
                nc.gpsimd.tensor_copy(split(brk_f), over_heads(c.brk_before[:, :, :])).then_inc(s["breaks"], 1)
                nc.gpsimd.tensor_copy(split(brk_b), over_heads(c.brk_after[:, :, :])).then_inc(s["breaks"], 1)

            @block.vector
            def _(dve):
                link = linker(dve, s["vec"])
                each = [P, SLOTS, H]
                link(nc.vector.tensor_tensor(out=c.e[:, 0:SLOTS, :], in0=c.e[:, 0:SLOTS, :],
                                             in1=c.valid[:, :].unsqueeze(2).to_broadcast(each), op=ALU.mult))
                nc.vector.tensor_tensor(out=c.e[:, 0:SLOTS, :], in0=c.e[:, 0:SLOTS, :],
                                        in1=c.invalid_neg[:, :].unsqueeze(2).to_broadcast(each), op=ALU.add)\
                  .then_inc(s["masked"], 1)
                link(nc.vector.memset(over[:, :], 0.0))
                link(nc.vector.tensor_scalar(slot_keep[:, :], c.slot_brk[:, 0, :], 0.0, None, ALU.is_equal))

                def scan(n, values, brk, through, backward, total=False):
                    step = -1 if backward else 1
                    op0, op1, start = (ALU.mult, ALU.add, 0.0) if total else (ALU.add, ALU.max, NEG)
                    link(nc.vector.tensor_tensor_scan(out=run[:, ::step], data0=brk[:, ::step],
                                                      data1=values[:, ::step], initial=start, op0=op0, op1=op1))
                    nc.vector.tensor_copy(ends[:, :], split(run)[:, :, :, 0 if backward else P - 1]
                                          .rearrange("r b h -> r (b h)")).then_inc(s["ends"], 1)
                    dve.wait_ge(s["slots"], n + 1)
                    link(nc.vector.memset(over[:, :], start))
                    brk_slot = slot_keep[:, :] if total else c.slot_brk[:, int(backward), :]
                    nc.vector.tensor_tensor_scan(out=over[:, 1:1 + SLOTS][:, ::step], data0=brk_slot[:, ::step],
                                                 data1=ps[0:H, 0:SLOTS][:, ::step], initial=start,
                                                 op0=op0, op1=op1).then_inc(s["over"], 1)
                    dve.wait_ge(s["carried"], n + 1)
                    link(nc.vector.tensor_copy(carry[:, :], ps[0:SB, BANK:BANK + SLOT_BLOCKS * H]))
                    wide = carry[:, :].rearrange("r (b h) -> r b h", h=H).unsqueeze(3)\
                        .to_broadcast([SB, SLOT_BLOCKS, H, P])
                    if total:
                        link(nc.vector.tensor_scalar(more, more, 0.0, None, ALU.is_equal))
                        link(nc.vector.tensor_tensor(out=split(more), in0=split(more), in1=wide, op=ALU.mult))
                        link(nc.vector.tensor_tensor(out=run, in0=run, in1=more, op=ALU.add))
                    else:
                        link(nc.vector.tensor_tensor(out=split(more), in0=over_heads(through), in1=wide, op=ALU.add))
                        link(nc.vector.tensor_tensor(out=run, in0=run, in1=more, op=ALU.max))

                dve.wait_ge(s["breaks"], 2)
                dve.wait_ge(s["rows"], 2)
                scan(0, er, brk_f, c.open_from_start[:, :, :], False)
                scan(1, run, brk_b, c.open_to_end[:, :, :], True)
                link(nc.vector.tensor_tensor(out=run, in0=run, in1=es, op=ALU.max))
                nc.vector.tensor_tensor(out=er, in0=er, in1=run, op=ALU.subtract).then_inc(s["pick"], 1)
                nc.vector.tensor_tensor(out=es, in0=es, in1=run, op=ALU.subtract).then_inc(s["pick"], 1)
                link(nc.vector.tensor_scalar(brk_f, brk_f, 0.0, None, ALU.is_equal))
                link(nc.vector.tensor_copy(split(more), over_heads(c.open_from_start[:, :, :])))
                dve.wait_ge(s["ex"], 2)
                scan(2, er, brk_f, None, False, total=True)
                scan(3, run, brk_b, c.open_to_end[:, :, :], True)
                link(nc.vector.tensor_tensor(out=run, in0=run, in1=es, op=ALU.add))
                link(nc.vector.reciprocal(run, run))
                nc.vector.scalar_tensor_tensor(out=es, in0=er, scalar=1.0 / H, in1=run, op0=ALU.mult, op1=ALU.mult)\
                  .then_inc(s["alpha"], 1)


def gat_messages(nc, c, g, xl_table, h):
    HOTS = 4
    with ExitStack() as ctx:
        hot = ctx.enter_context(nc.sbuf_tensor(fresh(nc, "hot_a"), [P, HOTS, H + 1, P], F32))
        share = ctx.enter_context(nc.sbuf_tensor(fresh(nc, "share"), [P, NODE_TILES * H], F32))
        acc = ctx.enter_context(nc.psum_tensor(fresh(nc, "acc1"), [P, BANKS * BANK], F32))
        assert HOTS == HALF

        with phase(nc, idx_ready=2, used=0, let_go=0, gathered=GROUP, hot=0, cleared=0) as (block, s):

            @block.gpsimd
            def _(pool):
                gather_rows(nc, c, pool, xl_table, XLW, s)

            @block.scalar
            def _(act):
                with act.Fori(0, ITERS) as i:
                    for half in range(2):
                        for u in range(half * HALF, (half + 1) * HALF):
                            act.wait_ge(s["gathered"][u], 16 * i + 16)
                        next_indices(nc, c, act, nc.scalar.copy, i, half, s["idx_ready"])

            @block.vector
            def _(dve):
                first_indices(nc, c, s["idx_ready"])
                dve.sem_inc(s["used"], GROUP)
                with dve.Fori(0, ITERS) as i:
                    for u in range(GROUP):
                        slot = i * GROUP + u
                        dve.wait_ge(s["used"], GROUP * i + u + 1 + GROUP - HOTS)
                        for k in range(H):
                            nc.vector.tensor_scalar(hot[:, u % HOTS, k, :], c.iota[:, :], c.rel[:, bass.ds(slot, 1)],
                                                    c.e[:, bass.ds(slot, 1), k], ALU.is_equal, ALU.mult)
                        nc.vector.tensor_scalar(hot[:, u % HOTS, H, :], c.iota[:, :], c.rel[:, bass.ds(slot, 1)],
                                                None, ALU.is_equal).then_inc(s["hot"], 1)

            @block.tensor
            def _(pe):
                clear_sums(nc, c, acc).then_inc(s["cleared"], 1)
                pe.wait_ge(s["cleared"], 1)
                with pe.Fori(0, ITERS) as i:
                    tiles = load_tiles(nc, c, i)
                    for u in range(GROUP):
                        pe.wait_ge(s["hot"], GROUP * i + u + 1)
                        pe.wait_ge(s["gathered"][u], 16 * i + 16)
                        for k in range(H):
                            nc.tensor.matmul(acc[:, bass.ds(tiles[u] * C, C)], hot[:, u % HOTS, k, :],
                                             c.rows[:, u, k * C:(k + 1) * C], start=False, stop=False,
                                             skip_group_check=True)
                        nc.tensor.matmul(acc[:, bass.ds(tiles[u] * H + SIDE, H)], hot[:, u % HOTS, H, :],
                                         c.e[:, bass.ds(i * GROUP + u, 1), :].rearrange("p a h -> p (a h)"),
                                         start=False, stop=False, skip_group_check=True).then_inc(s["used"], 1)

        U = 5
        with phase(nc, vec=0, mixed=0) as (block, s):

            @block.vector
            def _(dve):
                link = linker(dve, s["vec"])
                link(nc.vector.tensor_scalar(share[:, :], acc[:, SIDE:SIDE + NODE_TILES * H], -1.0, 1.0 / H,
                                             ALU.mult, ALU.add))
                link(nc.vector.tensor_tensor(out=h[:, :, :], in0=h[:, :, :],
                                             in1=g.b_out[:, :].unsqueeze(1).to_broadcast([P, NODE_TILES, C]),
                                             op=ALU.add))
                with dve.Fori(0, NODE_TILES // U) as i:
                    for k in range(H + 1):
                        for u in range(U):
                            t = i * U + u
                            mine = h[:, bass.ds(t, 1), :].rearrange("p a c -> p (a c)")
                            if k == 0:
                                nc.vector.tensor_tensor(out=mine, in0=acc[:, bass.ds(t * C, C)], in1=mine,
                                                        op=ALU.add).then_inc(s["mixed"], 1)
                            else:
                                dve.wait_ge(s["mixed"], i * (U * (H + 1)) + (k - 1) * U + u + 1)
                                nc.vector.scalar_tensor_tensor(
                                    out=mine, in0=g.xl[:, bass.ds(t, 1), (k - 1) * C:k * C].rearrange("p a c -> p (a c)"),
                                    scalar=share[:, bass.ds(t * H + k - 1, 1)], in1=mine,
                                    op0=ALU.mult, op1=ALU.add).then_inc(s["mixed"], 1)


def sage(nc, c, sums, inv_deg, h, out, w_self, w_neigh, bias, relu, x=None):
    U = 5
    with ExitStack() as ctx:
        turned = ctx.enter_context(nc.sbuf_tensor(fresh(nc, "turned_sb"), [P, 2, 2, P], F32))
        ps = ctx.enter_context(nc.psum_tensor(fresh(nc, "sage_ps"), [P, 4, BANK], F32))

        with phase(nc, turned=0, copied=0, prod=0, out=0) as (block, s):

            @block.tensor
            def _(pe):
                for t in range(NODE_TILES):
                    b = t % U % 2
                    pe.wait_ge(s["out"], t + 1 + (t % U == 0))
                    for k, m in ((0, h), (1, sums)):
                        last = nc.tensor.transpose(ps[:, b, k * P:(k + 1) * P], m[:, t, :], c.ident[:, :])
                    last.then_inc(s["turned"], 1)
                    pe.wait_ge(s["copied"], t + 1)
                    nc.tensor.matmul(ps[:, 2 + b, 0:C], turned[:, b, 0, :], w_self, start=True, stop=False)
                    nc.tensor.matmul(ps[:, 2 + b, 0:C], turned[:, b, 1, :], w_neigh, start=False, stop=True)\
                      .then_inc(s["prod"], 1)

            @block.scalar
            def _(act):
                with act.Fori(0, NODE_TILES // U) as i:
                    for u in range(U):
                        act.wait_ge(s["turned"], i * U + u + 1)
                        nc.scalar.copy(turned[:, u % 2, :, :].rearrange("p k c -> p (k c)"),
                                       ps[:, u % 2, 0:2 * P]).then_inc(s["copied"], 1)

            @block.vector
            def _(dve):
                dve.sem_inc(s["out"], 2)
                with dve.Fori(0, NODE_TILES // U) as i:
                    for u in range(U):
                        t = i * U + u
                        dve.wait_ge(s["prod"], t + 1)
                        nc.vector.tensor_tensor(out=out[:, bass.ds(t, 1), :].rearrange("p a c -> p (a c)"),
                                                in0=ps[:, 2 + u % 2, 0:C], in1=bias, op=ALU.add).then_inc(s["out"], 1)
                dve.wait_ge(s["out"], NODE_TILES + 2)
                if relu:
                    nc.vector.tensor_scalar(out[:, :, :], out[:, :, :], 0.0, None, ALU.max)
                else:
                    nc.vector.tensor_tensor(out=x[:, :, :], in0=x[:, :, :], in1=out[:, :, :], op=ALU.add)


def scaled_sums(nc, acc, scale, out, x=None):
    with phase(nc, tile=0) as (block, s):

        @block.vector
        def _(dve):
            for t in range(NODE_TILES):
                part = acc[:, t * C:(t + 1) * C]
                if x is None:
                    nc.vector.tensor_scalar(out[:, t, :], part, scale[:, t:t + 1], None, ALU.mult).then_inc(s["tile"], 1)
                else:
                    nc.vector.scalar_tensor_tensor(out=x[:, t, :], in0=part, scalar=scale[:, t:t + 1],
                                                   in1=x[:, t, :], op0=ALU.mult, op1=ALU.add).then_inc(s["tile"], 1)


def graph_layers(nc, x_in, src, dst, gate_w, gate_b, Wl, bl, Wr, br, att, bias, ln_g, ln_b,
                 W_self1, W_neigh1, b1, W_self2, W_neigh2, b2, out):
    rel_rows = nc.dram_tensor("rel_rows", ((SLOTS + GROUP) * P,), BF16, kind="Internal").ap()
    dst_line = nc.dram_tensor("dst_line", (SLOTS * P + 2,), F32, kind="Internal").ap()
    gate_table = nc.dram_tensor("gate_table", (NODE_TILES * P, C + 1), F32, kind="Internal").ap()
    h_tables = [nc.dram_tensor(f"h_table{k}", (NODE_TILES * P, C), F32, kind="Internal").ap() for k in range(3)]
    xl_tables = [nc.dram_tensor(f"xl_table{k}", (NODE_TILES * P, XLW), F32, kind="Internal").ap()
                 for k in range(LAYERS)]

    with ExitStack() as ctx:
        def sb(name, shape, dt=F32, within=ctx):
            return within.enter_context(nc.sbuf_tensor(fresh(nc, name), shape, dt))

        class c:
            iota = sb("iota", [P, P])
            part = sb("part", [P, 1])
            ident = sb("ident", [P, P])
            ones = sb("ones", [P, P])
            zeros = sb("zeros", [P, BANK], BF16)
            rel = sb("rel", [P, SLOTS])
            idx = sb("idx", [P, SLOTS + GROUP], I32)
            idx_now = sb("idx_now", [P, GROUP], I32)
            slot_tile = sb("slot_tile", [1, SLOTS], I32)
            valid = sb("valid", [P, SLOTS])
            invalid_neg = sb("invalid_neg", [P, SLOTS])
            brk_before = sb("brk_before", [SB, SLOT_BLOCKS, P])
            brk_after = sb("brk_after", [SB, SLOT_BLOCKS, P])
            open_from_start = sb("open_from_start", [SB, SLOT_BLOCKS, P])
            open_to_end = sb("open_to_end", [SB, SLOT_BLOCKS, P])
            slot_brk = sb("slot_brk", [H, 2, SLOTS])

        x = sb("x", [P, NODE_TILES, C])
        h_wide = sb("h", [P, NODE_TILES, C + 1])
        h = h_wide[:, :, 0:C]

        with phase(nc, clear=0, loads=0) as (block, s):

            @block.vector
            def _(dve):
                nc.vector.memset(x[:, :, :], 0.0).then_inc(s["clear"], 1)

            @block.sync
            def _(sp):
                sp.wait_ge(s["clear"], 1)
                sp.dma_start(x[:, 0:NODES_FULL, :], x_in[0:NODES_FULL * P, :].rearrange("(t p) c -> p t c", p=P))\
                  .then_inc(s["loads"], 16)
                sp.dma_start(x[0:NODES_REST, NODES_FULL, :], x_in[NODES_FULL * P:N, :]).then_inc(s["loads"], 16)
                sp.wait_ge(s["loads"], 32)

        make_slots(nc, c, src, dst, rel_rows, dst_line)

        c.rows = sb("rows", [P, GROUP, XRW])

        with ExitStack() as part:
            gate_w_all = sb("gate_w_all", [P, 2 * C], within=part)
            gate_b_all = sb("gate_b_all", [P, 1], within=part)
            node_gate = sb("node_gate", [P, NODE_TILES], within=part)
            with phase(nc, loads=0) as (block, s):

                @block.sync
                def _(sp):
                    sp.dma_start(gate_w_all[:, :], rows_of(gate_w, 0, 2 * C)).then_inc(s["loads"], 16)
                    sp.dma_start(gate_b_all[:, :], rows_of(gate_b, 0, 1)).then_inc(s["loads"], 16)
                    sp.wait_ge(s["loads"], 32)

            norm_relu(nc, c, x, h, table=gate_table, dot=(gate_w_all, h_wide, node_gate))
            gated_pass(nc, c, rel_rows, gate_table, node_gate, gate_b_all[:, 0:1], x, h)

        norm_relu(nc, c, x, h)
        with ExitStack() as part:
            c.e = sb("e", [P, SLOTS, H], within=part)
            c.e_self = sb("e_self", [P, SLOTS, H], within=part)

            class g:
                xl = sb("xl", [P, NODE_TILES, XLW], within=part)
                xr = sb("xr", [P, NODE_TILES, XRW], within=part)
                w = [sb(f"w{k}", [P, XLW], within=part) for k in range(2)]
                att = sb("att_all", [P, HC], within=part)
                b_sum = sb("b_sum", [P, XLW], within=part)
                b_out = sb("b_out", [P, C], within=part)
                gain = sb("gain", [P, C], within=part)
                shift = sb("shift_ln", [P, C], within=part)

            for layer in range(LAYERS):
                gat_weights(nc, c, g, layer, Wl, Wr, bl, br, att, bias, ln_g, ln_b)
                gat_tables(nc, c, g, h, xl_tables[layer])
                gat_scores(nc, c, g, rel_rows, xl_tables[layer])
                gat_softmax(nc, c, g.xr)
                gat_messages(nc, c, g, xl_tables[layer], h)
                norm_relu(nc, c, h, h, gain=g.gain[:, :], shift=g.shift[:, :])

        with phase(nc, vec=0) as (block, s):

            @block.vector
            def _(dve):
                nc.vector.tensor_tensor(out=x[:, :, :], in0=x[:, :, :], in1=h[:, :, :], op=ALU.add)

        inv_deg = sb("inv_deg", [P, NODE_TILES])
        norm_relu(nc, c, x, h, table=h_tables[0])
        with nc.psum_tensor(fresh(nc, "acc2"), [P, ACC_BANKS * BANK], F32) as acc:
            neighbour_pass(nc, c, h_tables[0], acc, True)
            with phase(nc, vec=0) as (block, s):

                @block.vector
                def _(dve):
                    link = linker(dve, s["vec"])
                    link(nc.vector.tensor_scalar(inv_deg[:, :], acc[:, SIDE:SIDE + NODE_TILES], 1.0, None, ALU.max))
                    link(nc.vector.reciprocal(inv_deg[:, :], inv_deg[:, :]))

            scaled_sums(nc, acc, inv_deg, None, x)

        mean = sb("mean", [P, NODE_TILES, C])
        weights = [sb(f"sage_w{k}", [P, C]) for k in range(4)]
        biases = [sb(f"sage_b{k}", [P, C]) for k in range(2)]
        with phase(nc, loads=0) as (block, s):

            @block.sync
            def _(sp):
                for ap, to in zip((W_self1, W_neigh1, W_self2, W_neigh2), weights):
                    sp.dma_start(to[:, :], ap).then_inc(s["loads"], 16)
                for ap, to in zip((b1, b2), biases):
                    sp.dma_start(to[:, :], rows_of(ap, 0, C)).then_inc(s["loads"], 16)
                sp.wait_ge(s["loads"], 6 * 16)

        norm_relu(nc, c, x, h, table=h_tables[1])
        for k in range(2):
            with nc.psum_tensor(fresh(nc, f"acc3{k}"), [P, ACC_BANKS * BANK], F32) as acc:
                neighbour_pass(nc, c, h_tables[1 + k], acc, False)
                scaled_sums(nc, acc, inv_deg, mean)
            sage(nc, c, mean, inv_deg, h, h, weights[2 * k][:, :], weights[2 * k + 1][:, :], biases[k][:, :],
                 relu=k == 0, x=x)
            with phase(nc, stored=0) as (block, s):

                @block.sync
                def _(sp):
                    if k == 0:
                        sp.dma_start(h_tables[2].rearrange("(t p) c -> p t c", p=P), h[:, :, :])\
                          .then_inc(s["stored"], 16)
                        sp.wait_ge(s["stored"], 16)
                    else:
                        sp.dma_start(out[0:NODES_FULL * P, :].rearrange("(t p) c -> p t c", p=P),
                                     x[:, 0:NODES_FULL, :]).then_inc(s["stored"], 16)
                        sp.dma_start(out[NODES_FULL * P:N, :], x[0:NODES_REST, NODES_FULL, :])\
                          .then_inc(s["stored"], 16)
                        sp.wait_ge(s["stored"], 32)


NAMES = ["x", "src", "dst", "L0_gnn_gate_w", "L0_gnn_gate_b", "L1_gnn_Wl", "L1_gnn_bl", "L1_gnn_Wr", "L1_gnn_br",
         "L1_gnn_att", "L1_gnn_bias", "L1_gnn_ln_g", "L1_gnn_ln_b", "L3_gnn_W_self1", "L3_gnn_W_neigh1", "L3_gnn_b1",
         "L3_gnn_W_self2", "L3_gnn_W_neigh2", "L3_gnn_b2"]


def kernel(**inputs):
    import numpy as np
    import concourse.bacc as bacc
    from concourse.bass_utils import run_bass_kernel_spmd

    nc = bacc.Bacc("TRN2", target_bir_lowering=False, num_devices=1)
    arrays, args = {}, []
    for name in NAMES:
        a = np.ascontiguousarray(inputs[name])
        arrays[f"in_{name}"] = a
        args.append(nc.dram_tensor(f"in_{name}", a.shape, mybir.dt.from_np(a.dtype), kind="ExternalInput").ap())
    args.append(nc.dram_tensor("out", (N, C), F32, kind="ExternalOutput").ap())
    graph_layers(nc, *args)
    result = run_bass_kernel_spmd(nc, [arrays], core_ids=[0])
    return result.results[0]["out"]
```

```python
from contextlib import ExitStack, contextmanager

import concourse.bass as bass
from concourse import mybir

F32 = mybir.dt.float32
BF16 = mybir.dt.bfloat16
U16 = mybir.dt.uint16
I32 = mybir.dt.int32
ALU = mybir.AluOpType
ACT = mybir.ActivationFunctionType
AX = mybir.AxisListType

P = 128
N = 3125
E = 50000
C = 128
H = 4
LAYERS = 2
NODE_TILES = -(-N // P)
NODES_FULL = N // P
NODES_REST = N - NODES_FULL * P
EDGE_TILES = -(-E // P)
EDGES_FULL = E // P
EDGES_REST = E - EDGES_FULL * P
EDGE_BLOCKS = -(-EDGE_TILES // P)
SLOT_BLOCKS = 4
GROUP = 8
WIDE = 16
HALF = GROUP // 2
SLOTS = -(-(EDGE_TILES + NODE_TILES - 1) // (2 * WIDE)) * 2 * WIDE
SB = SLOTS // SLOT_BLOCKS
ITERS = SLOTS // GROUP
WITERS = SLOTS // WIDE
HC = H * C
XLW = HC + H
XRW = HC + 2 * H
SIDE = NODE_TILES * C
BANK = 512
BANKS = 8
ACC_BANKS = -(-(SIDE + NODE_TILES * (H + 1)) // BANK)
GATE = 7 * BANK
W_SHIFT = 3
W_NODES = 1 << W_SHIFT
WINDOWS = -(-N // W_NODES)
W_COLS = NODE_TILES * W_NODES
SPARE = 4
WSLOTS = -(-(EDGE_TILES + WINDOWS) // 16) * 16
NEG = -1e30
LN_EPS = 1e-5
SLOPE = 0.2
L0_EPS = 0.1

assert SLOTS % SLOT_BLOCKS == 0 and SB <= P and ACC_BANKS < BANKS and SLOTS >= EDGE_TILES + NODE_TILES - 1
assert SIDE % BANK + NODE_TILES * (H + 1) <= BANK


def rows_of(ap, offset, n):
    return bass.AP(ap.tensor, ap.offset + offset, [[0, P], [1, n]])


def fresh(nc, name):
    return f"{name}_{nc.next_id()}"


def linker(engine, sem):
    count = [0]

    def link(ins):
        count[0] += 1
        ins.then_inc(sem, 1)
        engine.wait_ge(sem, count[0])

    return link


@contextmanager
def phase(nc, **counts):
    s, every = {}, []
    for name, n in counts.items():
        handles = [nc.alloc_semaphore(name=fresh(nc, name)) for _ in range(n or 1)]
        every += handles
        s[name] = handles if n else handles[0]
    with nc.Block() as block:
        yield block, s
    nc.clear_and_free_semaphores(every)
    nc.all_engine_barrier()


def make_slots(nc, c, src, dst, rel_rows, dst_line):
    with ExitStack() as ctx:
        def sb(name, shape, dt=F32):
            return ctx.enter_context(nc.sbuf_tensor(fresh(nc, name), shape, dt))

        dst_i = sb("dst_i", [P, EDGE_BLOCKS, P], I32)
        src_i = sb("src_i", [P, EDGE_BLOCKS, P], I32)
        dst_f = sb("dst_f", [P, EDGE_BLOCKS, P])
        src_f = sb("src_f", [P, EDGE_BLOCKS, P])
        span_i = sb("span_i", [P, EDGE_BLOCKS, 2], I32)
        span = sb("span", [P, EDGE_BLOCKS, 2])
        tile_id = sb("tile_id", [P, EDGE_BLOCKS])
        real = sb("real", [P, EDGE_BLOCKS])
        n_slots = sb("n_slots", [P, EDGE_BLOCKS])
        n_before = sb("n_before", [P, EDGE_BLOCKS])
        first = sb("first", [P, EDGE_BLOCKS])
        end = sb("end", [P, EDGE_BLOCKS])
        shift = sb("shift", [P, EDGE_BLOCKS])
        shift_w = sb("shift_w", [P, EDGE_BLOCKS, P])
        later = sb("later", [P, P])
        from_first = sb("from_first", [P, EDGE_BLOCKS, SLOTS])
        pick = sb("pick", [P, EDGE_BLOCKS, SLOTS])
        slot_no = sb("slot_no", [P, SLOTS])
        tile_f = sb("tile_f", [P, SLOTS])
        used_off = sb("used_off", [P, SLOTS])
        dst_slot = sb("dst_slot", [P, SLOTS])
        part_1 = sb("part_1", [P, SLOTS])
        rel_row = sb("rel_row", [SB, SLOT_BLOCKS, P], BF16)
        dst_row = sb("dst_row", [SB, SLOT_BLOCKS, P])
        dst_prev = sb("dst_prev", [SB, SLOT_BLOCKS, P])
        dst_next = sb("dst_next", [SB, SLOT_BLOCKS, P])
        outside = sb("outside", [1, 1])
        any_break = sb("any_break", [SB, 2, SLOT_BLOCKS, H])
        ps = ctx.enter_context(nc.psum_tensor(fresh(nc, "slot_ps"), [P, BANKS * BANK], F32))
        PRE, SRC, DST, TIL, USE, REL, ROW, BRK = (k * BANK for k in range(BANKS))

        with phase(nc, pads=0, loads=0, iotas=0, vec=0, pe=0, row_parts=0, rows_out=0, rows_back=0) as (block, s):

            @block.gpsimd
            def _(pool):
                link = linker(pool, s["iotas"])
                link(nc.gpsimd.iota(slot_no[:, :], [[1, SLOTS]], base=0, channel_multiplier=0,
                                    allow_small_or_imprecise_dtypes=True))
                link(nc.gpsimd.iota(c.part[:, :], [[1, 1]], base=0, channel_multiplier=1,
                                    allow_small_or_imprecise_dtypes=True))
                link(nc.gpsimd.iota(tile_id[:, :], [[P, EDGE_BLOCKS]], base=0, channel_multiplier=1,
                                    allow_small_or_imprecise_dtypes=True))
                link(nc.gpsimd.memset(c.ones[:, :], 1.0))
                link(nc.gpsimd.memset(c.zeros[:, :], 0.0))
                link(nc.gpsimd.memset(outside[:, :], -5.0))

            @block.sync
            def _(sp):
                sp.wait_ge(s["pads"], 2)
                whole = EDGES_FULL // P * P
                for ap, to in ((dst, dst_i), (src, src_i)):
                    sp.dma_start(to[:, 0:whole // P, :],
                                 ap[0:whole * P].rearrange("(b p e) -> p b e", p=P, e=P)).then_inc(s["loads"], 16)
                    sp.dma_start(to[0:EDGES_FULL - whole, whole // P, :],
                                 ap[whole * P:EDGES_FULL * P].rearrange("(p e) -> p e", e=P)).then_inc(s["loads"], 16)
                    sp.dma_start(to[EDGES_FULL - whole:EDGES_FULL - whole + 1, whole // P, 0:EDGES_REST],
                                 ap[EDGES_FULL * P:E].rearrange("(a e) -> a e", a=1)).then_inc(s["loads"], 16)
                sp.wait_ge(s["row_parts"], 2)
                sp.dma_start(rel_rows[0:SLOTS * P].rearrange("(b r e) -> r b e", r=SB, e=P),
                             rel_row[:, :, :]).then_inc(s["rows_out"], 16)
                sp.dma_start(rel_rows[SLOTS * P:(SLOTS + WIDE) * P].rearrange("(r e) -> r e", e=P),
                             rel_row[0:WIDE, 0, :]).then_inc(s["rows_out"], 16)
                sp.dma_start(dst_line[1:1 + SLOTS * P].rearrange("(b r e) -> r b e", r=SB, e=P),
                             dst_row[:, :, :]).then_inc(s["rows_out"], 16)
                for at in (0, 1 + SLOTS * P):
                    sp.dma_start(dst_line[at:at + 1].rearrange("(a e) -> a e", a=1),
                                 outside[:, :]).then_inc(s["rows_out"], 16)
                sp.wait_ge(s["rows_out"], 5 * 16)
                for to, at in ((dst_prev, 0), (dst_next, 2)):
                    sp.dma_start(to[:, :, :], dst_line[at:at + SLOTS * P].rearrange("(b r e) -> r b e", r=SB, e=P))\
                      .then_inc(s["rows_back"], 16)

            @block.vector
            def _(dve):
                nc.vector.memset(dst_i[:, :, :], NODE_TILES * P - 1).then_inc(s["pads"], 1)
                nc.vector.memset(src_i[:, :, :], 0).then_inc(s["pads"], 1)
                link = linker(dve, s["vec"])
                dve.wait_ge(s["iotas"], 6)
                link(nc.vector.tensor_copy(c.iota[:, :], slot_no[:, 0:P]))
                link(nc.vector.tensor_scalar(later[:, :], slot_no[:, 0:P], c.part[:, 0:1], None, ALU.is_gt))
                link(nc.vector.tensor_scalar(c.ident[:, :], slot_no[:, 0:P], c.part[:, 0:1], None, ALU.is_equal))
                link(nc.vector.tensor_scalar(real[:, :], tile_id[:, :], float(EDGE_TILES), None, ALU.is_lt))
                dve.wait_ge(s["loads"], 6 * 16)
                link(nc.vector.tensor_copy(dst_f[:, :, :], dst_i[:, :, :]))
                link(nc.vector.tensor_copy(src_f[:, :, :], src_i[:, :, :]))
                link(nc.vector.tensor_single_scalar(span_i[:, :, :], dst_i[:, :, 0:P:P - 1], 7,
                                                    op=ALU.arith_shift_right))
                link(nc.vector.tensor_copy(span[:, :, :], span_i[:, :, :]))
                link(nc.vector.tensor_tensor(out=n_slots[:, :], in0=span[:, :, 1], in1=span[:, :, 0], op=ALU.subtract))
                link(nc.vector.scalar_tensor_tensor(out=n_slots[:, :], in0=n_slots[:, :], scalar=1.0, in1=real[:, :],
                                                    op0=ALU.add, op1=ALU.mult))
                link(nc.vector.memset(n_before[:, 0:1], 0.0))
                for b in range(1, EDGE_BLOCKS):
                    link(nc.vector.tensor_tensor(out=n_before[:, b:b + 1], in0=n_before[:, b - 1:b],
                                                 in1=n_slots[:, b - 1:b], op=ALU.add))
                dve.wait_ge(s["pe"], 1)
                link(nc.vector.tensor_copy(first[:, :], ps[:, PRE:PRE + EDGE_BLOCKS]))
                link(nc.vector.tensor_tensor(out=end[:, :], in0=first[:, :], in1=n_slots[:, :], op=ALU.add))
                link(nc.vector.tensor_tensor(out=shift[:, :], in0=span[:, :, 0], in1=first[:, :], op=ALU.subtract))
                for b in range(EDGE_BLOCKS):
                    nc.vector.tensor_scalar(shift_w[:, b, :], c.ones[:, :], shift[:, b:b + 1], None, ALU.mult)
                    link(nc.vector.tensor_scalar(from_first[:, b, :], slot_no[:, :], first[:, b:b + 1], None, ALU.is_ge))
                    link(nc.vector.scalar_tensor_tensor(out=pick[:, b, :], in0=slot_no[:, :], scalar=end[:, b:b + 1],
                                                        in1=from_first[:, b, :], op0=ALU.is_lt, op1=ALU.mult))
                dve.wait_ge(s["pe"], 2)
                link(nc.vector.tensor_tensor(out=tile_f[:, :], in0=ps[:, TIL:TIL + SLOTS], in1=slot_no[:, :], op=ALU.add))
                link(nc.vector.tensor_tensor(out=tile_f[:, :], in0=ps[:, USE:USE + SLOTS], in1=tile_f[:, :], op=ALU.mult))
                link(nc.vector.tensor_copy(c.slot_tile[0:1, :], tile_f[0:1, :]))
                link(nc.vector.memset(c.idx[:, :], 0))
                link(nc.vector.tensor_copy(c.idx[:, 0:SLOTS], ps[:, SRC:SRC + SLOTS]))
                link(nc.vector.tensor_copy(dst_slot[:, :], ps[:, DST:DST + SLOTS]))
                link(nc.vector.tensor_scalar(used_off[:, :], ps[:, USE:USE + SLOTS], 1000.0, -1000.0, ALU.mult, ALU.add))
                link(nc.vector.scalar_tensor_tensor(out=c.rel[:, :], in0=tile_f[:, :], scalar=-float(P),
                                                    in1=dst_slot[:, :], op0=ALU.mult, op1=ALU.add))
                link(nc.vector.tensor_tensor(out=c.rel[:, :], in0=c.rel[:, :], in1=used_off[:, :], op=ALU.add))
                link(nc.vector.tensor_scalar(part_1[:, :], c.rel[:, :], 0.0, None, ALU.is_ge))
                link(nc.vector.scalar_tensor_tensor(out=c.valid[:, :], in0=c.rel[:, :], scalar=float(P),
                                                    in1=part_1[:, :], op0=ALU.is_lt, op1=ALU.mult))
                link(nc.vector.tensor_scalar(c.invalid_neg[:, :], c.valid[:, :], -1.0, -NEG, ALU.add, ALU.mult))
                dve.wait_ge(s["pe"], 3)
                nc.vector.tensor_copy(rel_row[:, :, :], ps[0:SB, REL:REL + BANK].rearrange("r (b e) -> r b e", e=P))\
                  .then_inc(s["row_parts"], 1)
                nc.vector.tensor_copy(dst_row[:, :, :], ps[0:SB, ROW:ROW + BANK].rearrange("r (b e) -> r b e", e=P))\
                  .then_inc(s["row_parts"], 1)
                dve.wait_ge(s["row_parts"], 2)
                dve.wait_ge(s["rows_back"], 32)
                for k, other, own, through in ((0, dst_prev, c.brk_before, c.open_from_start),
                                               (1, dst_next, c.brk_after, c.open_to_end)):
                    link(nc.vector.tensor_tensor(out=own[:, :, :], in0=dst_row[:, :, :], in1=other[:, :, :],
                                                 op=ALU.is_equal))
                    link(nc.vector.tensor_scalar(own[:, :, :], own[:, :, :], -1.0, -NEG, ALU.add, ALU.mult))
                    for b in range(SLOT_BLOCKS):
                        step = 1 if k == 0 else -1
                        link(nc.vector.tensor_tensor_scan(out=through[:, b, ::step], data0=own[:, b, ::step],
                                                          data1=own[:, b, ::step], initial=0.0,
                                                          op0=ALU.min, op1=ALU.min))
                    edge = P - 1 if k == 0 else 0
                    for h in range(H):
                        link(nc.vector.tensor_copy(any_break[:, k, :, h], through[:, :, edge]))
                    link(nc.vector.memset(own[:, :, P - 1 - edge:P - edge], NEG))
                dve.wait_ge(s["pe"], 4)
                link(nc.vector.tensor_copy(c.slot_brk[:, 0, :], ps[0:H, BRK:BRK + SLOTS]))
                link(nc.vector.tensor_copy(c.slot_brk[:, 1, :], ps[0:H, PRE:PRE + SLOTS]))

            @block.tensor
            def _(pe):
                V = 4 + 7 + EDGE_BLOCKS - 1
                pe.wait_ge(s["vec"], V)
                nc.tensor.matmul(ps[:, PRE:PRE + EDGE_BLOCKS], later[:, :], n_slots[:, :], start=True, stop=False)
                nc.tensor.matmul(ps[:, PRE:PRE + EDGE_BLOCKS], c.ones[:, :], n_before[:, :], start=False, stop=True)\
                  .then_inc(s["pe"], 1)
                V += 3 + 2 * EDGE_BLOCKS
                pe.wait_ge(s["vec"], V)
                for b in range(EDGE_BLOCKS):
                    for at, left in ((SRC, src_f[:, b, :]), (DST, dst_f[:, b, :]), (TIL, shift_w[:, b, :]),
                                     (USE, c.ones[:, :])):
                        last = nc.tensor.matmul(ps[:, at:at + SLOTS], left, pick[:, b, :], start=b == 0,
                                                stop=b == EDGE_BLOCKS - 1)
                last.then_inc(s["pe"], 1)
                V += 12
                pe.wait_ge(s["vec"], V)
                for b in range(SLOT_BLOCKS):
                    nc.tensor.transpose(ps[0:SB, REL + b * P:REL + (b + 1) * P], c.rel[:, b * SB:(b + 1) * SB],
                                        c.ident[:, :])
                    last = nc.tensor.transpose(ps[0:SB, ROW + b * P:ROW + (b + 1) * P],
                                               dst_slot[:, b * SB:(b + 1) * SB], c.ident[:, :])
                last.then_inc(s["pe"], 1)
                pe.wait_ge(s["vec"], V + 2 * (2 + SLOT_BLOCKS + H + 1))
                for k, at in ((0, BRK), (1, PRE)):
                    for b in range(SLOT_BLOCKS):
                        last = nc.tensor.transpose(ps[0:H, at + b * SB:at + (b + 1) * SB], any_break[:, k, b, :],
                                                   c.ident[0:SB, 0:SB])
                last.then_inc(s["pe"], 1)


def norm_relu(nc, c, x, out, table=None, gain=None, shift=None, dot=None):
    ACT_TILES = 10
    with ExitStack() as ctx:
        stats = ctx.enter_context(nc.sbuf_tensor(fresh(nc, "stats"), [P, NODE_TILES, 6], F32))
        mean_var = ctx.enter_context(nc.sbuf_tensor(fresh(nc, "mean_var"), [P, NODE_TILES, 2], F32))
        std = ctx.enter_context(nc.sbuf_tensor(fresh(nc, "std"), [P, NODE_TILES], F32))
        rstd = ctx.enter_context(nc.sbuf_tensor(fresh(nc, "rstd"), [P, NODE_TILES], F32))
        bias = ctx.enter_context(nc.sbuf_tensor(fresh(nc, "norm_bias"), [P, NODE_TILES], F32))
        if dot is not None:
            prod = ctx.enter_context(nc.sbuf_tensor(fresh(nc, "prod"), [P, C], F32))

        with phase(nc, stats=0, var=0, std=0, scaled=0, shifted=0, rows=0, vec=0, dots=0, out=0) as (block, s):

            @block.vector
            def _(dve):
                link = linker(dve, s["vec"])
                for t in range(NODE_TILES):
                    nc.vector.bn_stats(stats[:, t, :], x[:, t, :]).then_inc(s["stats"], 1)
                for t in range(NODE_TILES):
                    dve.wait_ge(s["stats"], t + 1)
                    nc.vector.bn_aggr(mean_var[:, t, :], stats[:, t, :]).then_inc(s["var"], 1)
                dve.wait_ge(s["var"], NODE_TILES)
                link(nc.vector.tensor_scalar(std[:, :], mean_var[:, :, 1], LN_EPS, None, ALU.add))
                dve.wait_ge(s["std"], 1)
                link(nc.vector.reciprocal(rstd[:, :], std[:, :]))
                link(nc.vector.scalar_tensor_tensor(out=bias[:, :], in0=mean_var[:, :, 0], scalar=-1.0,
                                                    in1=rstd[:, :], op0=ALU.mult, op1=ALU.mult))
                if gain is not None:
                    for t in range(NODE_TILES):
                        nc.vector.scalar_tensor_tensor(out=out[:, t, :], in0=x[:, t, :], scalar=mean_var[:, t, 0:1],
                                                       in1=gain, op0=ALU.subtract, op1=ALU.mult)\
                          .then_inc(s["scaled"], 1)
                    for t in range(NODE_TILES):
                        dve.wait_ge(s["scaled"], t + 1)
                        nc.vector.scalar_tensor_tensor(out=out[:, t, :], in0=out[:, t, :], scalar=rstd[:, t:t + 1],
                                                       in1=shift, op0=ALU.mult, op1=ALU.add).then_inc(s["shifted"], 1)
                    return
                for t in range(ACT_TILES, NODE_TILES):
                    nc.vector.tensor_scalar(out[:, t, :], x[:, t, :], rstd[:, t:t + 1], bias[:, t:t + 1],
                                            ALU.mult, ALU.add).then_inc(s["scaled"], 1)
                dve.wait_ge(s["scaled"], NODE_TILES - ACT_TILES)
                mine = out[:, ACT_TILES:NODE_TILES, :]
                nc.vector.tensor_scalar(mine, mine, 0.0, None, ALU.max).then_inc(s["rows"], 1)
                if dot is not None:
                    dve.wait_ge(s["rows"], 1 + ACT_TILES)
                    for k in range(2):
                        for t in range(NODE_TILES):
                            link(nc.vector.scalar_tensor_tensor(
                                out=prod[:, :], in0=out[:, t, :], scalar=1.0, in1=dot[0][:, k * C:(k + 1) * C],
                                op0=ALU.mult, op1=ALU.mult,
                                accum_out=dot[2][:, t:t + 1] if k else dot[1][:, t, C:C + 1]))
                        dve.sem_inc(s["dots"], 1)

            @block.scalar
            def _(act):
                act.wait_ge(s["vec"], 1)
                nc.scalar.activation(std[:, :], std[:, :], ACT.Sqrt).then_inc(s["std"], 1)
                if gain is not None:
                    for t in range(0, NODE_TILES, 5):
                        act.wait_ge(s["shifted"], t + 5)
                        nc.scalar.activation(out[:, t:t + 5, :], out[:, t:t + 5, :], ACT.Relu)
                    return
                act.wait_ge(s["vec"], 3)
                for t in range(ACT_TILES):
                    nc.scalar.activation(out[:, t, :], x[:, t, :], ACT.Relu, bias=bias[:, t:t + 1],
                                         scale=rstd[:, t:t + 1]).then_inc(s["rows"], 1)

            @block.sync
            def _(sp):
                if dot is not None:
                    sp.wait_ge(s["dots"], 1)
                    sp.dma_start(table.rearrange("(t p) c -> p t c", p=P), dot[1][:, :, :]).then_inc(s["out"], 16)
                    sp.wait_ge(s["out"], 16)
                elif table is not None:
                    sp.wait_ge(s["rows"], 1 + ACT_TILES)
                    sp.dma_start(table.rearrange("(t p) c -> p t c", p=P), out[:, :, :]).then_inc(s["out"], 16)
                    sp.wait_ge(s["out"], 16)


def first_indices(nc, c, idx_ready, group):
    n = group // 2
    for half in range(2):
        nc.vector.tensor_copy(c.idx_now[:, half * n:(half + 1) * n],
                              c.idx[:, half * n:(half + 1) * n]).then_inc(idx_ready[half], 1)


def gather_rows(nc, c, pool, rows, table, s, filled=None):
    group = rows.shape[1]
    n = group // 2
    with pool.Fori(0, SLOTS // group) as i:
        for u in range(group):
            half = u // n
            if filled is None and u % n == 0:
                pool.wait_ge(s["idx_ready"][half], i + 1)
                pool.wait_ge(s["used"], group * i + (half + 1) * n)
            elif filled is not None:
                pool.wait_ge(filled, group * i + u + 1 + HALF)
            if filled is not None or u % n == 0:
                pool.sem_inc(s["let_go"], 1)
            nc.gpsimd.indirect_dma_start(
                out=rows[:, u, :], out_offset=None, in_=table,
                in_offset=bass.IndirectOffsetOnAxis(ap=c.idx_now[:, u:u + 1], axis=0),
                compute_op=ALU.bypass if filled is None else ALU.add).then_inc(s["gathered"][u], 16)


def next_indices(nc, c, copy, i, half, idx_ready, group):
    n = group // 2
    copy(c.idx_now[:, half * n:(half + 1) * n],
         c.idx[:, bass.ds((i + 1) * group + half * n, n)]).then_inc(idx_ready[half], 1)


def load_tiles(nc, c, i, group):
    return nc.values_load_multi_w_load_instructions(
        c.slot_tile[0:1, bass.ds(i * group, group)], engines=[mybir.EngineType.PE], min_val=0,
        max_val=NODE_TILES - 1, skip_runtime_bounds_check_because="slots hold node tiles by construction")[1]


def clear_sums(nc, c, acc):
    for b in range(ACC_BANKS):
        last = nc.tensor.matmul(acc[:, b * BANK:(b + 1) * BANK], c.zeros[:, 0:P], c.zeros[:, :], start=True, stop=True)
    return last


def spread_rows(sp, rel_rows, spread, s, group):
    n = group // 2

    def load(first_slot, half):
        sp.dma_start(spread[:, half, :], bass.AP(rel_rows.tensor, (first_slot + half * n) * P,
                                                 [[0, P], [1, n * P]])).then_inc(s["spread"][half], 16)
    for half in range(2):
        load(0, half)
    with sp.Fori(0, SLOTS // group) as i:
        for half in range(2):
            sp.wait_ge(s["hot_t"], 2 * i + 1 + half)
            load((i + 1) * group, half)
    for half in range(2):
        sp.wait_ge(s["spread"][half], 16 * (SLOTS // group + 1))


def gated_pass(nc, c, rel_rows, table, node_gate, gate_b, x, h):
    with ExitStack() as ctx:
        def sb(name, shape, dt=F32):
            return ctx.enter_context(nc.sbuf_tensor(fresh(nc, name), shape, dt))

        n = WIDE // 2
        rows = sb("gate_rows", [P, WIDE, C + 1])
        hot_t = sb("hot_t", [P, 2, n * P], BF16)
        gate_parts = sb("gate_parts", [P, NODE_TILES, 3], BF16)
        gate_rest = sb("gate_rest", [P, NODE_TILES])
        spread = sb("spread", [P, 2, n * P], BF16)
        score = sb("score", [P, 2, n])
        weight = sb("weight", [P, 2, n])
        rel_now = sb("rel_now", [P, 2, n])
        hot = sb("hot", [P, n, P])
        inv = sb("inv", [P, NODE_TILES])
        acc = ctx.enter_context(nc.psum_tensor(fresh(nc, "acc0"), [P, BANKS * BANK], F32))

        with phase(nc, idx_ready=2, used=0, let_go=0, gathered=WIDE, spread=2, hot_t=0, gate_dst=0, score=0, tanh=0,
                   weight=0, hot=0, rel=0, split=0, summed=0, cleared=0) as (block, s):

            @block.gpsimd
            def _(pool):
                gather_rows(nc, c, pool, rows, table, s)

            @block.sync
            def _(sp):
                spread_rows(sp, rel_rows, spread, s, WIDE)

            @block.scalar
            def _(act):
                with act.Fori(0, WITERS) as i:
                    for half in range(2):
                        act.wait_ge(s["score"], 2 * i + 1 + half)
                        nc.scalar.activation(score[:, half, :], score[:, half, :], ACT.Tanh, bias=gate_b)\
                          .then_inc(s["tanh"], 1)
                        act.wait_ge(s["tanh"], 2 * i + 1 + half)
                        nc.scalar.activation(weight[:, half, :], score[:, half, :], ACT.Exp).then_inc(s["weight"], 1)

            @block.vector
            def _(dve):
                first_indices(nc, c, s["idx_ready"], WIDE)
                dve.sem_inc(s["used"], WIDE)
                link = linker(dve, s["split"])
                link(nc.vector.tensor_copy(gate_rest[:, :], node_gate[:, :]))
                for k in range(3):
                    link(nc.vector.tensor_copy(gate_parts[:, :, k], gate_rest[:, :]))
                    if k < 2:
                        link(nc.vector.tensor_tensor(out=gate_rest[:, :], in0=gate_rest[:, :],
                                                     in1=gate_parts[:, :, k], op=ALU.subtract))
                with dve.Fori(0, WITERS) as i:
                    for half in range(2):
                        dve.wait_ge(s["spread"][half], 16 * i + 16)
                        nc.vector.tensor_scalar(hot_t[:, half, :], spread[:, half, :], c.part[:, 0:1], None,
                                                ALU.is_equal).then_inc(s["hot_t"], 1)
                    for half in range(2):
                        q = half * n
                        dve.wait_ge(s["gate_dst"], 2 * i + 1 + half)
                        for u in range(q, q + n):
                            dve.wait_ge(s["gathered"][u], 16 * i + 16)
                        nc.vector.tensor_reduce(out=score[:, half, :], in_=acc[:, GATE + 3 * q:GATE + 3 * (q + n)]
                                                .rearrange("p (u k) -> p u k", k=3), axis=AX.X, op=ALU.add)\
                          .then_inc(s["summed"], 1)
                        dve.wait_ge(s["summed"], 2 * i + 1 + half)
                        nc.vector.tensor_tensor(out=score[:, half, :], in0=score[:, half, :],
                                                in1=rows[:, q:q + n, C], op=ALU.add).then_inc(s["score"], 1)
                        next_indices(nc, c, nc.vector.tensor_copy, i, half, s["idx_ready"], WIDE)
                        nc.vector.tensor_copy(rel_now[:, half, :], c.rel[:, bass.ds(i * WIDE + q, n)])\
                          .then_inc(s["rel"], 1)
                        dve.wait_ge(s["rel"], 2 * i + 1 + half)
                        dve.wait_ge(s["weight"], 2 * i + 1 + half)
                        for u in range(q, q + n):
                            dve.wait_ge(s["used"], WIDE * i + u + 1 + n)
                            nc.vector.tensor_scalar(hot[:, u % n, :], c.iota[:, :], rel_now[:, half, u % n:u % n + 1],
                                                    weight[:, half, u % n:u % n + 1],
                                                    ALU.is_equal, ALU.mult).then_inc(s["hot"], 1)

            @block.tensor
            def _(pe):
                clear_sums(nc, c, acc).then_inc(s["cleared"], 1)
                pe.wait_ge(s["cleared"], 1)
                with pe.Fori(0, WITERS) as i:
                    tiles = load_tiles(nc, c, i, WIDE)
                    for half in range(2):
                        pe.wait_ge(s["hot_t"], 2 * i + 1 + half)
                        if half:
                            pe.wait_ge(s["score"], 2 * i + 1)
                        for u in range(half * n, (half + 1) * n):
                            last = nc.tensor.matmul(acc[:, GATE + 3 * u:GATE + 3 * (u + 1)],
                                                    hot_t[:, half, u % n * P:(u % n + 1) * P],
                                                    gate_parts[:, bass.ds(tiles[u], 1), :]
                                                    .rearrange("p a k -> p (a k)"), start=True, stop=True)
                        last.then_inc(s["gate_dst"], 1)
                    for u in range(WIDE):
                        pe.wait_ge(s["hot"], WIDE * i + u + 1)
                        nc.tensor.matmul(acc[:, bass.ds(tiles[u] * C, C)], hot[:, u % n, :],
                                         rows[:, u, 0:C], start=False, stop=False, skip_group_check=True)
                        nc.tensor.matmul(acc[:, bass.ds(tiles[u] + SIDE, 1)], hot[:, u % n, :],
                                         c.ones[:, 0:1], start=False, stop=False, skip_group_check=True)\
                          .then_inc(s["used"], 1)

        with phase(nc, vec=0, tile=0) as (block, s):

            @block.vector
            def _(dve):
                link = linker(dve, s["vec"])
                link(nc.vector.tensor_scalar(inv[:, :], acc[:, SIDE:SIDE + NODE_TILES], 1e-30, None, ALU.max))
                link(nc.vector.reciprocal(inv[:, :], inv[:, :]))
                link(nc.vector.tensor_scalar(inv[:, :], inv[:, :], 1.0 - L0_EPS, None, ALU.mult))
                link(nc.vector.scalar_tensor_tensor(out=x[:, :, :], in0=h[:, :, :], scalar=L0_EPS, in1=x[:, :, :],
                                                    op0=ALU.mult, op1=ALU.add))
                for t in range(NODE_TILES):
                    nc.vector.scalar_tensor_tensor(out=x[:, t, :], in0=acc[:, t * C:(t + 1) * C],
                                                   scalar=inv[:, t:t + 1], in1=x[:, t, :],
                                                   op0=ALU.mult, op1=ALU.add).then_inc(s["tile"], 1)


def gat_weights(nc, c, g, layer, Wl, Wr, bl, br, att, bias, ln_g, ln_b):
    with nc.sbuf_tensor(fresh(nc, "prod_w"), [P, C], F32) as prod, nc.sbuf_tensor(fresh(nc, "bl_all"), [P, HC], F32) as bl_all:
        with phase(nc, loads=0, vec=0) as (block, s):

            @block.sync
            def _(sp):
                sp.dma_start(g.w[0][:, 0:HC], Wl[layer, :, :]).then_inc(s["loads"], 16)
                sp.dma_start(g.w[1][:, 0:HC], Wr[layer, :, :]).then_inc(s["loads"], 16)
                sp.dma_start(g.att[:, :], rows_of(att, layer * HC, HC)).then_inc(s["loads"], 16)
                sp.dma_start(bl_all[:, :], rows_of(bl, layer * HC, HC)).then_inc(s["loads"], 16)
                sp.dma_start(g.b_sum[:, 0:HC], rows_of(br, layer * HC, HC)).then_inc(s["loads"], 16)
                sp.dma_start(g.b_out[:, :], rows_of(bias, layer * C, C)).then_inc(s["loads"], 16)
                sp.dma_start(g.gain[:, :], rows_of(ln_g, layer * C, C)).then_inc(s["loads"], 16)
                sp.dma_start(g.shift[:, :], rows_of(ln_b, layer * C, C)).then_inc(s["loads"], 16)

            @block.vector
            def _(dve):
                link = linker(dve, s["vec"])
                dve.wait_ge(s["loads"], 8 * 16)
                link(nc.vector.tensor_tensor(out=g.b_sum[:, 0:HC], in0=g.b_sum[:, 0:HC], in1=bl_all[:, :], op=ALU.add))
                for m in (g.w[0], g.w[1], g.b_sum):
                    for h in range(H):
                        link(nc.vector.scalar_tensor_tensor(
                            out=prod[:, :], in0=m[:, h * C:(h + 1) * C], scalar=SLOPE, in1=g.att[:, h * C:(h + 1) * C],
                            op0=ALU.mult, op1=ALU.mult, accum_out=m[:, HC + h:HC + h + 1]))
                for h in range(H):
                    link(nc.vector.scalar_tensor_tensor(out=g.b_out[:, :], in0=bl_all[:, h * C:(h + 1) * C],
                                                        scalar=1.0 / H, in1=g.b_out[:, :], op0=ALU.mult, op1=ALU.add))


def gat_tables(nc, c, g, h, xl_table):
    U = 5
    with ExitStack() as ctx:
        h_t = ctx.enter_context(nc.sbuf_tensor(fresh(nc, "h_t"), [P, 2, P], F32))
        part = ctx.enter_context(nc.sbuf_tensor(fresh(nc, "self_part"), [P, NODE_TILES, H], F32))
        ps = ctx.enter_context(nc.psum_tensor(fresh(nc, "tab_ps"), [P, 4, 2, BANK], F32))
        TURNED, LEFT, RIGHT, LINEAR = range(4)

        with phase(nc, turned=0, h_t=0, proj=0, xl=0, xr=0, lin=0, z=0, parts=0, z_used=0, stored=0) as (block, s):

            @block.tensor
            def _(pe):
                def turn(t):
                    nc.tensor.transpose(ps[:, TURNED, t % 2, 0:P], h[:, t, :], c.ident[:, :]).then_inc(s["turned"], 1)

                turn(0)
                for t in range(NODE_TILES):
                    if t + 1 < NODE_TILES:
                        turn(t + 1)
                    pe.wait_ge(s["h_t"], t + 1)
                    if t >= 2:
                        pe.wait_ge(s["xl"], t - 1)
                        pe.wait_ge(s["xr"], t - 1)
                    nc.tensor.matmul(ps[:, LEFT, t % 2, :], h_t[:, t % 2, :], g.w[0][:, 0:HC], start=True, stop=True)
                    nc.tensor.matmul(ps[:, RIGHT, t % 2, :], h_t[:, t % 2, :], g.w[1][:, 0:HC], start=True, stop=True)
                    for k in range(2):
                        last = nc.tensor.matmul(ps[:, LINEAR, t % 2, k * H:(k + 1) * H], h_t[:, t % 2, :],
                                                g.w[k][:, HC:XLW], start=True, stop=True)
                    last.then_inc(s["proj"], 1)

            @block.scalar
            def _(act):
                def take_turned(t):
                    act.wait_ge(s["turned"], t + 1)
                    if t >= 2:
                        act.wait_ge(s["proj"], t - 1)
                    nc.scalar.copy(h_t[:, t % 2, :], ps[:, TURNED, t % 2, 0:P]).then_inc(s["h_t"], 1)

                take_turned(0)
                for t in range(NODE_TILES):
                    if t + 1 < NODE_TILES:
                        take_turned(t + 1)
                    act.wait_ge(s["proj"], t + 1)
                    nc.scalar.copy(g.xl[:, t, 0:HC], ps[:, LEFT, t % 2, :]).then_inc(s["xl"], 1)

            @block.gpsimd
            def _(pool):
                for t in range(NODE_TILES):
                    pool.wait_ge(s["xl"], t + 1)
                    pool.wait_ge(s["xr"], t + 1)
                    pool.wait_ge(s["z_used"], t + 1)
                    nc.gpsimd.tensor_tensor(out=c.rows[:, t % U, 0:HC], in0=g.xl[:, t, 0:HC], in1=g.xr[:, t, 0:HC],
                                            op=ALU.add).then_inc(s["z"], 1)

            @block.vector
            def _(dve):
                def scores_of(t):
                    dve.wait_ge(s["z"], t + 1)
                    relu_scores(nc, g, c.rows[:, t % U, :], part[:, t, :]).then_inc(s["z_used"], 1)

                dve.sem_inc(s["z_used"], U)
                LAG = 2
                for t in range(NODE_TILES):
                    dve.wait_ge(s["proj"], t + 1)
                    nc.vector.tensor_copy(g.xl[:, t, HC:XLW], ps[:, LINEAR, t % 2, 0:H]).then_inc(s["lin"], 1)
                    nc.vector.tensor_tensor(out=g.xr[:, t, HC:XLW], in0=ps[:, LINEAR, t % 2, H:2 * H],
                                            in1=g.b_sum[:, HC:XLW], op=ALU.add)
                    nc.vector.tensor_tensor(out=g.xr[:, t, 0:HC], in0=ps[:, RIGHT, t % 2, :],
                                            in1=g.b_sum[:, 0:HC], op=ALU.add).then_inc(s["xr"], 1)
                    if t >= LAG:
                        scores_of(t - LAG)
                for t in range(NODE_TILES - LAG, NODE_TILES):
                    scores_of(t)
                own = g.xr[:, :, XLW:XRW]
                dve.wait_ge(s["z_used"], U + NODE_TILES)
                dve.wait_ge(s["xr"], NODE_TILES)
                nc.vector.tensor_tensor(out=own, in0=g.xl[:, :, HC:XLW], in1=g.xr[:, :, HC:XLW], op=ALU.add)\
                  .then_inc(s["parts"], 1)
                dve.wait_ge(s["parts"], 1)
                nc.vector.scalar_tensor_tensor(out=own, in0=part[:, :, :], scalar=1.0 - SLOPE, in1=own,
                                               op0=ALU.mult, op1=ALU.add)

            @block.sync
            def _(sp):
                for t in range(NODE_TILES):
                    sp.wait_ge(s["xl"], t + 1)
                    sp.wait_ge(s["lin"], t + 1)
                    sp.dma_start(xl_table[t * P:(t + 1) * P, :], g.xl[:, t, :]).then_inc(s["stored"], 16)
                sp.wait_ge(s["stored"], 16 * NODE_TILES)


def relu_scores(nc, g, z, part):
    for h in range(H):
        last = nc.vector.scalar_tensor_tensor(out=z[:, h * C:(h + 1) * C], in0=z[:, h * C:(h + 1) * C], scalar=0.0,
                                              in1=g.att[:, h * C:(h + 1) * C], op0=ALU.max, op1=ALU.mult,
                                              accum_out=part[:, h:h + 1])
    return last


def gat_scores(nc, c, g, rel_rows, xl_table):
    PSB = 4
    with ExitStack() as ctx:
        hot_t = ctx.enter_context(nc.sbuf_tensor(fresh(nc, "hot_ta"), [P, 2, HALF * P], F32))
        spread = ctx.enter_context(nc.sbuf_tensor(fresh(nc, "spread_a"), [P, 2, HALF * P], BF16))
        part = ctx.enter_context(nc.sbuf_tensor(fresh(nc, "edge_part"), [P, GROUP, H], F32))
        ps = ctx.enter_context(nc.psum_tensor(fresh(nc, "xr_ps"), [P, PSB, 2, BANK], F32))
        assert PSB == HALF

        with phase(nc, used=0, let_go=0, gathered=GROUP, spread=2, hot_t=0, xr=0, placed=0, parts=0) as (block, s):

            @block.gpsimd
            def _(pool):
                gather_rows(nc, c, pool, c.rows[:, :, 0:XLW], xl_table, s, filled=s["placed"])

            @block.sync
            def _(sp):
                spread_rows(sp, rel_rows, spread, s, GROUP)

            @block.tensor
            def _(pe):
                with pe.Fori(0, ITERS) as i:
                    tiles = load_tiles(nc, c, i, GROUP)
                    for u in range(GROUP):
                        if u % HALF == 0:
                            pe.wait_ge(s["hot_t"], 2 * i + 1 + u // HALF)
                        pe.wait_ge(s["placed"], GROUP * i + u + 1)
                        left = hot_t[:, u // HALF, u % HALF * P:(u % HALF + 1) * P]
                        xr = g.xr[:, bass.ds(tiles[u], 1), :].rearrange("p a c -> p (a c)")
                        for k in range(2):
                            last = nc.tensor.matmul(ps[:, u % PSB, k, 0:XRW // 2], left,
                                                    xr[:, k * XRW // 2:(k + 1) * XRW // 2], start=True, stop=True)
                        last.then_inc(s["xr"], 1)

            @block.scalar
            def _(act):
                act.sem_inc(s["placed"], PSB)
                with act.Fori(0, ITERS) as i:
                    for u in range(GROUP):
                        if u % 2 == 0:
                            act.wait_ge(s["used"], GROUP * i + u + 2)
                            nc.scalar.copy(c.idx_now[:, u:u + 2], c.idx[:, bass.ds(i * GROUP + u, 2)])
                        act.wait_ge(s["xr"], GROUP * i + u + 1)
                        nc.scalar.copy(c.e_self[:, bass.ds(i * GROUP + u, 1), :].rearrange("p a h -> p (a h)"),
                                       ps[:, u % PSB, 1, XRW // 2 - H:XRW // 2])
                        nc.scalar.copy(c.rows[:, u, :].rearrange("p (k w) -> p k w", k=2),
                                       ps[:, u % PSB, :, 0:XRW // 2]).then_inc(s["placed"], 1)

            @block.vector
            def _(dve):
                def one_hot(spread_count, half, placed):
                    dve.wait_ge(s["spread"][half], spread_count)
                    if placed is not None:
                        dve.wait_ge(s["xr"], placed)
                    nc.vector.tensor_scalar(hot_t[:, half, :], spread[:, half, :], c.part[:, 0:1], None,
                                            ALU.is_equal).then_inc(s["hot_t"], 1)

                dve.sem_inc(s["used"], GROUP)
                one_hot(16, 0, None)
                one_hot(16, 1, None)
                one_hot(32, 0, HALF)
                def scores_of_group(i, last):
                    def combine(u):
                        dve.wait_ge(s["parts"], GROUP * i + u + 1)
                        nc.vector.scalar_tensor_tensor(
                            out=c.e[:, bass.ds(i * GROUP + u, 1), 0:H], in0=part[:, u:u + 1, :], scalar=1.0 - SLOPE,
                            in1=c.rows[:, u:u + 1, HC:XLW], op0=ALU.mult, op1=ALU.add).then_inc(s["used"], 1)

                    for u in range(GROUP):
                        dve.wait_ge(s["used"], GROUP * i + u + 1)
                        dve.wait_ge(s["gathered"][u], 16 * i + 16)
                        relu_scores(nc, g, c.rows[:, u, :], part[:, u, :]).then_inc(s["parts"], 1)
                        if u > 0:
                            combine(u - 1)
                        if u % HALF == HALF - 1 and not last:
                            one_hot(16 * i + 32 + 16 * (u // HALF), 1 - u // HALF, GROUP * i + u // HALF * HALF + GROUP)
                    combine(GROUP - 1)

                with dve.Fori(0, ITERS - 1) as i:
                    scores_of_group(i, False)
                scores_of_group(ITERS - 1, True)


def gat_softmax(nc, c, scratch):
    ROWS = SLOT_BLOCKS * H * P
    flat = scratch.rearrange("p t c -> p (t c)")

    def part(k):
        return flat[0:SB, k * ROWS:(k + 1) * ROWS]

    def split(ap):
        return ap.rearrange("r (b h e) -> r b h e", b=SLOT_BLOCKS, h=H)

    def over_heads(brk):
        return brk.unsqueeze(2).to_broadcast([SB, SLOT_BLOCKS, H, P])

    er, es, run, more, brk_f, brk_b = (part(k) for k in range(6))
    with ExitStack() as ctx:
        carry = ctx.enter_context(nc.sbuf_tensor(fresh(nc, "carry"), [SB, SLOT_BLOCKS * H], F32))
        ends = ctx.enter_context(nc.sbuf_tensor(fresh(nc, "ends"), [SB, SLOT_BLOCKS * H], F32))
        over = ctx.enter_context(nc.sbuf_tensor(fresh(nc, "over"), [H, SLOTS + 2], F32))
        slot_keep = ctx.enter_context(nc.sbuf_tensor(fresh(nc, "slot_keep"), [H, SLOTS], F32))
        ps = ctx.enter_context(nc.psum_tensor(fresh(nc, "soft_ps"), [P, BANKS * BANK], F32))

        with phase(nc, masked=0, turned=0, rows=0, ends=0, slots=0, over=0, carried=0, pick=0, ex=0, vec=0, breaks=0,
                   alpha=0, back=0) as (block, s):

            @block.tensor
            def _(pe):
                for n, e in enumerate((c.e, c.e_self)):
                    if n == 0:
                        pe.wait_ge(s["masked"], 1)
                    for b in range(SLOT_BLOCKS):
                        for h in range(H):
                            at = n * ROWS + (b * H + h) * P
                            last = nc.tensor.transpose(ps[0:SB, at:at + P], e[:, b * SB:(b + 1) * SB, h], c.ident[:, :])
                    last.then_inc(s["turned"], 1)
                pe.wait_ge(s["rows"], 2)
                for n in range(4):
                    pe.wait_ge(s["ends"], n + 1)
                    for b in range(SLOT_BLOCKS):
                        last = nc.tensor.transpose(ps[0:H, b * SB:(b + 1) * SB], ends[:, b * H:(b + 1) * H],
                                                   c.ident[0:SB, 0:SB])
                    last.then_inc(s["slots"], 1)
                    pe.wait_ge(s["over"], n + 1)
                    back = n % 2 * 2
                    for b in range(SLOT_BLOCKS):
                        last = nc.tensor.transpose(ps[0:SB, BANK + b * H:BANK + (b + 1) * H],
                                                   over[:, back + b * SB:back + (b + 1) * SB], c.ident[0:H, 0:H])
                    last.then_inc(s["carried"], 1)
                pe.wait_ge(s["alpha"], 1)
                for h in range(H):
                    for b in range(SLOT_BLOCKS):
                        at = (2 + h) * BANK + b * SB
                        last = nc.tensor.transpose(ps[:, at:at + SB], part(1)[:, (b * H + h) * P:(b * H + h + 1) * P],
                                                   c.ident[0:SB, 0:SB])
                last.then_inc(s["back"], 1)

            @block.scalar
            def _(act):
                nc.scalar.copy(split(brk_f), over_heads(c.brk_before[:, :, :])).then_inc(s["breaks"], 1)
                nc.scalar.copy(split(brk_b), over_heads(c.brk_after[:, :, :])).then_inc(s["breaks"], 1)
                for n, to in enumerate((er, es)):
                    act.wait_ge(s["turned"], n + 1)
                    nc.scalar.copy(to, ps[0:SB, n * ROWS:(n + 1) * ROWS]).then_inc(s["rows"], 1)
                for n, x in enumerate((er, es)):
                    act.wait_ge(s["pick"], n + 1)
                    nc.scalar.activation(x, x, ACT.Exp).then_inc(s["ex"], 1)
                act.wait_ge(s["back"], 1)
                for h in range(H):
                    nc.scalar.mul(c.e[:, :, h], ps[:, (2 + h) * BANK:(2 + h) * BANK + SLOTS], 1.0 / H)

            @block.vector
            def _(dve):
                link = linker(dve, s["vec"])
                each = [P, SLOTS, H]
                link(nc.vector.tensor_tensor(out=c.e[:, :, 0:H], in0=c.e[:, :, 0:H],
                                             in1=c.valid[:, :].unsqueeze(2).to_broadcast(each), op=ALU.mult))
                nc.vector.tensor_tensor(out=c.e[:, :, 0:H], in0=c.e[:, :, 0:H],
                                        in1=c.invalid_neg[:, :].unsqueeze(2).to_broadcast(each), op=ALU.add)\
                  .then_inc(s["masked"], 1)
                link(nc.vector.memset(over[:, :], 0.0))
                link(nc.vector.tensor_scalar(slot_keep[:, :], c.slot_brk[:, 0, :], 0.0, None, ALU.is_equal))

                def scan(n, values, brk, through, backward, total=False):
                    step = -1 if backward else 1
                    op0, op1, start = (ALU.mult, ALU.add, 0.0) if total else (ALU.add, ALU.max, NEG)
                    link(nc.vector.tensor_tensor_scan(out=run[:, ::step], data0=brk[:, ::step],
                                                      data1=values[:, ::step], initial=start, op0=op0, op1=op1))
                    nc.vector.tensor_copy(ends[:, :], split(run)[:, :, :, 0 if backward else P - 1]
                                          .rearrange("r b h -> r (b h)")).then_inc(s["ends"], 1)
                    dve.wait_ge(s["slots"], n + 1)
                    link(nc.vector.memset(over[:, :], start))
                    brk_slot = slot_keep[:, :] if total else c.slot_brk[:, int(backward), :]
                    nc.vector.tensor_tensor_scan(out=over[:, 1:1 + SLOTS][:, ::step], data0=brk_slot[:, ::step],
                                                 data1=ps[0:H, 0:SLOTS][:, ::step], initial=start,
                                                 op0=op0, op1=op1).then_inc(s["over"], 1)
                    dve.wait_ge(s["carried"], n + 1)
                    link(nc.vector.tensor_copy(carry[:, :], ps[0:SB, BANK:BANK + SLOT_BLOCKS * H]))
                    wide = carry[:, :].rearrange("r (b h) -> r b h", h=H).unsqueeze(3)\
                        .to_broadcast([SB, SLOT_BLOCKS, H, P])
                    if total:
                        link(nc.vector.tensor_scalar(more, more, 0.0, None, ALU.is_equal))
                        link(nc.vector.tensor_tensor(out=split(more), in0=split(more), in1=wide, op=ALU.mult))
                        link(nc.vector.tensor_tensor(out=run, in0=run, in1=more, op=ALU.add))
                    else:
                        link(nc.vector.tensor_tensor(out=split(more), in0=over_heads(through), in1=wide, op=ALU.add))
                        link(nc.vector.tensor_tensor(out=run, in0=run, in1=more, op=ALU.max))

                dve.wait_ge(s["breaks"], 2)
                dve.wait_ge(s["rows"], 2)
                scan(0, er, brk_f, c.open_from_start[:, :, :], False)
                scan(1, run, brk_b, c.open_to_end[:, :, :], True)
                link(nc.vector.tensor_tensor(out=run, in0=run, in1=es, op=ALU.max))
                nc.vector.tensor_tensor(out=er, in0=er, in1=run, op=ALU.subtract).then_inc(s["pick"], 1)
                nc.vector.tensor_tensor(out=es, in0=es, in1=run, op=ALU.subtract).then_inc(s["pick"], 1)
                link(nc.vector.tensor_scalar(brk_f, brk_f, 0.0, None, ALU.is_equal))
                link(nc.vector.tensor_copy(split(more), over_heads(c.open_from_start[:, :, :])))
                dve.wait_ge(s["ex"], 2)
                scan(2, er, brk_f, None, False, total=True)
                scan(3, run, brk_b, c.open_to_end[:, :, :], True)
                link(nc.vector.tensor_tensor(out=run, in0=run, in1=es, op=ALU.add))
                link(nc.vector.reciprocal(run, run))
                nc.vector.tensor_tensor(out=es, in0=er, in1=run, op=ALU.mult)\
                  .then_inc(s["alpha"], 1)


def gat_messages(nc, c, g, xl_table, h, inv_deg):
    HOTS = 4
    with ExitStack() as ctx:
        hot = ctx.enter_context(nc.sbuf_tensor(fresh(nc, "hot_a"), [P, HOTS, H, P], F32))
        plain = ctx.enter_context(nc.sbuf_tensor(fresh(nc, "plain"), [P, 2, HALF, P], F32))
        share = ctx.enter_context(nc.sbuf_tensor(fresh(nc, "share"), [P, NODE_TILES * H], F32))
        acc = ctx.enter_context(nc.psum_tensor(fresh(nc, "acc1"), [P, BANKS * BANK], F32))
        assert HOTS == HALF

        with phase(nc, idx_ready=2, used=0, let_go=0, gathered=GROUP, hot=0, plain=0, cleared=0) as (block, s):

            @block.gpsimd
            def _(pool):
                gather_rows(nc, c, pool, c.rows[:, :, 0:XLW], xl_table, s)

            @block.scalar
            def _(act):
                with act.Fori(0, ITERS) as i:
                    for half in range(2):
                        for u in range(half * HALF, (half + 1) * HALF):
                            act.wait_ge(s["gathered"][u], 16 * i + 16)
                        next_indices(nc, c, nc.scalar.copy, i, half, s["idx_ready"], GROUP)

            @block.vector
            def _(dve):
                first_indices(nc, c, s["idx_ready"], GROUP)
                dve.sem_inc(s["used"], GROUP)
                dve.sem_inc(s["hot"], GROUP)
                nc.vector.memset(c.e[:, :, H:H + 1], 1.0)
                with dve.Fori(0, ITERS) as i:
                    for u in range(GROUP):
                        half, r = u // HALF, u % HALF
                        if r == 0:
                            dve.wait_ge(s["used"], GROUP * i + u + HALF)
                            dve.wait_ge(s["hot"], GROUP * i + u + HALF)
                            nc.vector.tensor_tensor(
                                out=plain[:, half, :, :], in0=c.iota[:, :].unsqueeze(1).to_broadcast([P, HALF, P]),
                                in1=c.rel[:, bass.ds(i * GROUP + u, HALF)].unsqueeze(2).to_broadcast([P, HALF, P]),
                                op=ALU.is_equal).then_inc(s["plain"], 1)
                            dve.wait_ge(s["plain"], 2 * i + half + 1)
                        dve.wait_ge(s["used"], GROUP * i + u + 1 + GROUP - HOTS)
                        nc.vector.tensor_tensor(
                            out=hot[:, u % HOTS, :, :],
                            in0=plain[:, half, r:r + 1, :].to_broadcast([P, H, P]),
                            in1=c.e[:, bass.ds(i * GROUP + u, 1), 0:H].rearrange("p a h -> p (a h)").unsqueeze(2)
                            .to_broadcast([P, H, P]), op=ALU.mult).then_inc(s["hot"], 1)

            @block.tensor
            def _(pe):
                clear_sums(nc, c, acc).then_inc(s["cleared"], 1)
                pe.wait_ge(s["cleared"], 1)
                with pe.Fori(0, ITERS) as i:
                    tiles = load_tiles(nc, c, i, GROUP)
                    for u in range(GROUP):
                        pe.wait_ge(s["hot"], GROUP * i + u + 1 + GROUP)
                        pe.wait_ge(s["gathered"][u], 16 * i + 16)
                        for k in range(H):
                            nc.tensor.matmul(acc[:, bass.ds(tiles[u] * C, C)], hot[:, u % HOTS, k, :],
                                             c.rows[:, u, k * C:(k + 1) * C], start=False, stop=False,
                                             skip_group_check=True)
                        nc.tensor.matmul(acc[:, bass.ds(tiles[u] * (H + 1) + SIDE, H + 1)], plain[:, u // HALF, u % HALF, :],
                                         c.e[:, bass.ds(i * GROUP + u, 1), :].rearrange("p a h -> p (a h)"),
                                         start=False, stop=False, skip_group_check=True).then_inc(s["used"], 1)

        with phase(nc, vec=0, mixed=0) as (block, s):

            @block.vector
            def _(dve):
                link = linker(dve, s["vec"])
                side = acc[:, SIDE:SIDE + NODE_TILES * (H + 1)].rearrange("p (t k) -> p t k", k=H + 1)
                link(nc.vector.tensor_scalar(share[:, :].rearrange("p (t h) -> p t h", h=H), side[:, :, 0:H],
                                             -1.0, 1.0 / H, ALU.mult, ALU.add))
                link(nc.vector.tensor_scalar(inv_deg[:, :], side[:, :, H], 1.0, None, ALU.max))
                link(nc.vector.reciprocal(inv_deg[:, :], inv_deg[:, :]))
                link(nc.vector.tensor_tensor(out=h[:, :, :], in0=h[:, :, :],
                                             in1=g.b_out[:, :].unsqueeze(1).to_broadcast([P, NODE_TILES, C]),
                                             op=ALU.add))
                for k in range(H + 1):
                    for t in range(NODE_TILES):
                        if k == 0:
                            nc.vector.tensor_tensor(out=h[:, t, :], in0=acc[:, t * C:(t + 1) * C], in1=h[:, t, :],
                                                    op=ALU.add).then_inc(s["mixed"], 1)
                        else:
                            dve.wait_ge(s["mixed"], (k - 1) * NODE_TILES + t + 1)
                            nc.vector.scalar_tensor_tensor(
                                out=h[:, t, :], in0=g.xl[:, t, (k - 1) * C:k * C],
                                scalar=share[:, t * H + k - 1:t * H + k], in1=h[:, t, :],
                                op0=ALU.mult, op1=ALU.add).then_inc(s["mixed"], 1)


def window_slots(nc, c, src, dst, lo, key, bank, place):
    HALF_W = WSLOTS // 2
    with ExitStack() as ctx:
        def sb(name, shape, dt=F32):
            return ctx.enter_context(nc.sbuf_tensor(fresh(nc, name), shape, dt))

        dst_i = sb("w_dst_i", [P, EDGE_BLOCKS, P], I32)
        src_i = sb("w_src_i", [P, EDGE_BLOCKS, P], I32)
        dst_f = sb("w_dst_f", [P, EDGE_BLOCKS, P])
        lo_i = sb("w_lo_i", [P, EDGE_BLOCKS, P], I32)
        hi_i = sb("w_hi_i", [P, EDGE_BLOCKS, P], I32)
        lo_f = sb("w_lo_f", [P, EDGE_BLOCKS, P])
        hi_f = sb("w_hi_f", [P, EDGE_BLOCKS, P])
        ends_i = sb("w_ends_i", [P, 3, EDGE_BLOCKS], I32)
        ends = sb("w_ends", [P, 3, EDGE_BLOCKS])
        tile_id = sb("w_tile_id", [P, EDGE_BLOCKS])
        real = sb("w_real", [P, EDGE_BLOCKS])
        n_slots = sb("w_n_slots", [P, EDGE_BLOCKS])
        n_before = sb("w_n_before", [P, EDGE_BLOCKS])
        first = sb("w_first", [P, EDGE_BLOCKS])
        end = sb("w_end", [P, EDGE_BLOCKS])
        shift = sb("w_shift", [P, EDGE_BLOCKS])
        shift_w = sb("w_shift_w", [P, EDGE_BLOCKS, P])
        later = sb("w_later", [P, P])
        from_first = sb("w_from_first", [P, EDGE_BLOCKS, WSLOTS])
        pick = sb("w_pick", [P, EDGE_BLOCKS, WSLOTS])
        slot_no = sb("w_slot_no", [P, WSLOTS])
        win_f = sb("w_win_f", [P, WSLOTS])
        rel = sb("w_rel", [P, WSLOTS])
        inside = sb("w_inside", [P, WSLOTS])
        spare_i = sb("w_spare_i", [P, WSLOTS], I32)
        ps = ctx.enter_context(nc.psum_tensor(fresh(nc, "win_ps"), [P, 4, 2, BANK], F32))
        LO, HI, DST, WIN = range(4)

        with phase(nc, pads=0, loads=0, iotas=0, vec=0, pe=0) as (block, s):

            @block.gpsimd
            def _(pool):
                link = linker(pool, s["iotas"])
                link(nc.gpsimd.iota(slot_no[:, :], [[1, WSLOTS]], base=0, channel_multiplier=0,
                                    allow_small_or_imprecise_dtypes=True))
                link(nc.gpsimd.iota(tile_id[:, :], [[P, EDGE_BLOCKS]], base=0, channel_multiplier=1,
                                    allow_small_or_imprecise_dtypes=True))

            @block.sync
            def _(sp):
                sp.wait_ge(s["pads"], 3)
                whole = EDGES_FULL // P * P
                for ap, to in ((dst, dst_i), (src, src_i)):
                    sp.dma_start(to[:, 0:whole // P, :],
                                 ap[0:whole * P].rearrange("(b p e) -> p b e", p=P, e=P)).then_inc(s["loads"], 16)
                    sp.dma_start(to[0:EDGES_FULL - whole, whole // P, :],
                                 ap[whole * P:EDGES_FULL * P].rearrange("(p e) -> p e", e=P)).then_inc(s["loads"], 16)
                    sp.dma_start(to[EDGES_FULL - whole:EDGES_FULL - whole + 1, whole // P, 0:EDGES_REST],
                                 ap[EDGES_FULL * P:E].rearrange("(a e) -> a e", a=1)).then_inc(s["loads"], 16)
                for b in range(EDGE_BLOCKS):
                    low, high = max(b * P, 1), min(b * P + P, EDGE_TILES)
                    sp.dma_start(ends_i[low - b * P:high - b * P, 0, b:b + 1],
                                 bass.AP(dst.tensor, dst.offset + low * P - 1, [[P, high - low], [1, 1]]),
                                 allow_slow_non_contiguous=True)\
                      .then_inc(s["loads"], 16)

            @block.vector
            def _(dve):
                nc.vector.memset(dst_i[:, :, :], WINDOWS * W_NODES).then_inc(s["pads"], 1)
                nc.vector.memset(src_i[:, :, :], 0).then_inc(s["pads"], 1)
                nc.vector.memset(ends_i[:, :, :], -W_NODES).then_inc(s["pads"], 1)
                link = linker(dve, s["vec"])
                dve.wait_ge(s["iotas"], 2)
                link(nc.vector.tensor_scalar(later[:, :], slot_no[:, 0:P], c.part[:, 0:1], None, ALU.is_gt))
                link(nc.vector.tensor_scalar(real[:, :], tile_id[:, :], float(EDGE_TILES), None, ALU.is_lt))
                dve.wait_ge(s["loads"], (6 + EDGE_BLOCKS) * 16)
                link(nc.vector.tensor_copy(ends_i[:, 1, :], dst_i[:, :, P - 1]))
                link(nc.vector.tensor_copy(ends_i[:, 2, :], dst_i[:, :, 0]))
                link(nc.vector.tensor_single_scalar(ends_i[:, :, :], ends_i[:, :, :], W_SHIFT,
                                                    op=ALU.arith_shift_right))
                link(nc.vector.tensor_copy(ends[:, :, :], ends_i[:, :, :]))
                link(nc.vector.scalar_tensor_tensor(out=ends[:, 0, :], in0=ends[:, 0, :], scalar=1.0,
                                                    in1=ends[:, 2, :], op0=ALU.add, op1=ALU.min))
                link(nc.vector.tensor_tensor(out=n_slots[:, :], in0=ends[:, 1, :], in1=ends[:, 0, :], op=ALU.subtract))
                link(nc.vector.scalar_tensor_tensor(out=n_slots[:, :], in0=n_slots[:, :], scalar=1.0, in1=real[:, :],
                                                    op0=ALU.add, op1=ALU.mult))
                link(nc.vector.memset(n_before[:, 0:1], 0.0))
                for b in range(1, EDGE_BLOCKS):
                    link(nc.vector.tensor_tensor(out=n_before[:, b:b + 1], in0=n_before[:, b - 1:b],
                                                 in1=n_slots[:, b - 1:b], op=ALU.add))
                nc.vector.tensor_copy(dst_f[:, :, :], dst_i[:, :, :])
                nc.vector.tensor_single_scalar(lo_i[:, :, :], src_i[:, :, :], P - 1, op=ALU.bitwise_and)
                link(nc.vector.tensor_single_scalar(hi_i[:, :, :], src_i[:, :, :], 7, op=ALU.arith_shift_right))
                nc.vector.tensor_copy(lo_f[:, :, :], lo_i[:, :, :])
                link(nc.vector.tensor_scalar(hi_f[:, :, :], hi_i[:, :, :], float(W_NODES), None, ALU.mult))
                dve.wait_ge(s["pe"], 1)
                link(nc.vector.tensor_copy(first[:, :], ps[:, WIN, 1, 0:EDGE_BLOCKS]))
                link(nc.vector.tensor_tensor(out=end[:, :], in0=first[:, :], in1=n_slots[:, :], op=ALU.add))
                link(nc.vector.tensor_tensor(out=shift[:, :], in0=ends[:, 0, :], in1=first[:, :], op=ALU.subtract))
                for b in range(EDGE_BLOCKS):
                    nc.vector.tensor_scalar(shift_w[:, b, :], c.ones[:, :], shift[:, b:b + 1], None, ALU.mult)
                    link(nc.vector.tensor_scalar(from_first[:, b, :], slot_no[:, :], first[:, b:b + 1], None, ALU.is_ge))
                    link(nc.vector.scalar_tensor_tensor(out=pick[:, b, :], in0=slot_no[:, :], scalar=end[:, b:b + 1],
                                                        in1=from_first[:, b, :], op0=ALU.is_lt, op1=ALU.mult))
                dve.wait_ge(s["pe"], 2)

                def halves(k):
                    return ps[:, k, :, 0:HALF_W]

                def both(ap):
                    return ap.rearrange("p (k s) -> p k s", k=2)
                link(nc.vector.tensor_tensor(out=both(win_f[:, :]), in0=halves(WIN), in1=both(slot_no[:, :]), op=ALU.add))
                link(nc.vector.tensor_scalar(win_f[:, :], win_f[:, :], float(WINDOWS), None, ALU.min))
                link(nc.vector.tensor_copy(spare_i[:, :], slot_no[:, :]))
                link(nc.vector.tensor_single_scalar(spare_i[:, :], spare_i[:, :], SPARE - 1, op=ALU.bitwise_and))
                link(nc.vector.tensor_copy(rel[:, :], spare_i[:, :]))
                link(nc.vector.scalar_tensor_tensor(out=rel[:, :], in0=rel[:, :], scalar=1.0 + WINDOWS, in1=win_f[:, :],
                                                    op0=ALU.add, op1=ALU.subtract))
                link(nc.vector.tensor_tensor(out=inside[:, 1:], in0=win_f[:, 1:], in1=win_f[:, :WSLOTS - 1],
                                             op=ALU.is_equal))
                link(nc.vector.memset(inside[:, 0:1], 0.0))
                link(nc.vector.tensor_tensor(out=rel[:, :], in0=rel[:, :], in1=inside[:, :], op=ALU.mult))
                link(nc.vector.tensor_tensor(out=rel[:, :], in0=rel[:, :], in1=win_f[:, :], op=ALU.add))
                link(nc.vector.tensor_scalar(place[:, :], rel[:, :], float(W_COLS), None, ALU.mult))
                link(nc.vector.tensor_scalar(inside[:, :], win_f[:, :], c.part[:, 0:1], None, ALU.add))
                link(nc.vector.tensor_copy(spare_i[:, :], inside[:, :]))
                link(nc.vector.tensor_single_scalar(spare_i[:, :], spare_i[:, :], BANKS - 1, op=ALU.bitwise_and))
                link(nc.vector.tensor_scalar(bank[:, :], spare_i[:, :], float(BANK), None, ALU.mult))
                link(nc.vector.tensor_copy(both(lo[:, :]), halves(LO)))
                link(nc.vector.tensor_scalar(win_f[:, :], win_f[:, :], -float(W_NODES), None, ALU.mult))
                link(nc.vector.tensor_tensor(out=both(rel[:, :]), in0=halves(DST), in1=both(win_f[:, :]), op=ALU.add))
                link(nc.vector.tensor_scalar(inside[:, :], rel[:, :], 0.0, None, ALU.is_ge))
                link(nc.vector.scalar_tensor_tensor(out=inside[:, :], in0=rel[:, :], scalar=float(W_NODES),
                                                    in1=inside[:, :], op0=ALU.is_lt, op1=ALU.mult))
                link(nc.vector.scalar_tensor_tensor(out=both(rel[:, :]), in0=both(rel[:, :]), scalar=1.0,
                                                    in1=halves(HI), op0=ALU.add, op1=ALU.add))
                link(nc.vector.tensor_tensor(out=rel[:, :], in0=rel[:, :], in1=inside[:, :], op=ALU.mult))
                link(nc.vector.tensor_scalar(key[:, :], rel[:, :], -1.0, None, ALU.add))

            @block.tensor
            def _(pe):
                V = 2 + 8 + EDGE_BLOCKS - 1
                pe.wait_ge(s["vec"], V)
                before = ps[:, WIN, 1, 0:EDGE_BLOCKS]
                nc.tensor.matmul(before, later[:, :], n_slots[:, :], start=True, stop=False)
                nc.tensor.matmul(before, c.ones[:, :], n_before[:, :], start=False, stop=True).then_inc(s["pe"], 1)
                V += 5 + 2 * EDGE_BLOCKS
                pe.wait_ge(s["vec"], V)
                for b in range(EDGE_BLOCKS):
                    for k, left in ((LO, lo_f), (HI, hi_f), (DST, dst_f), (WIN, shift_w)):
                        for half in range(2):
                            last = nc.tensor.matmul(ps[:, k, half, 0:HALF_W], left[:, b, :],
                                                    pick[:, b, half * HALF_W:(half + 1) * HALF_W], start=b == 0,
                                                    stop=b == EDGE_BLOCKS - 1)
                last.then_inc(s["pe"], 1)


def count_edges(nc, c, lo, key, bank, place, counts):
    G = 16
    HOTS = 8
    QUAD = 4
    LEAD = BANKS - 2
    with ExitStack() as ctx:
        hot_lo = ctx.enter_context(nc.sbuf_tensor(fresh(nc, "hot_lo"), [P, HOTS, P], BF16))
        hot_key = ctx.enter_context(nc.sbuf_tensor(fresh(nc, "hot_key"), [P, HOTS, W_COLS], BF16))
        numbers = ctx.enter_context(nc.sbuf_tensor(fresh(nc, "numbers"), [P, W_COLS], BF16))
        ps = ctx.enter_context(nc.psum_tensor(fresh(nc, "count_ps"), [P, BANKS * BANK], F32))

        def load(table, row, i, engine, high):
            return nc.values_load_multi_w_load_instructions(
                table[row:row + 1, bass.ds(i * G, G)], engines=[engine], min_val=0, max_val=high,
                skip_runtime_bounds_check_because="slots hold windows by construction")[1]

        with phase(nc, numbers=0, cleared=0, hot=0, added=0, taken=0) as (block, s):

            @block.gpsimd
            def _(pool):
                nc.gpsimd.iota(numbers[:, :], [[1, W_COLS]], base=0, channel_multiplier=0,
                               allow_small_or_imprecise_dtypes=True).then_inc(s["numbers"], 1)

            @block.vector
            def _(dve):
                dve.wait_ge(s["numbers"], 1)
                dve.sem_inc(s["added"], HOTS)
                with dve.Fori(0, WSLOTS // G) as i:
                    for u in range(G):
                        if u % QUAD == 0:
                            dve.wait_ge(s["added"], G * i + u + QUAD)
                        nc.vector.tensor_scalar(hot_lo[:, u % HOTS, :], numbers[:, 0:P],
                                                lo[:, bass.ds(i * G + u, 1)], None, ALU.is_equal)
                        nc.vector.tensor_scalar(hot_key[:, u % HOTS, :], numbers[:, :],
                                                key[:, bass.ds(i * G + u, 1)], None, ALU.is_equal)\
                          .then_inc(s["hot"], 1)

            @block.tensor
            def _(pe):
                for b in range(BANKS):
                    last = nc.tensor.matmul(ps[:, b * BANK:(b + 1) * BANK], c.zeros[:, 0:P], c.zeros[:, :],
                                            start=True, stop=True)
                last.then_inc(s["cleared"], 1)
                pe.wait_ge(s["cleared"], 1)
                with pe.Fori(0, WSLOTS // G) as i:
                    now = load(bank, 0, i, mybir.EngineType.PE, (BANKS - 1) * BANK)
                    following = load(bank, 1, i, mybir.EngineType.PE, (BANKS - 1) * BANK)
                    for u in range(G):
                        if u % QUAD == 0:
                            pe.wait_ge(s["hot"], G * i + u + QUAD)
                        if u % 2 == 0:
                            pe.wait_ge(s["taken"], G * i + u + 2)
                        nc.tensor.matmul(ps[:, bass.ds(now[u], W_COLS)], hot_lo[:, u % HOTS, :],
                                         hot_key[:, u % HOTS, :], start=False, stop=False, skip_group_check=True)
                        nc.tensor.matmul(ps[:, bass.ds(following[u], W_COLS)], c.zeros[:, 0:P],
                                         c.zeros[:, 0:W_COLS], start=True, stop=True, skip_group_check=True)\
                          .then_inc(s["added"], 1)

            @block.scalar
            def _(act):
                act.sem_inc(s["taken"], LEAD)
                flat = counts[:, :, :].rearrange("p w c -> p (w c)")
                with act.Fori(0, WSLOTS // G) as i:
                    before = load(bank, BANKS - 1, i, mybir.EngineType.Activation, (BANKS - 1) * BANK)
                    to = load(place, 0, i, mybir.EngineType.Activation, (WINDOWS + SPARE) * W_COLS)
                    for u in range(G):
                        if u % 2 == 0:
                            act.wait_ge(s["added"], G * i + u + 2 + HOTS)
                            act.wait_ge(s["taken"], G * i + u + 2 + LEAD - SPARE)
                        nc.scalar.copy(flat[:, bass.ds(to[u], W_COLS)], ps[:, bass.ds(before[u], W_COLS)])\
                          .then_inc(s["taken"], 1)


def dense_layer(nc, c, counts, work, h, inv_deg, x, sage=None, table=None):
    CHUNK = BANK // W_NODES
    chunks = [(w, min(CHUNK, WINDOWS - w)) for w in range(0, WINDOWS, CHUNK)]
    T = BANK // P
    BUFS = 4
    with ExitStack() as ctx:
        cnt = ctx.enter_context(nc.sbuf_tensor(fresh(nc, "cnt"), [P, BUFS, BANK], F32))
        sum_t, h_t, res = (work[:, k, :, :] for k in range(3))
        ps = ctx.enter_context(nc.psum_tensor(fresh(nc, "dense_ps"), [P, 4, 2, BANK], F32))
        SUM, TURNED, OWN, NEIGH = range(4)

        def tiles_of(q):
            return range(q * T, min(NODE_TILES, (q + 1) * T))

        def step(q, k):
            return q * NODE_TILES + k

        with phase(nc, cast_a=0, cast_d=0, used=0, summed=0, sum_t=0, turned=0, h_t=0, prod=0, vec=0, res=0,
                   stored=2) as (block, s):

            def cast(engine, copy, q, k, done):
                n = step(q, k)
                low, size = chunks[q]
                if n >= BUFS:
                    engine.wait_ge(s["used"], n - BUFS + 1)
                copy(cnt[:, n % BUFS, 0:size * W_NODES].rearrange("p (w d) -> p w d", d=W_NODES),
                     counts[:, 1 + low:1 + low + size, k * W_NODES:(k + 1) * W_NODES]).then_inc(s[done], 1)

            @block.tensor
            def _(pe):
                def turn(q):
                    if q >= 2:
                        pe.wait_ge(s["h_t"], q - 1)
                    for t in tiles_of(q):
                        last = nc.tensor.transpose(ps[:, TURNED, q % 2, t % T * P:(t % T + 1) * P], h[:, t, :],
                                                   c.ident[:, :])
                    last.then_inc(s["turned"], 1)

                def finish(q):
                    pe.wait_ge(s["sum_t"], q + 1)
                    if sage is not None:
                        pe.wait_ge(s["h_t"], q + 1)
                    if q >= 2:
                        pe.wait_ge(s["res"], q - 1)
                    for t in tiles_of(q):
                        at = slice(t % T * P, (t % T + 1) * P)
                        if sage is None:
                            last = nc.tensor.transpose(ps[:, NEIGH, q % 2, at], sum_t[:, q % 2, at], c.ident[:, :])
                        else:
                            nc.tensor.matmul(ps[:, OWN, q % 2, at], h_t[:, q % 2, at], sage[0], start=True, stop=True)
                            last = nc.tensor.matmul(ps[:, NEIGH, q % 2, at], sum_t[:, q % 2, at], sage[1],
                                                    start=True, stop=True)
                    last.then_inc(s["prod"], 1)

                for q, (low, size) in enumerate(chunks):
                    for k in range(NODE_TILES):
                        n = step(q, k)
                        if n % 2:
                            pe.wait_ge(s["cast_d"], n // 2 + 1)
                        else:
                            pe.wait_ge(s["cast_a"], n // 2 + 1)
                        if k == 0 and q >= 2:
                            pe.wait_ge(s["sum_t"], q - 1)
                        last = nc.tensor.matmul(ps[:, SUM, q % 2, 0:size * W_NODES], h[:, k, :],
                                                cnt[:, n % BUFS, 0:size * W_NODES], start=k == 0,
                                                stop=k == NODE_TILES - 1)
                        last.then_inc(s["used"], 1)
                        if k == 4 and sage is not None:
                            turn(q)
                        if k == 12 and q > 0:
                            finish(q - 1)
                finish(len(chunks) - 1)

            @block.scalar
            def _(act):
                def copy_sums(q):
                    act.wait_ge(s["used"], step(q + 1, 0))
                    if q >= 2:
                        act.wait_ge(s["prod"], q - 1)
                    size = chunks[q][1] * W_NODES
                    nc.scalar.copy(sum_t[:, q % 2, 0:size], ps[:, SUM, q % 2, 0:size]).then_inc(s["sum_t"], 1)

                for q in range(len(chunks)):
                    for k in range(NODE_TILES):
                        if step(q, k) % 2 == 0:
                            cast(act, nc.scalar.copy, q, k, "cast_a")
                        if k == 7 and q > 0:
                            copy_sums(q - 1)
                        if k == 15 and sage is not None:
                            act.wait_ge(s["turned"], q + 1)
                            size = len(tiles_of(q)) * P
                            nc.scalar.copy(h_t[:, q % 2, 0:size], ps[:, TURNED, q % 2, 0:size]).then_inc(s["h_t"], 1)
                copy_sums(len(chunks) - 1)

            @block.vector
            def _(dve):
                link = linker(dve, s["vec"])

                def result(q):
                    tiles = tiles_of(q)
                    dve.wait_ge(s["prod"], q + 1)
                    if sage is None:
                        for t in tiles:
                            last = nc.vector.scalar_tensor_tensor(
                                out=x[:, t, :], in0=ps[:, NEIGH, q % 2, t % T * P:(t % T + 1) * P],
                                scalar=inv_deg[:, t:t + 1], in1=x[:, t, :], op0=ALU.mult, op1=ALU.add)
                        last.then_inc(s["res"], 1)
                        return
                    if table is not None and q >= 2:
                        dve.wait_ge(s["stored"][q % 2], 16 * (q // 2))
                    out = res[:, q % 2, 0:len(tiles) * P].rearrange("p (t c) -> p t c", c=C)
                    link(nc.vector.tensor_tensor(
                        out=out, in0=ps[:, OWN, q % 2, 0:len(tiles) * P].rearrange("p (t c) -> p t c", c=C),
                        in1=sage[2].unsqueeze(1).to_broadcast([P, len(tiles), C]), op=ALU.add))
                    for t in tiles:
                        last = nc.vector.scalar_tensor_tensor(
                            out=out[:, t % T, :], in0=ps[:, NEIGH, q % 2, t % T * P:(t % T + 1) * P],
                            scalar=inv_deg[:, t:t + 1], in1=out[:, t % T, :], op0=ALU.mult, op1=ALU.add)
                    link(last)
                    if table is not None:
                        nc.vector.tensor_scalar(out, out, 0.0, None, ALU.max).then_inc(s["res"], 1)
                    else:
                        to = x[:, tiles[0]:tiles[-1] + 1, :]
                        nc.vector.tensor_tensor(out=to, in0=to, in1=out, op=ALU.add).then_inc(s["res"], 1)

                for q in range(len(chunks)):
                    for k in range(NODE_TILES):
                        if step(q, k) % 2:
                            cast(dve, nc.vector.tensor_copy, q, k, "cast_d")
                        if k == 18 and q > 0:
                            result(q - 1)
                result(len(chunks) - 1)

            @block.sync
            def _(sp):
                if table is not None:
                    for q in range(len(chunks)):
                        tiles = tiles_of(q)
                        sp.wait_ge(s["res"], q + 1)
                        sp.dma_start(table[tiles[0] * P:(tiles[-1] + 1) * P, :].rearrange("(t p) c -> p t c", p=P),
                                     res[:, q % 2, 0:len(tiles) * P].rearrange("p (t c) -> p t c", c=C))\
                          .then_inc(s["stored"][q % 2], 16)
                    for half in range(2):
                        sp.wait_ge(s["stored"][half], 16 * ((len(chunks) + 1 - half) // 2))


def graph_layers(nc, x_in, src, dst, gate_w, gate_b, Wl, bl, Wr, br, att, bias, ln_g, ln_b,
                 W_self1, W_neigh1, b1, W_self2, W_neigh2, b2, out):
    rel_rows = nc.dram_tensor("rel_rows", ((SLOTS + WIDE) * P,), BF16, kind="Internal").ap()
    dst_line = nc.dram_tensor("dst_line", (SLOTS * P + 2,), F32, kind="Internal").ap()
    gate_table = nc.dram_tensor("gate_table", (NODE_TILES * P, C + 1), F32, kind="Internal").ap()
    h_table = nc.dram_tensor("h_table", (NODE_TILES * P, C), F32, kind="Internal").ap()
    xl_tables = [nc.dram_tensor(f"xl_table{k}", (NODE_TILES * P, XLW), F32, kind="Internal").ap()
                 for k in range(LAYERS)]

    with ExitStack() as ctx, ExitStack() as early:
        def sb(name, shape, dt=F32, within=ctx):
            return within.enter_context(nc.sbuf_tensor(fresh(nc, name), shape, dt))

        x = sb("x", [P, NODE_TILES, C])
        h_wide = sb("h", [P, NODE_TILES, C + 1])
        h = h_wide[:, :, 0:C]
        inv_deg = sb("inv_deg", [P, NODE_TILES])
        weights = [sb(f"sage_w{k}", [P, C]) for k in range(4)]
        biases = [sb(f"sage_b{k}", [P, C]) for k in range(2)]

        class c:
            iota = sb("iota", [P, P])
            part = sb("part", [P, 1])
            ident = sb("ident", [P, P])
            ones = sb("ones", [P, P])
            zeros = sb("zeros", [P, BANK], BF16)
            rel = sb("rel", [P, SLOTS], within=early)
            idx = sb("idx", [P, SLOTS + WIDE], I32, within=early)
            idx_now = sb("idx_now", [P, WIDE], I32, within=early)
            slot_tile = sb("slot_tile", [1, SLOTS], I32, within=early)
            valid = sb("valid", [P, SLOTS], within=early)
            invalid_neg = sb("invalid_neg", [P, SLOTS], within=early)
            brk_before = sb("brk_before", [SB, SLOT_BLOCKS, P], within=early)
            brk_after = sb("brk_after", [SB, SLOT_BLOCKS, P], within=early)
            open_from_start = sb("open_from_start", [SB, SLOT_BLOCKS, P], within=early)
            open_to_end = sb("open_to_end", [SB, SLOT_BLOCKS, P], within=early)
            slot_brk = sb("slot_brk", [H, 2, SLOTS], within=early)

        with phase(nc, clear=0, loads=0) as (block, s):

            @block.vector
            def _(dve):
                nc.vector.memset(x[:, :, :], 0.0).then_inc(s["clear"], 1)

            @block.sync
            def _(sp):
                sp.wait_ge(s["clear"], 1)
                sp.dma_start(x[:, 0:NODES_FULL, :], x_in[0:NODES_FULL * P, :].rearrange("(t p) c -> p t c", p=P))\
                  .then_inc(s["loads"], 16)
                sp.dma_start(x[0:NODES_REST, NODES_FULL, :], x_in[NODES_FULL * P:N, :]).then_inc(s["loads"], 16)
                for ap, to in zip((W_self1, W_neigh1, W_self2, W_neigh2), weights):
                    sp.dma_start(to[:, :], ap).then_inc(s["loads"], 16)
                for ap, to in zip((b1, b2), biases):
                    sp.dma_start(to[:, :], rows_of(ap, 0, C)).then_inc(s["loads"], 16)
                sp.wait_ge(s["loads"], 8 * 16)

        make_slots(nc, c, src, dst, rel_rows, dst_line)

        with ExitStack() as part:
            gate_w_all = sb("gate_w_all", [P, 2 * C], within=part)
            gate_b_all = sb("gate_b_all", [P, 1], within=part)
            node_gate = sb("node_gate", [P, NODE_TILES], within=part)
            with phase(nc, loads=0) as (block, s):

                @block.sync
                def _(sp):
                    sp.dma_start(gate_w_all[:, :], rows_of(gate_w, 0, 2 * C)).then_inc(s["loads"], 16)
                    sp.dma_start(gate_b_all[:, :], rows_of(gate_b, 0, 1)).then_inc(s["loads"], 16)
                    sp.wait_ge(s["loads"], 32)

            norm_relu(nc, c, x, h, table=gate_table, dot=(gate_w_all, h_wide, node_gate))
            gated_pass(nc, c, rel_rows, gate_table, node_gate, gate_b_all[:, 0:1], x, h)

        norm_relu(nc, c, x, h)
        with ExitStack() as part:
            c.rows = sb("rows", [P, GROUP, XRW], within=part)
            c.e = sb("e", [P, SLOTS, H + 1], within=part)
            c.e_self = sb("e_self", [P, SLOTS, H], within=part)

            class g:
                xl = sb("xl", [P, NODE_TILES, XLW], within=part)
                xr = sb("xr", [P, NODE_TILES, XRW], within=part)
                w = [sb(f"w{k}", [P, XLW], within=part) for k in range(2)]
                att = sb("att_all", [P, HC], within=part)
                b_sum = sb("b_sum", [P, XLW], within=part)
                b_out = sb("b_out", [P, C], within=part)
                gain = sb("gain", [P, C], within=part)
                shift = sb("shift_ln", [P, C], within=part)

            for layer in range(LAYERS):
                gat_weights(nc, c, g, layer, Wl, Wr, bl, br, att, bias, ln_g, ln_b)
                gat_tables(nc, c, g, h, xl_tables[layer])
                gat_scores(nc, c, g, rel_rows, xl_tables[layer])
                gat_softmax(nc, c, g.xr)
                gat_messages(nc, c, g, xl_tables[layer], h, inv_deg)
                norm_relu(nc, c, h, h, gain=g.gain[:, :], shift=g.shift[:, :])

        with phase(nc, vec=0) as (block, s):

            @block.vector
            def _(dve):
                nc.vector.tensor_tensor(out=x[:, :, :], in0=x[:, :, :], in1=h[:, :, :], op=ALU.add)

        early.close()
        assert E < 1 << 16
        tables = sb("tables", [P, 4, WSLOTS])
        lo, key = tables[:, 0, :], tables[:, 1, :]
        bank, place = tables[:, 2, :].bitcast(I32), tables[:, 3, :].bitcast(I32)
        work = tables[:, :, :].rearrange("p k s -> p (k s)")[:, 0:3 * 2 * BANK]\
            .rearrange("p (k b s) -> p k b s", k=3, b=2)
        window_slots(nc, c, src, dst, lo, key, bank, place)
        counts = sb("counts", [P, 1 + WINDOWS + SPARE, W_COLS], U16)
        count_edges(nc, c, lo, key, bank, place, counts)

        norm_relu(nc, c, x, h)
        dense_layer(nc, c, counts, work, h, inv_deg, x)

        norm_relu(nc, c, x, h)
        for k in range(2):
            dense_layer(nc, c, counts, work, h, inv_deg, x,
                        sage=(weights[2 * k][:, :], weights[2 * k + 1][:, :], biases[k][:, :]),
                        table=h_table if k == 0 else None)
            with phase(nc, moved=0) as (block, s):

                @block.sync
                def _(sp):
                    if k == 0:
                        sp.dma_start(h[:, :, :], h_table.rearrange("(t p) c -> p t c", p=P)).then_inc(s["moved"], 16)
                        sp.wait_ge(s["moved"], 16)
                    else:
                        sp.dma_start(out[0:NODES_FULL * P, :].rearrange("(t p) c -> p t c", p=P),
                                     x[:, 0:NODES_FULL, :]).then_inc(s["moved"], 16)
                        sp.dma_start(out[NODES_FULL * P:N, :], x[0:NODES_REST, NODES_FULL, :])\
                          .then_inc(s["moved"], 16)
                        sp.wait_ge(s["moved"], 32)


NAMES = ["x", "src", "dst", "L0_gnn_gate_w", "L0_gnn_gate_b", "L1_gnn_Wl", "L1_gnn_bl", "L1_gnn_Wr", "L1_gnn_br",
         "L1_gnn_att", "L1_gnn_bias", "L1_gnn_ln_g", "L1_gnn_ln_b", "L3_gnn_W_self1", "L3_gnn_W_neigh1", "L3_gnn_b1",
         "L3_gnn_W_self2", "L3_gnn_W_neigh2", "L3_gnn_b2"]


def kernel(**inputs):
    import numpy as np
    import concourse.bacc as bacc
    from concourse.bass_utils import run_bass_kernel_spmd

    nc = bacc.Bacc("TRN2", target_bir_lowering=False, num_devices=1)
    arrays, args = {}, []
    for name in NAMES:
        a = np.ascontiguousarray(inputs[name])
        arrays[f"in_{name}"] = a
        args.append(nc.dram_tensor(f"in_{name}", a.shape, mybir.dt.from_np(a.dtype), kind="ExternalInput").ap())
    args.append(nc.dram_tensor("out", (N, C), F32, kind="ExternalOutput").ap())
    graph_layers(nc, *args)
    result = run_bass_kernel_spmd(nc, [arrays], core_ids=[0])
    return result.results[0]["out"]
```

```python
from contextlib import ExitStack, contextmanager

import concourse.bass as bass
from concourse import mybir

F32 = mybir.dt.float32
BF16 = mybir.dt.bfloat16
U16 = mybir.dt.uint16
I32 = mybir.dt.int32
ALU = mybir.AluOpType
ACT = mybir.ActivationFunctionType

P = 128
N = 3125
E = 50000
C = 128
H = 4
LAYERS = 2
NODE_TILES = -(-N // P)
NODES_FULL = N // P
NODES_REST = N - NODES_FULL * P
EDGE_TILES = -(-E // P)
EDGES_FULL = E // P
EDGES_REST = E - EDGES_FULL * P
EDGE_BLOCKS = -(-EDGE_TILES // P)
SLOT_BLOCKS = 4
GROUP = 8
WIDE = 16
HALF = GROUP // 2
SLOTS = -(-(EDGE_TILES + NODE_TILES - 1) // (2 * WIDE)) * 2 * WIDE
SB = SLOTS // SLOT_BLOCKS
ITERS = SLOTS // GROUP
HC = H * C
XLW = HC + H
XRW = HC + 2 * H
SIDE = NODE_TILES * C
BANK = 512
BANKS = 8
ACC_BANKS = -(-(SIDE + NODE_TILES * (H + 1)) // BANK)
W_SHIFT = 3
W_NODES = 1 << W_SHIFT
WINDOWS = -(-N // W_NODES)
W_COLS = NODE_TILES * W_NODES
SPARE = 4
WSLOTS = -(-(EDGE_TILES + WINDOWS) // 16) * 16
NEG = -1e30
LN_EPS = 1e-5
SLOPE = 0.2
L0_EPS = 0.1

assert SLOTS % SLOT_BLOCKS == 0 and SB <= P and ACC_BANKS < BANKS and SLOTS >= EDGE_TILES + NODE_TILES - 1
assert SIDE % BANK + NODE_TILES * (H + 1) <= BANK


def rows_of(ap, offset, n):
    return bass.AP(ap.tensor, ap.offset + offset, [[0, P], [1, n]])


def fresh(nc, name):
    return f"{name}_{nc.next_id()}"


def linker(engine, sem):
    count = [0]

    def link(ins):
        count[0] += 1
        ins.then_inc(sem, 1)
        engine.wait_ge(sem, count[0])

    return link


@contextmanager
def phase(nc, **counts):
    s, every = {}, []
    for name, n in counts.items():
        handles = [nc.alloc_semaphore(name=fresh(nc, name)) for _ in range(n or 1)]
        every += handles
        s[name] = handles if n else handles[0]
    with nc.Block() as block:
        yield block, s
    nc.clear_and_free_semaphores(every)
    nc.all_engine_barrier()


def make_slots(nc, c, src, dst, rel_rows, dst_line):
    with ExitStack() as ctx:
        def sb(name, shape, dt=F32):
            return ctx.enter_context(nc.sbuf_tensor(fresh(nc, name), shape, dt))

        dst_i = sb("dst_i", [P, EDGE_BLOCKS, P], I32)
        src_i = sb("src_i", [P, EDGE_BLOCKS, P], I32)
        dst_f = sb("dst_f", [P, EDGE_BLOCKS, P])
        src_f = sb("src_f", [P, EDGE_BLOCKS, P])
        span_i = sb("span_i", [P, EDGE_BLOCKS, 2], I32)
        span = sb("span", [P, EDGE_BLOCKS, 2])
        tile_id = sb("tile_id", [P, EDGE_BLOCKS])
        real = sb("real", [P, EDGE_BLOCKS])
        n_slots = sb("n_slots", [P, EDGE_BLOCKS])
        n_before = sb("n_before", [P, EDGE_BLOCKS])
        first = sb("first", [P, EDGE_BLOCKS])
        end = sb("end", [P, EDGE_BLOCKS])
        shift = sb("shift", [P, EDGE_BLOCKS])
        shift_w = sb("shift_w", [P, EDGE_BLOCKS, P])
        later = sb("later", [P, P])
        from_first = sb("from_first", [P, EDGE_BLOCKS, SLOTS])
        pick = sb("pick", [P, EDGE_BLOCKS, SLOTS])
        slot_no = sb("slot_no", [P, SLOTS])
        tile_f = sb("tile_f", [P, SLOTS])
        used_off = sb("used_off", [P, SLOTS])
        dst_slot = sb("dst_slot", [P, SLOTS])
        part_1 = sb("part_1", [P, SLOTS])
        rel_row = sb("rel_row", [SB, SLOT_BLOCKS, P], BF16)
        dst_row = sb("dst_row", [SB, SLOT_BLOCKS, P])
        dst_prev = sb("dst_prev", [SB, SLOT_BLOCKS, P])
        dst_next = sb("dst_next", [SB, SLOT_BLOCKS, P])
        outside = sb("outside", [1, 1])
        any_break = sb("any_break", [SB, 2, SLOT_BLOCKS, H])
        ps = ctx.enter_context(nc.psum_tensor(fresh(nc, "slot_ps"), [P, BANKS * BANK], F32))
        PRE, SRC, DST, TIL, USE, REL, ROW, BRK = (k * BANK for k in range(BANKS))

        with phase(nc, pads=0, loads=0, iotas=0, vec=0, pe=0, row_parts=0, rows_out=0, rows_back=0) as (block, s):

            @block.gpsimd
            def _(pool):
                link = linker(pool, s["iotas"])
                link(nc.gpsimd.iota(slot_no[:, :], [[1, SLOTS]], base=0, channel_multiplier=0,
                                    allow_small_or_imprecise_dtypes=True))
                link(nc.gpsimd.iota(tile_id[:, :], [[P, EDGE_BLOCKS]], base=0, channel_multiplier=1,
                                    allow_small_or_imprecise_dtypes=True))
                link(nc.gpsimd.memset(outside[:, :], -5.0))

            @block.sync
            def _(sp):
                sp.wait_ge(s["pads"], 2)
                whole = EDGES_FULL // P * P
                for ap, to in ((dst, dst_i), (src, src_i)):
                    sp.dma_start(to[:, 0:whole // P, :],
                                 ap[0:whole * P].rearrange("(b p e) -> p b e", p=P, e=P)).then_inc(s["loads"], 16)
                    sp.dma_start(to[0:EDGES_FULL - whole, whole // P, :],
                                 ap[whole * P:EDGES_FULL * P].rearrange("(p e) -> p e", e=P)).then_inc(s["loads"], 16)
                    sp.dma_start(to[EDGES_FULL - whole:EDGES_FULL - whole + 1, whole // P, 0:EDGES_REST],
                                 ap[EDGES_FULL * P:E].rearrange("(a e) -> a e", a=1)).then_inc(s["loads"], 16)
                sp.wait_ge(s["row_parts"], 2)
                sp.dma_start(rel_rows[0:SLOTS * P].rearrange("(b r e) -> r b e", r=SB, e=P),
                             rel_row[:, :, :]).then_inc(s["rows_out"], 16)
                sp.dma_start(rel_rows[SLOTS * P:(SLOTS + WIDE) * P].rearrange("(r e) -> r e", e=P),
                             rel_row[0:WIDE, 0, :]).then_inc(s["rows_out"], 16)
                sp.dma_start(dst_line[1:1 + SLOTS * P].rearrange("(b r e) -> r b e", r=SB, e=P),
                             dst_row[:, :, :]).then_inc(s["rows_out"], 16)
                for at in (0, 1 + SLOTS * P):
                    sp.dma_start(dst_line[at:at + 1].rearrange("(a e) -> a e", a=1),
                                 outside[:, :]).then_inc(s["rows_out"], 16)
                sp.wait_ge(s["rows_out"], 5 * 16)
                for to, at in ((dst_prev, 0), (dst_next, 2)):
                    sp.dma_start(to[:, :, :], dst_line[at:at + SLOTS * P].rearrange("(b r e) -> r b e", r=SB, e=P))\
                      .then_inc(s["rows_back"], 16)

            @block.vector
            def _(dve):
                nc.vector.memset(dst_i[:, :, :], NODE_TILES * P - 1).then_inc(s["pads"], 1)
                nc.vector.memset(src_i[:, :, :], 0).then_inc(s["pads"], 1)
                link = linker(dve, s["vec"])
                dve.wait_ge(s["iotas"], 3)
                link(nc.vector.tensor_scalar(later[:, :], slot_no[:, 0:P], c.part[:, 0:1], None, ALU.is_gt))
                link(nc.vector.tensor_scalar(real[:, :], tile_id[:, :], float(EDGE_TILES), None, ALU.is_lt))
                dve.wait_ge(s["loads"], 6 * 16)
                link(nc.vector.tensor_copy(dst_f[:, :, :], dst_i[:, :, :]))
                link(nc.vector.tensor_copy(src_f[:, :, :], src_i[:, :, :]))
                link(nc.vector.tensor_single_scalar(span_i[:, :, :], dst_i[:, :, 0:P:P - 1], 7,
                                                    op=ALU.arith_shift_right))
                link(nc.vector.tensor_copy(span[:, :, :], span_i[:, :, :]))
                link(nc.vector.tensor_tensor(out=n_slots[:, :], in0=span[:, :, 1], in1=span[:, :, 0], op=ALU.subtract))
                link(nc.vector.scalar_tensor_tensor(out=n_slots[:, :], in0=n_slots[:, :], scalar=1.0, in1=real[:, :],
                                                    op0=ALU.add, op1=ALU.mult))
                link(nc.vector.memset(n_before[:, 0:1], 0.0))
                for b in range(1, EDGE_BLOCKS):
                    link(nc.vector.tensor_tensor(out=n_before[:, b:b + 1], in0=n_before[:, b - 1:b],
                                                 in1=n_slots[:, b - 1:b], op=ALU.add))
                dve.wait_ge(s["pe"], 1)
                link(nc.vector.tensor_copy(first[:, :], ps[:, PRE:PRE + EDGE_BLOCKS]))
                link(nc.vector.tensor_tensor(out=end[:, :], in0=first[:, :], in1=n_slots[:, :], op=ALU.add))
                link(nc.vector.tensor_tensor(out=shift[:, :], in0=span[:, :, 0], in1=first[:, :], op=ALU.subtract))
                for b in range(EDGE_BLOCKS):
                    nc.vector.tensor_scalar(shift_w[:, b, :], c.ones[:, :], shift[:, b:b + 1], None, ALU.mult)
                    link(nc.vector.tensor_scalar(from_first[:, b, :], slot_no[:, :], first[:, b:b + 1], None, ALU.is_ge))
                    link(nc.vector.scalar_tensor_tensor(out=pick[:, b, :], in0=slot_no[:, :], scalar=end[:, b:b + 1],
                                                        in1=from_first[:, b, :], op0=ALU.is_lt, op1=ALU.mult))
                dve.wait_ge(s["pe"], 2)
                link(nc.vector.tensor_tensor(out=tile_f[:, :], in0=ps[:, TIL:TIL + SLOTS], in1=slot_no[:, :], op=ALU.add))
                link(nc.vector.tensor_tensor(out=tile_f[:, :], in0=ps[:, USE:USE + SLOTS], in1=tile_f[:, :], op=ALU.mult))
                link(nc.vector.tensor_copy(c.slot_tile[0:1, :], tile_f[0:1, :]))
                link(nc.vector.memset(c.idx[:, :], 0))
                link(nc.vector.tensor_copy(c.idx[:, 0:SLOTS], ps[:, SRC:SRC + SLOTS]))
                link(nc.vector.tensor_copy(dst_slot[:, :], ps[:, DST:DST + SLOTS]))
                link(nc.vector.tensor_scalar(used_off[:, :], ps[:, USE:USE + SLOTS], 1000.0, -1000.0, ALU.mult, ALU.add))
                link(nc.vector.scalar_tensor_tensor(out=c.rel[:, :], in0=tile_f[:, :], scalar=-float(P),
                                                    in1=dst_slot[:, :], op0=ALU.mult, op1=ALU.add))
                link(nc.vector.tensor_tensor(out=c.rel[:, :], in0=c.rel[:, :], in1=used_off[:, :], op=ALU.add))
                link(nc.vector.tensor_scalar(part_1[:, :], c.rel[:, :], 0.0, None, ALU.is_ge))
                link(nc.vector.scalar_tensor_tensor(out=c.valid[:, :], in0=c.rel[:, :], scalar=float(P),
                                                    in1=part_1[:, :], op0=ALU.is_lt, op1=ALU.mult))
                link(nc.vector.tensor_scalar(c.invalid_neg[:, :], c.valid[:, :], -1.0, -NEG, ALU.add, ALU.mult))
                dve.wait_ge(s["pe"], 3)
                nc.vector.tensor_copy(rel_row[:, :, :], ps[0:SB, REL:REL + BANK].rearrange("r (b e) -> r b e", e=P))\
                  .then_inc(s["row_parts"], 1)
                nc.vector.tensor_copy(dst_row[:, :, :], ps[0:SB, ROW:ROW + BANK].rearrange("r (b e) -> r b e", e=P))\
                  .then_inc(s["row_parts"], 1)
                dve.wait_ge(s["row_parts"], 2)
                dve.wait_ge(s["rows_back"], 32)
                for k, other, own, through in ((0, dst_prev, c.brk_before, c.open_from_start),
                                               (1, dst_next, c.brk_after, c.open_to_end)):
                    link(nc.vector.tensor_tensor(out=own[:, :, :], in0=dst_row[:, :, :], in1=other[:, :, :],
                                                 op=ALU.is_equal))
                    link(nc.vector.tensor_scalar(own[:, :, :], own[:, :, :], -1.0, -NEG, ALU.add, ALU.mult))
                    for b in range(SLOT_BLOCKS):
                        step = 1 if k == 0 else -1
                        link(nc.vector.tensor_tensor_scan(out=through[:, b, ::step], data0=own[:, b, ::step],
                                                          data1=own[:, b, ::step], initial=0.0,
                                                          op0=ALU.min, op1=ALU.min))
                    edge = P - 1 if k == 0 else 0
                    for h in range(H):
                        link(nc.vector.tensor_copy(any_break[:, k, :, h], through[:, :, edge]))
                    link(nc.vector.memset(own[:, :, P - 1 - edge:P - edge], NEG))
                dve.wait_ge(s["pe"], 4)
                link(nc.vector.tensor_copy(c.slot_brk[:, 0, :], ps[0:H, BRK:BRK + SLOTS]))
                link(nc.vector.tensor_copy(c.slot_brk[:, 1, :], ps[0:H, PRE:PRE + SLOTS]))

            @block.tensor
            def _(pe):
                V = 2 + 7 + EDGE_BLOCKS - 1
                pe.wait_ge(s["vec"], V)
                nc.tensor.matmul(ps[:, PRE:PRE + EDGE_BLOCKS], later[:, :], n_slots[:, :], start=True, stop=False)
                nc.tensor.matmul(ps[:, PRE:PRE + EDGE_BLOCKS], c.ones[:, :], n_before[:, :], start=False, stop=True)\
                  .then_inc(s["pe"], 1)
                V += 3 + 2 * EDGE_BLOCKS
                pe.wait_ge(s["vec"], V)
                for b in range(EDGE_BLOCKS):
                    for at, left in ((SRC, src_f[:, b, :]), (DST, dst_f[:, b, :]), (TIL, shift_w[:, b, :]),
                                     (USE, c.ones[:, :])):
                        last = nc.tensor.matmul(ps[:, at:at + SLOTS], left, pick[:, b, :], start=b == 0,
                                                stop=b == EDGE_BLOCKS - 1)
                last.then_inc(s["pe"], 1)
                V += 12
                pe.wait_ge(s["vec"], V)
                for b in range(SLOT_BLOCKS):
                    nc.tensor.transpose(ps[0:SB, REL + b * P:REL + (b + 1) * P], c.rel[:, b * SB:(b + 1) * SB],
                                        c.ident[:, :])
                    last = nc.tensor.transpose(ps[0:SB, ROW + b * P:ROW + (b + 1) * P],
                                               dst_slot[:, b * SB:(b + 1) * SB], c.ident[:, :])
                last.then_inc(s["pe"], 1)
                pe.wait_ge(s["vec"], V + 2 * (2 + SLOT_BLOCKS + H + 1))
                for k, at in ((0, BRK), (1, PRE)):
                    for b in range(SLOT_BLOCKS):
                        last = nc.tensor.transpose(ps[0:H, at + b * SB:at + (b + 1) * SB], any_break[:, k, b, :],
                                                   c.ident[0:SB, 0:SB])
                last.then_inc(s["pe"], 1)


def norm_relu(nc, c, x, out, gain=None, shift=None, dot=None):
    ACT_TILES = 10
    with ExitStack() as ctx:
        stats = ctx.enter_context(nc.sbuf_tensor(fresh(nc, "stats"), [P, NODE_TILES, 6], F32))
        mean_var = ctx.enter_context(nc.sbuf_tensor(fresh(nc, "mean_var"), [P, NODE_TILES, 2], F32))
        std = ctx.enter_context(nc.sbuf_tensor(fresh(nc, "std"), [P, NODE_TILES], F32))
        rstd = ctx.enter_context(nc.sbuf_tensor(fresh(nc, "rstd"), [P, NODE_TILES], F32))
        bias = ctx.enter_context(nc.sbuf_tensor(fresh(nc, "norm_bias"), [P, NODE_TILES], F32))
        if dot is not None:
            prod = ctx.enter_context(nc.sbuf_tensor(fresh(nc, "prod"), [P, C], F32))

        with phase(nc, stats=0, var=0, std=0, scaled=0, shifted=0, rows=0, vec=0) as (block, s):

            @block.vector
            def _(dve):
                link = linker(dve, s["vec"])
                for t in range(NODE_TILES):
                    nc.vector.bn_stats(stats[:, t, :], x[:, t, :]).then_inc(s["stats"], 1)
                for t in range(NODE_TILES):
                    dve.wait_ge(s["stats"], t + 1)
                    nc.vector.bn_aggr(mean_var[:, t, :], stats[:, t, :]).then_inc(s["var"], 1)
                dve.wait_ge(s["var"], NODE_TILES)
                link(nc.vector.tensor_scalar(std[:, :], mean_var[:, :, 1], LN_EPS, None, ALU.add))
                dve.wait_ge(s["std"], 1)
                link(nc.vector.reciprocal(rstd[:, :], std[:, :]))
                link(nc.vector.scalar_tensor_tensor(out=bias[:, :], in0=mean_var[:, :, 0], scalar=-1.0,
                                                    in1=rstd[:, :], op0=ALU.mult, op1=ALU.mult))
                if gain is not None:
                    for t in range(NODE_TILES):
                        nc.vector.scalar_tensor_tensor(out=out[:, t, :], in0=x[:, t, :], scalar=mean_var[:, t, 0:1],
                                                       in1=gain, op0=ALU.subtract, op1=ALU.mult)\
                          .then_inc(s["scaled"], 1)
                    for t in range(NODE_TILES):
                        dve.wait_ge(s["scaled"], t + 1)
                        nc.vector.scalar_tensor_tensor(out=out[:, t, :], in0=out[:, t, :], scalar=rstd[:, t:t + 1],
                                                       in1=shift, op0=ALU.mult, op1=ALU.add).then_inc(s["shifted"], 1)
                    return
                for t in range(ACT_TILES, NODE_TILES):
                    nc.vector.tensor_scalar(out[:, t, :], x[:, t, :], rstd[:, t:t + 1], bias[:, t:t + 1],
                                            ALU.mult, ALU.add).then_inc(s["scaled"], 1)
                dve.wait_ge(s["scaled"], NODE_TILES - ACT_TILES)
                mine = out[:, ACT_TILES:NODE_TILES, :]
                nc.vector.tensor_scalar(mine, mine, 0.0, None, ALU.max).then_inc(s["rows"], 1)
                if dot is not None:
                    dve.wait_ge(s["rows"], 1 + ACT_TILES)
                    for k in range(2):
                        for t in range(NODE_TILES):
                            link(nc.vector.scalar_tensor_tensor(
                                out=prod[:, :], in0=out[:, t, :], scalar=1.0, in1=dot[0][:, k * C:(k + 1) * C],
                                op0=ALU.mult, op1=ALU.mult,
                                accum_out=dot[2][:, t:t + 1] if k else dot[1][:, t, C:C + 1]))

            @block.scalar
            def _(act):
                act.wait_ge(s["vec"], 1)
                nc.scalar.activation(std[:, :], std[:, :], ACT.Sqrt).then_inc(s["std"], 1)
                if gain is not None:
                    for t in range(0, NODE_TILES, 5):
                        act.wait_ge(s["shifted"], t + 5)
                        nc.scalar.activation(out[:, t:t + 5, :], out[:, t:t + 5, :], ACT.Relu)
                    return
                act.wait_ge(s["vec"], 3)
                for t in range(ACT_TILES):
                    nc.scalar.activation(out[:, t, :], x[:, t, :], ACT.Relu, bias=bias[:, t:t + 1],
                                         scale=rstd[:, t:t + 1]).then_inc(s["rows"], 1)


def first_indices(nc, c, idx_ready, group):
    n = group // 2
    for half in range(2):
        nc.vector.tensor_copy(c.idx_now[:, half * n:(half + 1) * n],
                              c.idx[:, half * n:(half + 1) * n]).then_inc(idx_ready[half], 1)


def gather_rows(nc, c, pool, rows, table, s, filled=None):
    group = rows.shape[1]
    n = group // 2
    with pool.Fori(0, SLOTS // group) as i:
        for u in range(group):
            half = u // n
            if filled is None and u % n == 0:
                pool.wait_ge(s["idx_ready"][half], i + 1)
                pool.wait_ge(s["used"], group * i + (half + 1) * n)
            elif filled is not None:
                pool.wait_ge(filled, group * i + u + 1 + HALF)
            if filled is not None or u % n == 0:
                pool.sem_inc(s["let_go"], 1)
            nc.gpsimd.indirect_dma_start(
                out=rows[:, u, :], out_offset=None, in_=table,
                in_offset=bass.IndirectOffsetOnAxis(ap=c.idx_now[:, u:u + 1], axis=0),
                compute_op=ALU.bypass if filled is None else ALU.add).then_inc(s["gathered"][u], 16)


def next_indices(nc, c, copy, i, half, idx_ready, group):
    n = group // 2
    copy(c.idx_now[:, half * n:(half + 1) * n],
         c.idx[:, bass.ds((i + 1) * group + half * n, n)]).then_inc(idx_ready[half], 1)


def load_tiles(nc, c, i, group):
    return nc.values_load_multi_w_load_instructions(
        c.slot_tile[0:1, bass.ds(i * group, group)], engines=[mybir.EngineType.PE], min_val=0,
        max_val=NODE_TILES - 1, skip_runtime_bounds_check_because="slots hold node tiles by construction")[1]


def clear_sums(nc, c, acc):
    for b in range(ACC_BANKS):
        last = nc.tensor.matmul(acc[:, b * BANK:(b + 1) * BANK], c.zeros[:, 0:P], c.zeros[:, :], start=True, stop=True)
    return last


def spread_rows(sp, rel_rows, spread, s, group):
    n = group // 2

    def load(first_slot, half):
        sp.dma_start(spread[:, half, :], bass.AP(rel_rows.tensor, (first_slot + half * n) * P,
                                                 [[0, P], [1, n * P]])).then_inc(s["spread"][half], 16)
    for half in range(2):
        load(0, half)
    with sp.Fori(0, SLOTS // group) as i:
        for half in range(2):
            sp.wait_ge(s["hot_t"], 2 * i + 1 + half)
            load((i + 1) * group, half)
    for half in range(2):
        sp.wait_ge(s["spread"][half], 16 * (SLOTS // group + 1))


def gat_weights(nc, c, g, layer, Wl, Wr, bl, br, att, bias, ln_g, ln_b):
    with nc.sbuf_tensor(fresh(nc, "prod_w"), [P, C], F32) as prod, nc.sbuf_tensor(fresh(nc, "bl_all"), [P, HC], F32) as bl_all:
        with phase(nc, loads=0, vec=0) as (block, s):

            @block.sync
            def _(sp):
                sp.dma_start(g.w[0][:, 0:HC], Wl[layer, :, :]).then_inc(s["loads"], 16)
                sp.dma_start(g.w[1][:, 0:HC], Wr[layer, :, :]).then_inc(s["loads"], 16)
                sp.dma_start(g.att[:, :], rows_of(att, layer * HC, HC)).then_inc(s["loads"], 16)
                sp.dma_start(bl_all[:, :], rows_of(bl, layer * HC, HC)).then_inc(s["loads"], 16)
                sp.dma_start(g.b_sum[:, 0:HC], rows_of(br, layer * HC, HC)).then_inc(s["loads"], 16)
                sp.dma_start(g.b_out[:, :], rows_of(bias, layer * C, C)).then_inc(s["loads"], 16)
                sp.dma_start(g.gain[:, :], rows_of(ln_g, layer * C, C)).then_inc(s["loads"], 16)
                sp.dma_start(g.shift[:, :], rows_of(ln_b, layer * C, C)).then_inc(s["loads"], 16)

            @block.vector
            def _(dve):
                link = linker(dve, s["vec"])
                dve.wait_ge(s["loads"], 8 * 16)
                link(nc.vector.tensor_tensor(out=g.b_sum[:, 0:HC], in0=g.b_sum[:, 0:HC], in1=bl_all[:, :], op=ALU.add))
                for m in (g.w[0], g.w[1], g.b_sum):
                    for h in range(H):
                        link(nc.vector.scalar_tensor_tensor(
                            out=prod[:, :], in0=m[:, h * C:(h + 1) * C], scalar=SLOPE, in1=g.att[:, h * C:(h + 1) * C],
                            op0=ALU.mult, op1=ALU.mult, accum_out=m[:, HC + h:HC + h + 1]))
                for h in range(H):
                    link(nc.vector.scalar_tensor_tensor(out=g.b_out[:, :], in0=bl_all[:, h * C:(h + 1) * C],
                                                        scalar=1.0 / H, in1=g.b_out[:, :], op0=ALU.mult, op1=ALU.add))


def gat_tables(nc, c, g, h, xl_table):
    U = 5
    with ExitStack() as ctx:
        h_t = ctx.enter_context(nc.sbuf_tensor(fresh(nc, "h_t"), [P, 2, P], F32))
        part = ctx.enter_context(nc.sbuf_tensor(fresh(nc, "self_part"), [P, NODE_TILES, H], F32))
        ps = ctx.enter_context(nc.psum_tensor(fresh(nc, "tab_ps"), [P, 4, 2, BANK], F32))
        TURNED, LEFT, RIGHT, LINEAR = range(4)

        with phase(nc, turned=0, h_t=0, proj=0, xl=0, xr=0, lin=0, z=0, parts=0, z_used=0, stored=0) as (block, s):

            @block.tensor
            def _(pe):
                def turn(t):
                    nc.tensor.transpose(ps[:, TURNED, t % 2, 0:P], h[:, t, :], c.ident[:, :]).then_inc(s["turned"], 1)

                turn(0)
                for t in range(NODE_TILES):
                    if t + 1 < NODE_TILES:
                        turn(t + 1)
                    pe.wait_ge(s["h_t"], t + 1)
                    if t >= 2:
                        pe.wait_ge(s["xl"], t - 1)
                        pe.wait_ge(s["xr"], t - 1)
                    nc.tensor.matmul(ps[:, LEFT, t % 2, :], h_t[:, t % 2, :], g.w[0][:, 0:HC], start=True, stop=True)
                    nc.tensor.matmul(ps[:, RIGHT, t % 2, :], h_t[:, t % 2, :], g.w[1][:, 0:HC], start=True, stop=True)
                    for k in range(2):
                        last = nc.tensor.matmul(ps[:, LINEAR, t % 2, k * H:(k + 1) * H], h_t[:, t % 2, :],
                                                g.w[k][:, HC:XLW], start=True, stop=True)
                    last.then_inc(s["proj"], 1)

            @block.scalar
            def _(act):
                def take_turned(t):
                    act.wait_ge(s["turned"], t + 1)
                    if t >= 2:
                        act.wait_ge(s["proj"], t - 1)
                    nc.scalar.copy(h_t[:, t % 2, :], ps[:, TURNED, t % 2, 0:P]).then_inc(s["h_t"], 1)

                take_turned(0)
                for t in range(NODE_TILES):
                    if t + 1 < NODE_TILES:
                        take_turned(t + 1)
                    act.wait_ge(s["proj"], t + 1)
                    nc.scalar.copy(g.xl[:, t, 0:HC], ps[:, LEFT, t % 2, :]).then_inc(s["xl"], 1)

            @block.gpsimd
            def _(pool):
                for t in range(NODE_TILES):
                    pool.wait_ge(s["xl"], t + 1)
                    pool.wait_ge(s["xr"], t + 1)
                    pool.wait_ge(s["z_used"], t + 1)
                    nc.gpsimd.tensor_tensor(out=c.rows[:, t % U, 0:HC], in0=g.xl[:, t, 0:HC], in1=g.xr[:, t, 0:HC],
                                            op=ALU.add).then_inc(s["z"], 1)

            @block.vector
            def _(dve):
                def scores_of(t):
                    dve.wait_ge(s["z"], t + 1)
                    relu_scores(nc, g, c.rows[:, t % U, :], part[:, t, :]).then_inc(s["z_used"], 1)

                dve.sem_inc(s["z_used"], U)
                LAG = 2
                for t in range(NODE_TILES):
                    dve.wait_ge(s["proj"], t + 1)
                    nc.vector.tensor_copy(g.xl[:, t, HC:XLW], ps[:, LINEAR, t % 2, 0:H]).then_inc(s["lin"], 1)
                    nc.vector.tensor_tensor(out=g.xr[:, t, HC:XLW], in0=ps[:, LINEAR, t % 2, H:2 * H],
                                            in1=g.b_sum[:, HC:XLW], op=ALU.add)
                    nc.vector.tensor_tensor(out=g.xr[:, t, 0:HC], in0=ps[:, RIGHT, t % 2, :],
                                            in1=g.b_sum[:, 0:HC], op=ALU.add).then_inc(s["xr"], 1)
                    if t >= LAG:
                        scores_of(t - LAG)
                for t in range(NODE_TILES - LAG, NODE_TILES):
                    scores_of(t)
                own = g.xr[:, :, XLW:XRW]
                dve.wait_ge(s["z_used"], U + NODE_TILES)
                dve.wait_ge(s["xr"], NODE_TILES)
                nc.vector.tensor_tensor(out=own, in0=g.xl[:, :, HC:XLW], in1=g.xr[:, :, HC:XLW], op=ALU.add)\
                  .then_inc(s["parts"], 1)
                dve.wait_ge(s["parts"], 1)
                nc.vector.scalar_tensor_tensor(out=own, in0=part[:, :, :], scalar=1.0 - SLOPE, in1=own,
                                               op0=ALU.mult, op1=ALU.add)

            @block.sync
            def _(sp):
                for t in range(NODE_TILES):
                    sp.wait_ge(s["xl"], t + 1)
                    sp.wait_ge(s["lin"], t + 1)
                    sp.dma_start(xl_table[t * P:(t + 1) * P, :], g.xl[:, t, :]).then_inc(s["stored"], 16)
                sp.wait_ge(s["stored"], 16 * NODE_TILES)


def relu_scores(nc, g, z, part):
    for h in range(H):
        last = nc.vector.scalar_tensor_tensor(out=z[:, h * C:(h + 1) * C], in0=z[:, h * C:(h + 1) * C], scalar=0.0,
                                              in1=g.att[:, h * C:(h + 1) * C], op0=ALU.max, op1=ALU.mult,
                                              accum_out=part[:, h:h + 1])
    return last


def gat_scores(nc, c, g, rel_rows, xl_table):
    PSB = 4
    with ExitStack() as ctx:
        hot_t = ctx.enter_context(nc.sbuf_tensor(fresh(nc, "hot_ta"), [P, 2, HALF * P], F32))
        spread = ctx.enter_context(nc.sbuf_tensor(fresh(nc, "spread_a"), [P, 2, HALF * P], BF16))
        part = ctx.enter_context(nc.sbuf_tensor(fresh(nc, "edge_part"), [P, GROUP, H], F32))
        ps = ctx.enter_context(nc.psum_tensor(fresh(nc, "xr_ps"), [P, PSB, 2, BANK], F32))
        assert PSB == HALF

        with phase(nc, used=0, let_go=0, gathered=GROUP, spread=2, hot_t=0, xr=0, placed=0, parts=0) as (block, s):

            @block.gpsimd
            def _(pool):
                gather_rows(nc, c, pool, c.rows[:, :, 0:XLW], xl_table, s, filled=s["placed"])

            @block.sync
            def _(sp):
                spread_rows(sp, rel_rows, spread, s, GROUP)

            @block.tensor
            def _(pe):
                with pe.Fori(0, ITERS) as i:
                    tiles = load_tiles(nc, c, i, GROUP)
                    for u in range(GROUP):
                        if u % HALF == 0:
                            pe.wait_ge(s["hot_t"], 2 * i + 1 + u // HALF)
                        pe.wait_ge(s["placed"], GROUP * i + u + 1)
                        left = hot_t[:, u // HALF, u % HALF * P:(u % HALF + 1) * P]
                        xr = g.xr[:, bass.ds(tiles[u], 1), :].rearrange("p a c -> p (a c)")
                        for k in range(2):
                            last = nc.tensor.matmul(ps[:, u % PSB, k, 0:XRW // 2], left,
                                                    xr[:, k * XRW // 2:(k + 1) * XRW // 2], start=True, stop=True)
                        last.then_inc(s["xr"], 1)

            @block.scalar
            def _(act):
                act.sem_inc(s["placed"], PSB)
                with act.Fori(0, ITERS) as i:
                    for u in range(GROUP):
                        if u % 2 == 0:
                            act.wait_ge(s["used"], GROUP * i + u + 2)
                            nc.scalar.copy(c.idx_now[:, u:u + 2], c.idx[:, bass.ds(i * GROUP + u, 2)])
                        act.wait_ge(s["xr"], GROUP * i + u + 1)
                        nc.scalar.copy(c.e_self[:, bass.ds(i * GROUP + u, 1), :].rearrange("p a h -> p (a h)"),
                                       ps[:, u % PSB, 1, XRW // 2 - H:XRW // 2])
                        nc.scalar.copy(c.rows[:, u, :].rearrange("p (k w) -> p k w", k=2),
                                       ps[:, u % PSB, :, 0:XRW // 2]).then_inc(s["placed"], 1)

            @block.vector
            def _(dve):
                def one_hot(spread_count, half, placed):
                    dve.wait_ge(s["spread"][half], spread_count)
                    if placed is not None:
                        dve.wait_ge(s["xr"], placed)
                    nc.vector.tensor_scalar(hot_t[:, half, :], spread[:, half, :], c.part[:, 0:1], None,
                                            ALU.is_equal).then_inc(s["hot_t"], 1)

                dve.sem_inc(s["used"], GROUP)
                one_hot(16, 0, None)
                one_hot(16, 1, None)
                one_hot(32, 0, HALF)
                def scores_of_group(i, last):
                    def combine(u):
                        dve.wait_ge(s["parts"], GROUP * i + u + 1)
                        nc.vector.scalar_tensor_tensor(
                            out=c.e[:, bass.ds(i * GROUP + u, 1), 0:H], in0=part[:, u:u + 1, :], scalar=1.0 - SLOPE,
                            in1=c.rows[:, u:u + 1, HC:XLW], op0=ALU.mult, op1=ALU.add).then_inc(s["used"], 1)

                    for u in range(GROUP):
                        dve.wait_ge(s["used"], GROUP * i + u + 1)
                        dve.wait_ge(s["gathered"][u], 16 * i + 16)
                        relu_scores(nc, g, c.rows[:, u, :], part[:, u, :]).then_inc(s["parts"], 1)
                        if u > 0:
                            combine(u - 1)
                        if u % HALF == HALF - 1 and not last:
                            one_hot(16 * i + 32 + 16 * (u // HALF), 1 - u // HALF, GROUP * i + u // HALF * HALF + GROUP)
                    combine(GROUP - 1)

                with dve.Fori(0, ITERS - 1) as i:
                    scores_of_group(i, False)
                scores_of_group(ITERS - 1, True)


def gat_softmax(nc, c, scratch):
    ROWS = SLOT_BLOCKS * H * P
    flat = scratch.rearrange("p t c -> p (t c)")

    def part(k):
        return flat[0:SB, k * ROWS:(k + 1) * ROWS]

    def split(ap):
        return ap.rearrange("r (b h e) -> r b h e", b=SLOT_BLOCKS, h=H)

    def over_heads(brk):
        return brk.unsqueeze(2).to_broadcast([SB, SLOT_BLOCKS, H, P])

    er, es, run, more, brk_f, brk_b = (part(k) for k in range(6))
    with ExitStack() as ctx:
        carry = ctx.enter_context(nc.sbuf_tensor(fresh(nc, "carry"), [SB, SLOT_BLOCKS * H], F32))
        ends = ctx.enter_context(nc.sbuf_tensor(fresh(nc, "ends"), [SB, SLOT_BLOCKS * H], F32))
        over = ctx.enter_context(nc.sbuf_tensor(fresh(nc, "over"), [H, SLOTS + 2], F32))
        slot_keep = ctx.enter_context(nc.sbuf_tensor(fresh(nc, "slot_keep"), [H, SLOTS], F32))
        ps = ctx.enter_context(nc.psum_tensor(fresh(nc, "soft_ps"), [P, BANKS * BANK], F32))

        with phase(nc, masked=0, turned=0, rows=0, ends=0, slots=0, over=0, carried=0, pick=0, ex=0, vec=0, breaks=0,
                   alpha=0, back=0) as (block, s):

            @block.tensor
            def _(pe):
                for n, e in enumerate((c.e, c.e_self)):
                    if n == 0:
                        pe.wait_ge(s["masked"], 1)
                    for b in range(SLOT_BLOCKS):
                        for h in range(H):
                            at = n * ROWS + (b * H + h) * P
                            last = nc.tensor.transpose(ps[0:SB, at:at + P], e[:, b * SB:(b + 1) * SB, h], c.ident[:, :])
                    last.then_inc(s["turned"], 1)
                pe.wait_ge(s["rows"], 2)
                for n in range(4):
                    pe.wait_ge(s["ends"], n + 1)
                    for b in range(SLOT_BLOCKS):
                        last = nc.tensor.transpose(ps[0:H, b * SB:(b + 1) * SB], ends[:, b * H:(b + 1) * H],
                                                   c.ident[0:SB, 0:SB])
                    last.then_inc(s["slots"], 1)
                    pe.wait_ge(s["over"], n + 1)
                    back = n % 2 * 2
                    for b in range(SLOT_BLOCKS):
                        last = nc.tensor.transpose(ps[0:SB, BANK + b * H:BANK + (b + 1) * H],
                                                   over[:, back + b * SB:back + (b + 1) * SB], c.ident[0:H, 0:H])
                    last.then_inc(s["carried"], 1)
                pe.wait_ge(s["alpha"], 1)
                for h in range(H):
                    for b in range(SLOT_BLOCKS):
                        at = (2 + h) * BANK + b * SB
                        last = nc.tensor.transpose(ps[:, at:at + SB], part(1)[:, (b * H + h) * P:(b * H + h + 1) * P],
                                                   c.ident[0:SB, 0:SB])
                last.then_inc(s["back"], 1)

            @block.scalar
            def _(act):
                nc.scalar.copy(split(brk_f), over_heads(c.brk_before[:, :, :])).then_inc(s["breaks"], 1)
                nc.scalar.copy(split(brk_b), over_heads(c.brk_after[:, :, :])).then_inc(s["breaks"], 1)
                for n, to in enumerate((er, es)):
                    act.wait_ge(s["turned"], n + 1)
                    nc.scalar.copy(to, ps[0:SB, n * ROWS:(n + 1) * ROWS]).then_inc(s["rows"], 1)
                for n, x in enumerate((er, es)):
                    act.wait_ge(s["pick"], n + 1)
                    nc.scalar.activation(x, x, ACT.Exp).then_inc(s["ex"], 1)
                act.wait_ge(s["back"], 1)
                for h in range(H):
                    nc.scalar.mul(c.e[:, :, h], ps[:, (2 + h) * BANK:(2 + h) * BANK + SLOTS], 1.0 / H)

            @block.vector
            def _(dve):
                link = linker(dve, s["vec"])
                each = [P, SLOTS, H]
                link(nc.vector.tensor_tensor(out=c.e[:, :, 0:H], in0=c.e[:, :, 0:H],
                                             in1=c.valid[:, :].unsqueeze(2).to_broadcast(each), op=ALU.mult))
                nc.vector.tensor_tensor(out=c.e[:, :, 0:H], in0=c.e[:, :, 0:H],
                                        in1=c.invalid_neg[:, :].unsqueeze(2).to_broadcast(each), op=ALU.add)\
                  .then_inc(s["masked"], 1)
                link(nc.vector.memset(over[:, :], 0.0))
                link(nc.vector.tensor_scalar(slot_keep[:, :], c.slot_brk[:, 0, :], 0.0, None, ALU.is_equal))

                def scan(n, values, brk, through, backward, total=False):
                    step = -1 if backward else 1
                    op0, op1, start = (ALU.mult, ALU.add, 0.0) if total else (ALU.add, ALU.max, NEG)
                    link(nc.vector.tensor_tensor_scan(out=run[:, ::step], data0=brk[:, ::step],
                                                      data1=values[:, ::step], initial=start, op0=op0, op1=op1))
                    nc.vector.tensor_copy(ends[:, :], split(run)[:, :, :, 0 if backward else P - 1]
                                          .rearrange("r b h -> r (b h)")).then_inc(s["ends"], 1)
                    dve.wait_ge(s["slots"], n + 1)
                    link(nc.vector.memset(over[:, :], start))
                    brk_slot = slot_keep[:, :] if total else c.slot_brk[:, int(backward), :]
                    nc.vector.tensor_tensor_scan(out=over[:, 1:1 + SLOTS][:, ::step], data0=brk_slot[:, ::step],
                                                 data1=ps[0:H, 0:SLOTS][:, ::step], initial=start,
                                                 op0=op0, op1=op1).then_inc(s["over"], 1)
                    dve.wait_ge(s["carried"], n + 1)
                    link(nc.vector.tensor_copy(carry[:, :], ps[0:SB, BANK:BANK + SLOT_BLOCKS * H]))
                    wide = carry[:, :].rearrange("r (b h) -> r b h", h=H).unsqueeze(3)\
                        .to_broadcast([SB, SLOT_BLOCKS, H, P])
                    if total:
                        link(nc.vector.tensor_scalar(more, more, 0.0, None, ALU.is_equal))
                        link(nc.vector.tensor_tensor(out=split(more), in0=split(more), in1=wide, op=ALU.mult))
                        link(nc.vector.tensor_tensor(out=run, in0=run, in1=more, op=ALU.add))
                    else:
                        link(nc.vector.tensor_tensor(out=split(more), in0=over_heads(through), in1=wide, op=ALU.add))
                        link(nc.vector.tensor_tensor(out=run, in0=run, in1=more, op=ALU.max))

                dve.wait_ge(s["breaks"], 2)
                dve.wait_ge(s["rows"], 2)
                scan(0, er, brk_f, c.open_from_start[:, :, :], False)
                scan(1, run, brk_b, c.open_to_end[:, :, :], True)
                link(nc.vector.tensor_tensor(out=run, in0=run, in1=es, op=ALU.max))
                nc.vector.tensor_tensor(out=er, in0=er, in1=run, op=ALU.subtract).then_inc(s["pick"], 1)
                nc.vector.tensor_tensor(out=es, in0=es, in1=run, op=ALU.subtract).then_inc(s["pick"], 1)
                link(nc.vector.tensor_scalar(brk_f, brk_f, 0.0, None, ALU.is_equal))
                link(nc.vector.tensor_copy(split(more), over_heads(c.open_from_start[:, :, :])))
                dve.wait_ge(s["ex"], 2)
                scan(2, er, brk_f, None, False, total=True)
                scan(3, run, brk_b, c.open_to_end[:, :, :], True)
                link(nc.vector.tensor_tensor(out=run, in0=run, in1=es, op=ALU.add))
                link(nc.vector.reciprocal(run, run))
                nc.vector.tensor_tensor(out=es, in0=er, in1=run, op=ALU.mult)\
                  .then_inc(s["alpha"], 1)


def gat_messages(nc, c, g, xl_table, h, inv_deg):
    HOTS = 4
    with ExitStack() as ctx:
        hot = ctx.enter_context(nc.sbuf_tensor(fresh(nc, "hot_a"), [P, HOTS, H, P], F32))
        plain = ctx.enter_context(nc.sbuf_tensor(fresh(nc, "plain"), [P, 2, HALF, P], F32))
        share = ctx.enter_context(nc.sbuf_tensor(fresh(nc, "share"), [P, NODE_TILES * H], F32))
        acc = ctx.enter_context(nc.psum_tensor(fresh(nc, "acc1"), [P, BANKS * BANK], F32))
        assert HOTS == HALF

        with phase(nc, idx_ready=2, used=0, let_go=0, gathered=GROUP, hot=0, plain=0, cleared=0) as (block, s):

            @block.gpsimd
            def _(pool):
                gather_rows(nc, c, pool, c.rows[:, :, 0:XLW], xl_table, s)

            @block.scalar
            def _(act):
                with act.Fori(0, ITERS) as i:
                    for half in range(2):
                        for u in range(half * HALF, (half + 1) * HALF):
                            act.wait_ge(s["gathered"][u], 16 * i + 16)
                        next_indices(nc, c, nc.scalar.copy, i, half, s["idx_ready"], GROUP)

            @block.vector
            def _(dve):
                first_indices(nc, c, s["idx_ready"], GROUP)
                dve.sem_inc(s["used"], GROUP)
                dve.sem_inc(s["hot"], GROUP)
                nc.vector.memset(c.e[:, :, H:H + 1], 1.0)
                with dve.Fori(0, ITERS) as i:
                    for u in range(GROUP):
                        half, r = u // HALF, u % HALF
                        if r == 0:
                            dve.wait_ge(s["used"], GROUP * i + u + HALF)
                            dve.wait_ge(s["hot"], GROUP * i + u + HALF)
                            nc.vector.tensor_tensor(
                                out=plain[:, half, :, :], in0=c.iota[:, :].unsqueeze(1).to_broadcast([P, HALF, P]),
                                in1=c.rel[:, bass.ds(i * GROUP + u, HALF)].unsqueeze(2).to_broadcast([P, HALF, P]),
                                op=ALU.is_equal).then_inc(s["plain"], 1)
                            dve.wait_ge(s["plain"], 2 * i + half + 1)
                        dve.wait_ge(s["used"], GROUP * i + u + 1 + GROUP - HOTS)
                        nc.vector.tensor_tensor(
                            out=hot[:, u % HOTS, :, :],
                            in0=plain[:, half, r:r + 1, :].to_broadcast([P, H, P]),
                            in1=c.e[:, bass.ds(i * GROUP + u, 1), 0:H].rearrange("p a h -> p (a h)").unsqueeze(2)
                            .to_broadcast([P, H, P]), op=ALU.mult).then_inc(s["hot"], 1)

            @block.tensor
            def _(pe):
                clear_sums(nc, c, acc).then_inc(s["cleared"], 1)
                pe.wait_ge(s["cleared"], 1)
                with pe.Fori(0, ITERS) as i:
                    tiles = load_tiles(nc, c, i, GROUP)
                    for u in range(GROUP):
                        pe.wait_ge(s["hot"], GROUP * i + u + 1 + GROUP)
                        pe.wait_ge(s["gathered"][u], 16 * i + 16)
                        for k in range(H):
                            nc.tensor.matmul(acc[:, bass.ds(tiles[u] * C, C)], hot[:, u % HOTS, k, :],
                                             c.rows[:, u, k * C:(k + 1) * C], start=False, stop=False,
                                             skip_group_check=True)
                        nc.tensor.matmul(acc[:, bass.ds(tiles[u] * (H + 1) + SIDE, H + 1)], plain[:, u // HALF, u % HALF, :],
                                         c.e[:, bass.ds(i * GROUP + u, 1), :].rearrange("p a h -> p (a h)"),
                                         start=False, stop=False, skip_group_check=True).then_inc(s["used"], 1)

        with phase(nc, vec=0, mixed=0) as (block, s):

            @block.vector
            def _(dve):
                link = linker(dve, s["vec"])
                side = acc[:, SIDE:SIDE + NODE_TILES * (H + 1)].rearrange("p (t k) -> p t k", k=H + 1)
                link(nc.vector.tensor_scalar(share[:, :].rearrange("p (t h) -> p t h", h=H), side[:, :, 0:H],
                                             -1.0, 1.0 / H, ALU.mult, ALU.add))
                link(nc.vector.tensor_scalar(inv_deg[:, :], side[:, :, H], 1.0, None, ALU.max))
                link(nc.vector.reciprocal(inv_deg[:, :], inv_deg[:, :]))
                link(nc.vector.tensor_tensor(out=h[:, :, :], in0=h[:, :, :],
                                             in1=g.b_out[:, :].unsqueeze(1).to_broadcast([P, NODE_TILES, C]),
                                             op=ALU.add))
                for k in range(H + 1):
                    for t in range(NODE_TILES):
                        if k == 0:
                            nc.vector.tensor_tensor(out=h[:, t, :], in0=acc[:, t * C:(t + 1) * C], in1=h[:, t, :],
                                                    op=ALU.add).then_inc(s["mixed"], 1)
                        else:
                            dve.wait_ge(s["mixed"], (k - 1) * NODE_TILES + t + 1)
                            nc.vector.scalar_tensor_tensor(
                                out=h[:, t, :], in0=g.xl[:, t, (k - 1) * C:k * C],
                                scalar=share[:, t * H + k - 1:t * H + k], in1=h[:, t, :],
                                op0=ALU.mult, op1=ALU.add).then_inc(s["mixed"], 1)


def window_slots(nc, c, src, dst, lo, key, bank, place):
    HALF_W = WSLOTS // 2
    with ExitStack() as ctx:
        def sb(name, shape, dt=F32):
            return ctx.enter_context(nc.sbuf_tensor(fresh(nc, name), shape, dt))

        dst_i = sb("w_dst_i", [P, EDGE_BLOCKS, P], I32)
        src_i = sb("w_src_i", [P, EDGE_BLOCKS, P], I32)
        dst_f = sb("w_dst_f", [P, EDGE_BLOCKS, P])
        lo_i = sb("w_lo_i", [P, EDGE_BLOCKS, P], I32)
        hi_i = sb("w_hi_i", [P, EDGE_BLOCKS, P], I32)
        lo_f = sb("w_lo_f", [P, EDGE_BLOCKS, P])
        hi_f = sb("w_hi_f", [P, EDGE_BLOCKS, P])
        ends_i = sb("w_ends_i", [P, 3, EDGE_BLOCKS], I32)
        ends = sb("w_ends", [P, 3, EDGE_BLOCKS])
        tile_id = sb("w_tile_id", [P, EDGE_BLOCKS])
        real = sb("w_real", [P, EDGE_BLOCKS])
        n_slots = sb("w_n_slots", [P, EDGE_BLOCKS])
        n_before = sb("w_n_before", [P, EDGE_BLOCKS])
        first = sb("w_first", [P, EDGE_BLOCKS])
        end = sb("w_end", [P, EDGE_BLOCKS])
        shift = sb("w_shift", [P, EDGE_BLOCKS])
        shift_w = sb("w_shift_w", [P, EDGE_BLOCKS, P])
        later = sb("w_later", [P, P])
        from_first = sb("w_from_first", [P, EDGE_BLOCKS, WSLOTS])
        pick = sb("w_pick", [P, EDGE_BLOCKS, WSLOTS])
        slot_no = sb("w_slot_no", [P, WSLOTS])
        win_f = sb("w_win_f", [P, WSLOTS])
        rel = sb("w_rel", [P, WSLOTS])
        inside = sb("w_inside", [P, WSLOTS])
        spare_i = sb("w_spare_i", [P, WSLOTS], I32)
        ps = ctx.enter_context(nc.psum_tensor(fresh(nc, "win_ps"), [P, 4, 2, BANK], F32))
        LO, HI, DST, WIN = range(4)

        with phase(nc, pads=0, loads=0, iotas=0, vec=0, pe=0) as (block, s):

            @block.gpsimd
            def _(pool):
                link = linker(pool, s["iotas"])
                link(nc.gpsimd.iota(slot_no[:, :], [[1, WSLOTS]], base=0, channel_multiplier=0,
                                    allow_small_or_imprecise_dtypes=True))
                link(nc.gpsimd.iota(tile_id[:, :], [[P, EDGE_BLOCKS]], base=0, channel_multiplier=1,
                                    allow_small_or_imprecise_dtypes=True))

            @block.sync
            def _(sp):
                sp.wait_ge(s["pads"], 3)
                whole = EDGES_FULL // P * P
                for ap, to in ((dst, dst_i), (src, src_i)):
                    sp.dma_start(to[:, 0:whole // P, :],
                                 ap[0:whole * P].rearrange("(b p e) -> p b e", p=P, e=P)).then_inc(s["loads"], 16)
                    sp.dma_start(to[0:EDGES_FULL - whole, whole // P, :],
                                 ap[whole * P:EDGES_FULL * P].rearrange("(p e) -> p e", e=P)).then_inc(s["loads"], 16)
                    sp.dma_start(to[EDGES_FULL - whole:EDGES_FULL - whole + 1, whole // P, 0:EDGES_REST],
                                 ap[EDGES_FULL * P:E].rearrange("(a e) -> a e", a=1)).then_inc(s["loads"], 16)
                for b in range(EDGE_BLOCKS):
                    low, high = max(b * P, 1), min(b * P + P, EDGE_TILES)
                    sp.dma_start(ends_i[low - b * P:high - b * P, 0, b:b + 1],
                                 bass.AP(dst.tensor, dst.offset + low * P - 1, [[P, high - low], [1, 1]]),
                                 allow_slow_non_contiguous=True)\
                      .then_inc(s["loads"], 16)

            @block.vector
            def _(dve):
                nc.vector.memset(dst_i[:, :, :], WINDOWS * W_NODES).then_inc(s["pads"], 1)
                nc.vector.memset(src_i[:, :, :], 0).then_inc(s["pads"], 1)
                nc.vector.memset(ends_i[:, :, :], -W_NODES).then_inc(s["pads"], 1)
                link = linker(dve, s["vec"])
                dve.wait_ge(s["iotas"], 2)
                link(nc.vector.tensor_scalar(later[:, :], slot_no[:, 0:P], c.part[:, 0:1], None, ALU.is_gt))
                link(nc.vector.tensor_scalar(real[:, :], tile_id[:, :], float(EDGE_TILES), None, ALU.is_lt))
                dve.wait_ge(s["loads"], (6 + EDGE_BLOCKS) * 16)
                link(nc.vector.tensor_copy(ends_i[:, 1, :], dst_i[:, :, P - 1]))
                link(nc.vector.tensor_copy(ends_i[:, 2, :], dst_i[:, :, 0]))
                link(nc.vector.tensor_single_scalar(ends_i[:, :, :], ends_i[:, :, :], W_SHIFT,
                                                    op=ALU.arith_shift_right))
                link(nc.vector.tensor_copy(ends[:, :, :], ends_i[:, :, :]))
                link(nc.vector.scalar_tensor_tensor(out=ends[:, 0, :], in0=ends[:, 0, :], scalar=1.0,
                                                    in1=ends[:, 2, :], op0=ALU.add, op1=ALU.min))
                link(nc.vector.tensor_tensor(out=n_slots[:, :], in0=ends[:, 1, :], in1=ends[:, 0, :], op=ALU.subtract))
                link(nc.vector.scalar_tensor_tensor(out=n_slots[:, :], in0=n_slots[:, :], scalar=1.0, in1=real[:, :],
                                                    op0=ALU.add, op1=ALU.mult))
                link(nc.vector.memset(n_before[:, 0:1], 0.0))
                for b in range(1, EDGE_BLOCKS):
                    link(nc.vector.tensor_tensor(out=n_before[:, b:b + 1], in0=n_before[:, b - 1:b],
                                                 in1=n_slots[:, b - 1:b], op=ALU.add))
                nc.vector.tensor_copy(dst_f[:, :, :], dst_i[:, :, :])
                nc.vector.tensor_single_scalar(lo_i[:, :, :], src_i[:, :, :], P - 1, op=ALU.bitwise_and)
                link(nc.vector.tensor_single_scalar(hi_i[:, :, :], src_i[:, :, :], 7, op=ALU.arith_shift_right))
                nc.vector.tensor_copy(lo_f[:, :, :], lo_i[:, :, :])
                link(nc.vector.tensor_scalar(hi_f[:, :, :], hi_i[:, :, :], float(W_NODES), None, ALU.mult))
                dve.wait_ge(s["pe"], 1)
                link(nc.vector.tensor_copy(first[:, :], ps[:, WIN, 1, 0:EDGE_BLOCKS]))
                link(nc.vector.tensor_tensor(out=end[:, :], in0=first[:, :], in1=n_slots[:, :], op=ALU.add))
                link(nc.vector.tensor_tensor(out=shift[:, :], in0=ends[:, 0, :], in1=first[:, :], op=ALU.subtract))
                for b in range(EDGE_BLOCKS):
                    nc.vector.tensor_scalar(shift_w[:, b, :], c.ones[:, :], shift[:, b:b + 1], None, ALU.mult)
                    link(nc.vector.tensor_scalar(from_first[:, b, :], slot_no[:, :], first[:, b:b + 1], None, ALU.is_ge))
                    link(nc.vector.scalar_tensor_tensor(out=pick[:, b, :], in0=slot_no[:, :], scalar=end[:, b:b + 1],
                                                        in1=from_first[:, b, :], op0=ALU.is_lt, op1=ALU.mult))
                dve.wait_ge(s["pe"], 2)

                def halves(k):
                    return ps[:, k, :, 0:HALF_W]

                def both(ap):
                    return ap.rearrange("p (k s) -> p k s", k=2)
                link(nc.vector.tensor_tensor(out=both(win_f[:, :]), in0=halves(WIN), in1=both(slot_no[:, :]), op=ALU.add))
                link(nc.vector.tensor_scalar(win_f[:, :], win_f[:, :], float(WINDOWS), None, ALU.min))
                link(nc.vector.tensor_copy(spare_i[:, :], slot_no[:, :]))
                link(nc.vector.tensor_single_scalar(spare_i[:, :], spare_i[:, :], SPARE - 1, op=ALU.bitwise_and))
                link(nc.vector.tensor_copy(rel[:, :], spare_i[:, :]))
                link(nc.vector.scalar_tensor_tensor(out=rel[:, :], in0=rel[:, :], scalar=1.0 + WINDOWS, in1=win_f[:, :],
                                                    op0=ALU.add, op1=ALU.subtract))
                link(nc.vector.tensor_tensor(out=inside[:, 1:], in0=win_f[:, 1:], in1=win_f[:, :WSLOTS - 1],
                                             op=ALU.is_equal))
                link(nc.vector.memset(inside[:, 0:1], 0.0))
                link(nc.vector.tensor_tensor(out=rel[:, :], in0=rel[:, :], in1=inside[:, :], op=ALU.mult))
                link(nc.vector.tensor_tensor(out=rel[:, :], in0=rel[:, :], in1=win_f[:, :], op=ALU.add))
                link(nc.vector.tensor_scalar(place[:, :], rel[:, :], float(W_COLS), None, ALU.mult))
                link(nc.vector.tensor_scalar(inside[:, :], win_f[:, :], c.part[:, 0:1], None, ALU.add))
                link(nc.vector.tensor_copy(spare_i[:, :], inside[:, :]))
                link(nc.vector.tensor_single_scalar(spare_i[:, :], spare_i[:, :], BANKS - 1, op=ALU.bitwise_and))
                link(nc.vector.tensor_scalar(bank[:, :], spare_i[:, :], float(BANK), None, ALU.mult))
                link(nc.vector.tensor_scalar(win_f[:, :], win_f[:, :], -float(W_NODES), None, ALU.mult))
                link(nc.vector.tensor_tensor(out=both(rel[:, :]), in0=halves(DST), in1=both(win_f[:, :]), op=ALU.add))
                link(nc.vector.tensor_scalar(inside[:, :], rel[:, :], 0.0, None, ALU.is_ge))
                link(nc.vector.scalar_tensor_tensor(out=inside[:, :], in0=rel[:, :], scalar=float(W_NODES),
                                                    in1=inside[:, :], op0=ALU.is_lt, op1=ALU.mult))
                link(nc.vector.scalar_tensor_tensor(out=both(rel[:, :]), in0=both(rel[:, :]), scalar=1.0,
                                                    in1=halves(HI), op0=ALU.add, op1=ALU.add))
                link(nc.vector.tensor_tensor(out=rel[:, :], in0=rel[:, :], in1=inside[:, :], op=ALU.mult))
                link(nc.vector.tensor_scalar(key[:, :], rel[:, :], -1.0, None, ALU.add))

            @block.scalar
            def _(act):
                act.wait_ge(s["pe"], 2)
                nc.scalar.copy(lo[:, :].rearrange("p (k s) -> p k s", k=2), ps[:, LO, :, 0:HALF_W])

            @block.tensor
            def _(pe):
                V = 2 + 8 + EDGE_BLOCKS - 1
                pe.wait_ge(s["vec"], V)
                before = ps[:, WIN, 1, 0:EDGE_BLOCKS]
                nc.tensor.matmul(before, later[:, :], n_slots[:, :], start=True, stop=False)
                nc.tensor.matmul(before, c.ones[:, :], n_before[:, :], start=False, stop=True).then_inc(s["pe"], 1)
                V += 5 + 2 * EDGE_BLOCKS
                pe.wait_ge(s["vec"], V)
                for b in range(EDGE_BLOCKS):
                    for k, left in ((LO, lo_f), (HI, hi_f), (DST, dst_f), (WIN, shift_w)):
                        for half in range(2):
                            last = nc.tensor.matmul(ps[:, k, half, 0:HALF_W], left[:, b, :],
                                                    pick[:, b, half * HALF_W:(half + 1) * HALF_W], start=b == 0,
                                                    stop=b == EDGE_BLOCKS - 1)
                last.then_inc(s["pe"], 1)


def count_edges(nc, c, lo, key, bank, place, counts):
    G = 16
    HOTS = 8
    QUAD = 4
    LEAD = BANKS - 2
    with ExitStack() as ctx:
        hot_lo = ctx.enter_context(nc.sbuf_tensor(fresh(nc, "hot_lo"), [P, HOTS, P], BF16))
        hot_key = ctx.enter_context(nc.sbuf_tensor(fresh(nc, "hot_key"), [P, HOTS, W_COLS], BF16))
        numbers = ctx.enter_context(nc.sbuf_tensor(fresh(nc, "numbers"), [P, W_COLS], BF16))
        ps = ctx.enter_context(nc.psum_tensor(fresh(nc, "count_ps"), [P, BANKS * BANK], F32))

        def load(table, row, i, engine, high):
            return nc.values_load_multi_w_load_instructions(
                table[row:row + 1, bass.ds(i * G, G)], engines=[engine], min_val=0, max_val=high,
                skip_runtime_bounds_check_because="slots hold windows by construction")[1]

        with phase(nc, numbers=0, cleared=0, hot=0, added=0, taken=0) as (block, s):

            @block.gpsimd
            def _(pool):
                nc.gpsimd.iota(numbers[:, :], [[1, W_COLS]], base=0, channel_multiplier=0,
                               allow_small_or_imprecise_dtypes=True).then_inc(s["numbers"], 1)

            @block.vector
            def _(dve):
                dve.wait_ge(s["numbers"], 1)
                dve.sem_inc(s["added"], HOTS)
                with dve.Fori(0, WSLOTS // G) as i:
                    for u in range(G):
                        if u % QUAD == 0:
                            dve.wait_ge(s["added"], G * i + u + QUAD)
                        nc.vector.tensor_scalar(hot_lo[:, u % HOTS, :], numbers[:, 0:P],
                                                lo[:, bass.ds(i * G + u, 1)], None, ALU.is_equal)
                        nc.vector.tensor_scalar(hot_key[:, u % HOTS, :], numbers[:, :],
                                                key[:, bass.ds(i * G + u, 1)], None, ALU.is_equal)\
                          .then_inc(s["hot"], 1)

            @block.tensor
            def _(pe):
                for b in range(BANKS):
                    last = nc.tensor.matmul(ps[:, b * BANK:(b + 1) * BANK], c.zeros[:, 0:P], c.zeros[:, :],
                                            start=True, stop=True)
                last.then_inc(s["cleared"], 1)
                pe.wait_ge(s["cleared"], 1)
                with pe.Fori(0, WSLOTS // G) as i:
                    now = load(bank, 0, i, mybir.EngineType.PE, (BANKS - 1) * BANK)
                    following = load(bank, 1, i, mybir.EngineType.PE, (BANKS - 1) * BANK)
                    for u in range(G):
                        if u % QUAD == 0:
                            pe.wait_ge(s["hot"], G * i + u + QUAD)
                        if u % 2 == 0:
                            pe.wait_ge(s["taken"], G * i + u + 2)
                        nc.tensor.matmul(ps[:, bass.ds(now[u], W_COLS)], hot_lo[:, u % HOTS, :],
                                         hot_key[:, u % HOTS, :], start=False, stop=False, skip_group_check=True)
                        nc.tensor.matmul(ps[:, bass.ds(following[u], W_COLS)], c.zeros[:, 0:P],
                                         c.zeros[:, 0:W_COLS], start=True, stop=True, skip_group_check=True)\
                          .then_inc(s["added"], 1)

            @block.scalar
            def _(act):
                act.sem_inc(s["taken"], LEAD)
                flat = counts[:, :, :].rearrange("p w c -> p (w c)")
                with act.Fori(0, WSLOTS // G) as i:
                    before = load(bank, BANKS - 1, i, mybir.EngineType.Activation, (BANKS - 1) * BANK)
                    to = load(place, 0, i, mybir.EngineType.Activation, (WINDOWS + SPARE) * W_COLS)
                    for u in range(G):
                        if u % 2 == 0:
                            act.wait_ge(s["added"], G * i + u + 2 + HOTS)
                            act.wait_ge(s["taken"], G * i + u + 2 + LEAD - SPARE)
                        nc.scalar.copy(flat[:, bass.ds(to[u], W_COLS)], ps[:, bass.ds(before[u], W_COLS)])\
                          .then_inc(s["taken"], 1)


def chunks_of_windows():
    size = BANK // W_NODES
    return [(w, min(size, WINDOWS - w)) for w in range(0, WINDOWS, size)]


def gate_row(nc, c, h_wide, node_gate, gate_b, gate_src, v_line):
    with nc.sbuf_tensor(fresh(nc, "v_rows"), [NODE_TILES, P], F32) as v_rows, \
            nc.psum_tensor(fresh(nc, "v_ps"), [NODE_TILES, P], F32) as ps:
        with phase(nc, turned=0, copied=0, stored=0) as (block, s):

            @block.tensor
            def _(pe):
                nc.tensor.transpose(ps[:, :], node_gate[:, :], c.ident[:, :]).then_inc(s["turned"], 1)

            @block.vector
            def _(dve):
                nc.vector.tensor_scalar(gate_src[:, :], h_wide[:, :, C], gate_b, None, ALU.add)
                dve.wait_ge(s["turned"], 1)
                nc.vector.tensor_copy(v_rows[:, :], ps[:, :]).then_inc(s["copied"], 1)

            @block.sync
            def _(sp):
                sp.wait_ge(s["copied"], 1)
                sp.dma_start(v_line.rearrange("(t p) -> t p", p=P), v_rows[:, :]).then_inc(s["stored"], 16)
                sp.wait_ge(s["stored"], 16)


def gated_layer(nc, c, counts, counts_line, work, inv, gate_src, v_line, x, h):
    chunks = chunks_of_windows()
    T = BANK // P
    BUFS = 4
    FIRST = 8
    with ExitStack() as ctx:
        wgt = ctx.enter_context(nc.sbuf_tensor(fresh(nc, "wgt"), [P, BUFS, BANK], F32))
        total_v = ctx.enter_context(nc.sbuf_tensor(fresh(nc, "total_v"), [P, BANK], F32))
        v_all, total, sum_t = (work[:, k, :, :] for k in range(3))
        ps = ctx.enter_context(nc.psum_tensor(fresh(nc, "gated_ps"), [P, 3, 2, BANK], F32))
        SUM, WEIGHTS, TURNED = range(3)

        def tiles_of(q):
            return range(q * T, min(NODE_TILES, (q + 1) * T))

        def step(q, k):
            return q * NODE_TILES + k

        STEPS = step(len(chunks), 0)

        def width(n):
            return chunks[n // NODE_TILES][1] * W_NODES

        def by_vector(n):
            return n % NODE_TILES >= FIRST and (n % NODE_TILES - FIRST) % 2 == 0

        def wait_summed(engine, n):
            mine = sum(by_vector(m) for m in range(n + 1))
            engine.wait_ge(s["added"], n + 1 - mine)
            if mine:
                engine.wait_ge(s["added_v"], mine)

        with phase(nc, v=2, saved=0, tanh=0, exp=0, wgt=0, used=0, added=0, added_v=0, sum_t=0, prod=0, res=0, vec=0)\
                as (block, s):

            @block.sync
            def _(sp):
                for q, (low, size) in enumerate(chunks):
                    if q >= 2:
                        sp.wait_ge(s["tanh"], step(q - 1, 0))
                    sp.dma_start(v_all[:, q % 2, 0:size * W_NODES], rows_of(v_line, low * W_NODES, size * W_NODES))\
                      .then_inc(s["v"][q % 2], 16)
                    sp.dma_start(counts_line[:, low:low + size, :], counts[:, 1 + low:1 + low + size, :])\
                      .then_inc(s["saved"], 16)
                sp.wait_ge(s["saved"], 16 * len(chunks))

            @block.scalar
            def _(act):
                def tanh(n):
                    q, k = n // NODE_TILES, n % NODE_TILES
                    if k == 0:
                        act.wait_ge(s["v"][q % 2], 16 * (q // 2 + 1))
                    if n >= BUFS:
                        act.wait_ge(s["used"], n - BUFS + 1)
                        wait_summed(act, n - BUFS)
                    nc.scalar.activation(wgt[:, n % BUFS, 0:width(n)], v_all[:, q % 2, 0:width(n)], ACT.Tanh,
                                         bias=gate_src[:, k:k + 1]).then_inc(s["tanh"], 1)

                tanh(0)
                for n in range(STEPS):
                    if n + 1 < STEPS:
                        tanh(n + 1)
                    act.wait_ge(s["tanh"], n + 1)
                    nc.scalar.activation(wgt[:, n % BUFS, 0:width(n)], wgt[:, n % BUFS, 0:width(n)], ACT.Exp)\
                      .then_inc(s["exp"], 1)

            @block.gpsimd
            def _(pool):
                done = 0
                for n in range(STEPS):
                    q, k = n // NODE_TILES, n % NODE_TILES
                    if by_vector(n):
                        continue
                    pool.wait_ge(s["wgt"], n + 1)
                    to = total[:, q % 2, 0:width(n)]
                    if k == 0:
                        if q >= 2:
                            pool.wait_ge(s["prod"], q - 1)
                        nc.gpsimd.tensor_copy(to, wgt[:, n % BUFS, 0:width(n)]).then_inc(s["added"], 1)
                    else:
                        pool.wait_ge(s["added"], done)
                        nc.gpsimd.tensor_tensor(out=to, in0=to, in1=wgt[:, n % BUFS, 0:width(n)], op=ALU.add)\
                          .then_inc(s["added"], 1)
                    done += 1

            @block.tensor
            def _(pe):
                def finish(q):
                    pe.wait_ge(s["sum_t"], q + 1)
                    wait_summed(pe, step(q + 1, 0) - 1)
                    if q >= 2:
                        pe.wait_ge(s["res"], q - 1)
                    for t in tiles_of(q):
                        at = slice(t % T * P, (t % T + 1) * P)
                        for k, sums in enumerate((total[:, q % 2, at], total_v[:, at])):
                            nc.tensor.matmul(ps[:, WEIGHTS, q % 2, t % T:t % T + 1], sums, c.ones[:, 0:1],
                                             start=k == 0, stop=k == 1)
                        last = nc.tensor.transpose(ps[:, TURNED, q % 2, at], sum_t[:, q % 2, at], c.ident[:, :])
                    last.then_inc(s["prod"], 1)

                for q in range(len(chunks)):
                    for k in range(NODE_TILES):
                        n = step(q, k)
                        pe.wait_ge(s["wgt"], n + 1)
                        if k == 0 and q >= 2:
                            pe.wait_ge(s["sum_t"], q - 1)
                        nc.tensor.matmul(ps[:, SUM, q % 2, 0:width(n)], h[:, k, :], wgt[:, n % BUFS, 0:width(n)],
                                         start=k == 0, stop=k == NODE_TILES - 1).then_inc(s["used"], 1)
                        if k == 6 and q > 0:
                            finish(q - 1)
                finish(len(chunks) - 1)

            @block.vector
            def _(dve):
                link = linker(dve, s["vec"])
                link(nc.vector.scalar_tensor_tensor(out=x[:, :, :], in0=h[:, :, :], scalar=L0_EPS, in1=x[:, :, :],
                                                    op0=ALU.mult, op1=ALU.add))

                def copy_sums(q):
                    dve.wait_ge(s["used"], step(q + 1, 0))
                    if q >= 2:
                        dve.wait_ge(s["prod"], q - 1)
                    size = chunks[q][1] * W_NODES
                    nc.vector.tensor_copy(sum_t[:, q % 2, 0:size], ps[:, SUM, q % 2, 0:size]).then_inc(s["sum_t"], 1)

                def result(q):
                    tiles = tiles_of(q)
                    own = inv[:, tiles[0]:tiles[-1] + 1]
                    dve.wait_ge(s["prod"], q + 1)
                    link(nc.vector.tensor_scalar(own, ps[:, WEIGHTS, q % 2, 0:len(tiles)], 1e-30, None, ALU.max))
                    link(nc.vector.reciprocal(own, own))
                    link(nc.vector.tensor_scalar(own, own, 1.0 - L0_EPS, None, ALU.mult))
                    for t in tiles:
                        last = nc.vector.scalar_tensor_tensor(
                            out=x[:, t, :], in0=ps[:, TURNED, q % 2, t % T * P:(t % T + 1) * P],
                            scalar=inv[:, t:t + 1], in1=x[:, t, :], op0=ALU.mult, op1=ALU.add)
                    last.then_inc(s["res"], 1)

                done = 0
                for q, (low, size) in enumerate(chunks):
                    for k in range(NODE_TILES):
                        n = step(q, k)
                        dve.wait_ge(s["exp"], n + 1)
                        both = wgt[:, n % BUFS, 0:width(n)].rearrange("p (w d) -> p w d", d=W_NODES)
                        nc.vector.tensor_tensor(
                            out=both, in0=both, in1=counts[:, 1 + low:1 + low + size, k * W_NODES:(k + 1) * W_NODES],
                            op=ALU.mult).then_inc(s["wgt"], 1)
                        if by_vector(n):
                            to = total_v[:, 0:width(n)]
                            dve.wait_ge(s["wgt"], n + 1)
                            if k == FIRST:
                                if q > 0:
                                    dve.wait_ge(s["prod"], q)
                                nc.vector.tensor_copy(to, wgt[:, n % BUFS, 0:width(n)]).then_inc(s["added_v"], 1)
                            else:
                                dve.wait_ge(s["added_v"], done)
                                nc.vector.tensor_tensor(out=to, in0=to, in1=wgt[:, n % BUFS, 0:width(n)], op=ALU.add)\
                                  .then_inc(s["added_v"], 1)
                            done += 1
                        if k == 3 and q > 0:
                            copy_sums(q - 1)
                        if k == 12 and q > 0:
                            result(q - 1)
                copy_sums(len(chunks) - 1)
                result(len(chunks) - 1)


def dense_layer(nc, c, counts, work, h, inv_deg, x, sage=None, table=None, counts_line=None):
    chunks = chunks_of_windows()
    T = BANK // P
    BUFS = 4
    with ExitStack() as ctx:
        cnt = ctx.enter_context(nc.sbuf_tensor(fresh(nc, "cnt"), [P, BUFS, BANK], F32))
        sum_t, h_t, res = (work[:, k, :, :] for k in range(3))
        ps = ctx.enter_context(nc.psum_tensor(fresh(nc, "dense_ps"), [P, 4, 2, BANK], F32))
        SUM, TURNED, OWN, NEIGH = range(4)

        def tiles_of(q):
            return range(q * T, min(NODE_TILES, (q + 1) * T))

        def step(q, k):
            return q * NODE_TILES + k

        with phase(nc, cast_a=0, cast_d=0, used=0, summed=0, sum_t=0, turned=0, h_t=0, prod=0, vec=0, res=0,
                   stored=2, restored=len(chunks)) as (block, s):

            def cast(engine, copy, q, k, done):
                n = step(q, k)
                low, size = chunks[q]
                if k < 2 and counts_line is not None:
                    engine.wait_ge(s["restored"][q], 16)
                if n >= BUFS:
                    engine.wait_ge(s["used"], n - BUFS + 1)
                copy(cnt[:, n % BUFS, 0:size * W_NODES].rearrange("p (w d) -> p w d", d=W_NODES),
                     counts[:, 1 + low:1 + low + size, k * W_NODES:(k + 1) * W_NODES]).then_inc(s[done], 1)

            @block.tensor
            def _(pe):
                def turn(q):
                    if q >= 2:
                        pe.wait_ge(s["h_t"], q - 1)
                    for t in tiles_of(q):
                        last = nc.tensor.transpose(ps[:, TURNED, q % 2, t % T * P:(t % T + 1) * P], h[:, t, :],
                                                   c.ident[:, :])
                    last.then_inc(s["turned"], 1)

                def finish(q):
                    pe.wait_ge(s["sum_t"], q + 1)
                    if sage is not None:
                        pe.wait_ge(s["h_t"], q + 1)
                    if q >= 2:
                        pe.wait_ge(s["res"], q - 1)
                    for t in tiles_of(q):
                        at = slice(t % T * P, (t % T + 1) * P)
                        if sage is None:
                            last = nc.tensor.transpose(ps[:, NEIGH, q % 2, at], sum_t[:, q % 2, at], c.ident[:, :])
                        else:
                            nc.tensor.matmul(ps[:, OWN, q % 2, at], h_t[:, q % 2, at], sage[0], start=True, stop=True)
                            last = nc.tensor.matmul(ps[:, NEIGH, q % 2, at], sum_t[:, q % 2, at], sage[1],
                                                    start=True, stop=True)
                    last.then_inc(s["prod"], 1)

                for q, (low, size) in enumerate(chunks):
                    for k in range(NODE_TILES):
                        n = step(q, k)
                        if n % 2:
                            pe.wait_ge(s["cast_d"], n // 2 + 1)
                        else:
                            pe.wait_ge(s["cast_a"], n // 2 + 1)
                        if k == 0 and q >= 2:
                            pe.wait_ge(s["sum_t"], q - 1)
                        last = nc.tensor.matmul(ps[:, SUM, q % 2, 0:size * W_NODES], h[:, k, :],
                                                cnt[:, n % BUFS, 0:size * W_NODES], start=k == 0,
                                                stop=k == NODE_TILES - 1)
                        last.then_inc(s["used"], 1)
                        if k == 4 and sage is not None:
                            turn(q)
                        if k == 12 and q > 0:
                            finish(q - 1)
                finish(len(chunks) - 1)

            @block.scalar
            def _(act):
                def copy_sums(q):
                    act.wait_ge(s["used"], step(q + 1, 0))
                    if q >= 2:
                        act.wait_ge(s["prod"], q - 1)
                    size = chunks[q][1] * W_NODES
                    nc.scalar.copy(sum_t[:, q % 2, 0:size], ps[:, SUM, q % 2, 0:size]).then_inc(s["sum_t"], 1)

                for q in range(len(chunks)):
                    for k in range(NODE_TILES):
                        if step(q, k) % 2 == 0:
                            cast(act, nc.scalar.copy, q, k, "cast_a")
                        if k == 7 and q > 0:
                            copy_sums(q - 1)
                        if k == 15 and sage is not None:
                            act.wait_ge(s["turned"], q + 1)
                            size = len(tiles_of(q)) * P
                            nc.scalar.copy(h_t[:, q % 2, 0:size], ps[:, TURNED, q % 2, 0:size]).then_inc(s["h_t"], 1)
                copy_sums(len(chunks) - 1)

            @block.vector
            def _(dve):
                link = linker(dve, s["vec"])

                def result(q):
                    tiles = tiles_of(q)
                    dve.wait_ge(s["prod"], q + 1)
                    if sage is None:
                        for t in tiles:
                            last = nc.vector.scalar_tensor_tensor(
                                out=x[:, t, :], in0=ps[:, NEIGH, q % 2, t % T * P:(t % T + 1) * P],
                                scalar=inv_deg[:, t:t + 1], in1=x[:, t, :], op0=ALU.mult, op1=ALU.add)
                        last.then_inc(s["res"], 1)
                        return
                    if table is not None and q >= 2:
                        dve.wait_ge(s["stored"][q % 2], 16 * (q // 2))
                    out = res[:, q % 2, 0:len(tiles) * P].rearrange("p (t c) -> p t c", c=C)
                    link(nc.vector.tensor_tensor(
                        out=out, in0=ps[:, OWN, q % 2, 0:len(tiles) * P].rearrange("p (t c) -> p t c", c=C),
                        in1=sage[2].unsqueeze(1).to_broadcast([P, len(tiles), C]), op=ALU.add))
                    for t in tiles:
                        last = nc.vector.scalar_tensor_tensor(
                            out=out[:, t % T, :], in0=ps[:, NEIGH, q % 2, t % T * P:(t % T + 1) * P],
                            scalar=inv_deg[:, t:t + 1], in1=out[:, t % T, :], op0=ALU.mult, op1=ALU.add)
                    link(last)
                    if table is not None:
                        nc.vector.tensor_scalar(out, out, 0.0, None, ALU.max).then_inc(s["res"], 1)
                    else:
                        to = x[:, tiles[0]:tiles[-1] + 1, :]
                        nc.vector.tensor_tensor(out=to, in0=to, in1=out, op=ALU.add).then_inc(s["res"], 1)

                for q in range(len(chunks)):
                    for k in range(NODE_TILES):
                        if step(q, k) % 2:
                            cast(dve, nc.vector.tensor_copy, q, k, "cast_d")
                        if k == 18 and q > 0:
                            result(q - 1)
                result(len(chunks) - 1)

            @block.sync
            def _(sp):
                if counts_line is not None:
                    for q, (low, size) in enumerate(chunks):
                        sp.dma_start(counts[:, 1 + low:1 + low + size, :], counts_line[:, low:low + size, :])\
                          .then_inc(s["restored"][q], 16)
                if table is not None:
                    for q in range(len(chunks)):
                        tiles = tiles_of(q)
                        sp.wait_ge(s["res"], q + 1)
                        sp.dma_start(table[tiles[0] * P:(tiles[-1] + 1) * P, :].rearrange("(t p) c -> p t c", p=P),
                                     res[:, q % 2, 0:len(tiles) * P].rearrange("p (t c) -> p t c", c=C))\
                          .then_inc(s["stored"][q % 2], 16)
                    for half in range(2):
                        sp.wait_ge(s["stored"][half], 16 * ((len(chunks) + 1 - half) // 2))


def graph_layers(nc, x_in, src, dst, gate_w, gate_b, Wl, bl, Wr, br, att, bias, ln_g, ln_b,
                 W_self1, W_neigh1, b1, W_self2, W_neigh2, b2, out):
    rel_rows = nc.dram_tensor("rel_rows", ((SLOTS + WIDE) * P,), BF16, kind="Internal").ap()
    dst_line = nc.dram_tensor("dst_line", (SLOTS * P + 2,), F32, kind="Internal").ap()
    v_line = nc.dram_tensor("v_line", (NODE_TILES * P,), F32, kind="Internal").ap()
    counts_line = nc.dram_tensor("counts_line", (P, WINDOWS, W_COLS), U16, kind="Internal").ap()
    h_table = nc.dram_tensor("h_table", (NODE_TILES * P, C), F32, kind="Internal").ap()
    xl_tables = [nc.dram_tensor(f"xl_table{k}", (NODE_TILES * P, XLW), F32, kind="Internal").ap()
                 for k in range(LAYERS)]

    with ExitStack() as ctx, ExitStack() as early:
        def sb(name, shape, dt=F32, within=ctx):
            return within.enter_context(nc.sbuf_tensor(fresh(nc, name), shape, dt))

        x = sb("x", [P, NODE_TILES, C])
        h_wide = sb("h", [P, NODE_TILES, C + 1])
        h = h_wide[:, :, 0:C]
        inv_deg = sb("inv_deg", [P, NODE_TILES])
        weights = [sb(f"sage_w{k}", [P, C]) for k in range(4)]
        biases = [sb(f"sage_b{k}", [P, C]) for k in range(2)]

        class c:
            iota = sb("iota", [P, P])
            part = sb("part", [P, 1])
            ident = sb("ident", [P, P])
            ones = sb("ones", [P, P])
            zeros = sb("zeros", [P, BANK], BF16)

        with phase(nc, clear=0, loads=0) as (block, s):

            @block.vector
            def _(dve):
                nc.vector.memset(x[:, :, :], 0.0).then_inc(s["clear"], 1)

            @block.sync
            def _(sp):
                sp.wait_ge(s["clear"], 1)
                sp.dma_start(x[:, 0:NODES_FULL, :], x_in[0:NODES_FULL * P, :].rearrange("(t p) c -> p t c", p=P))\
                  .then_inc(s["loads"], 16)
                sp.dma_start(x[0:NODES_REST, NODES_FULL, :], x_in[NODES_FULL * P:N, :]).then_inc(s["loads"], 16)
                for ap, to in zip((W_self1, W_neigh1, W_self2, W_neigh2), weights):
                    sp.dma_start(to[:, :], ap).then_inc(s["loads"], 16)
                for ap, to in zip((b1, b2), biases):
                    sp.dma_start(to[:, :], rows_of(ap, 0, C)).then_inc(s["loads"], 16)
                sp.wait_ge(s["loads"], 8 * 16)

        with phase(nc, iotas=0) as (block, s):

            @block.gpsimd
            def _(pool):
                link = linker(pool, s["iotas"])
                link(nc.gpsimd.iota(c.iota[:, :], [[1, P]], base=0, channel_multiplier=0,
                                    allow_small_or_imprecise_dtypes=True))
                link(nc.gpsimd.iota(c.part[:, :], [[1, 1]], base=0, channel_multiplier=1,
                                    allow_small_or_imprecise_dtypes=True))

            @block.vector
            def _(dve):
                nc.vector.memset(c.ones[:, :], 1.0)
                nc.vector.memset(c.zeros[:, :], 0.0)
                dve.wait_ge(s["iotas"], 2)
                nc.vector.tensor_scalar(c.ident[:, :], c.iota[:, :], c.part[:, 0:1], None, ALU.is_equal)

        assert E < 1 << 16
        with ExitStack() as part:
            tables = sb("tables", [P, 4, WSLOTS], within=part)
            lo, key = tables[:, 0, :], tables[:, 1, :]
            bank, place = tables[:, 2, :].bitcast(I32), tables[:, 3, :].bitcast(I32)
            flat = tables[:, :, :].rearrange("p k s -> p (k s)")
            work = flat[:, 0:3 * 2 * BANK].rearrange("p (k b s) -> p k b s", k=3, b=2)
            inv = flat[:, 3 * 2 * BANK:3 * 2 * BANK + NODE_TILES]
            window_slots(nc, c, src, dst, lo, key, bank, place)
            counts = sb("counts", [P, 1 + WINDOWS + SPARE, W_COLS], U16, within=part)
            count_edges(nc, c, lo, key, bank, place, counts)

            gate_src = sb("gate_src", [P, NODE_TILES], within=part)
            with ExitStack() as inner:
                gate_w_all = sb("gate_w_all", [P, 2 * C], within=inner)
                gate_b_all = sb("gate_b_all", [P, 1], within=inner)
                node_gate = sb("node_gate", [P, NODE_TILES], within=inner)
                with phase(nc, loads=0) as (block, s):

                    @block.sync
                    def _(sp):
                        sp.dma_start(gate_w_all[:, :], rows_of(gate_w, 0, 2 * C)).then_inc(s["loads"], 16)
                        sp.dma_start(gate_b_all[:, :], rows_of(gate_b, 0, 1)).then_inc(s["loads"], 16)
                        sp.wait_ge(s["loads"], 32)

                norm_relu(nc, c, x, h, dot=(gate_w_all, h_wide, node_gate))
                gate_row(nc, c, h_wide, node_gate, gate_b_all[:, 0:1], gate_src, v_line)
            gated_layer(nc, c, counts, counts_line, work, inv, gate_src, v_line, x, h)

        c.rel = sb("rel", [P, SLOTS], within=early)
        c.idx = sb("idx", [P, SLOTS + WIDE], I32, within=early)
        c.idx_now = sb("idx_now", [P, WIDE], I32, within=early)
        c.slot_tile = sb("slot_tile", [1, SLOTS], I32, within=early)
        c.valid = sb("valid", [P, SLOTS], within=early)
        c.invalid_neg = sb("invalid_neg", [P, SLOTS], within=early)
        c.brk_before = sb("brk_before", [SB, SLOT_BLOCKS, P], within=early)
        c.brk_after = sb("brk_after", [SB, SLOT_BLOCKS, P], within=early)
        c.open_from_start = sb("open_from_start", [SB, SLOT_BLOCKS, P], within=early)
        c.open_to_end = sb("open_to_end", [SB, SLOT_BLOCKS, P], within=early)
        c.slot_brk = sb("slot_brk", [H, 2, SLOTS], within=early)
        make_slots(nc, c, src, dst, rel_rows, dst_line)

        norm_relu(nc, c, x, h)
        with ExitStack() as part:
            c.rows = sb("rows", [P, GROUP, XRW], within=part)
            c.e = sb("e", [P, SLOTS, H + 1], within=part)
            c.e_self = sb("e_self", [P, SLOTS, H], within=part)

            class g:
                xl = sb("xl", [P, NODE_TILES, XLW], within=part)
                xr = sb("xr", [P, NODE_TILES, XRW], within=part)
                w = [sb(f"w{k}", [P, XLW], within=part) for k in range(2)]
                att = sb("att_all", [P, HC], within=part)
                b_sum = sb("b_sum", [P, XLW], within=part)
                b_out = sb("b_out", [P, C], within=part)
                gain = sb("gain", [P, C], within=part)
                shift = sb("shift_ln", [P, C], within=part)

            for layer in range(LAYERS):
                gat_weights(nc, c, g, layer, Wl, Wr, bl, br, att, bias, ln_g, ln_b)
                gat_tables(nc, c, g, h, xl_tables[layer])
                gat_scores(nc, c, g, rel_rows, xl_tables[layer])
                gat_softmax(nc, c, g.xr)
                gat_messages(nc, c, g, xl_tables[layer], h, inv_deg)
                norm_relu(nc, c, h, h, gain=g.gain[:, :], shift=g.shift[:, :])

        with phase(nc, vec=0) as (block, s):

            @block.vector
            def _(dve):
                nc.vector.tensor_tensor(out=x[:, :, :], in0=x[:, :, :], in1=h[:, :, :], op=ALU.add)

        early.close()
        work = sb("work", [P, 3, 2, BANK])
        counts = sb("counts", [P, 1 + WINDOWS, W_COLS], U16)

        norm_relu(nc, c, x, h)
        dense_layer(nc, c, counts, work, h, inv_deg, x, counts_line=counts_line)

        norm_relu(nc, c, x, h)
        for k in range(2):
            dense_layer(nc, c, counts, work, h, inv_deg, x,
                        sage=(weights[2 * k][:, :], weights[2 * k + 1][:, :], biases[k][:, :]),
                        table=h_table if k == 0 else None)
            with phase(nc, moved=0) as (block, s):

                @block.sync
                def _(sp):
                    if k == 0:
                        sp.dma_start(h[:, :, :], h_table.rearrange("(t p) c -> p t c", p=P)).then_inc(s["moved"], 16)
                        sp.wait_ge(s["moved"], 16)
                    else:
                        sp.dma_start(out[0:NODES_FULL * P, :].rearrange("(t p) c -> p t c", p=P),
                                     x[:, 0:NODES_FULL, :]).then_inc(s["moved"], 16)
                        sp.dma_start(out[NODES_FULL * P:N, :], x[0:NODES_REST, NODES_FULL, :])\
                          .then_inc(s["moved"], 16)
                        sp.wait_ge(s["moved"], 32)


NAMES = ["x", "src", "dst", "L0_gnn_gate_w", "L0_gnn_gate_b", "L1_gnn_Wl", "L1_gnn_bl", "L1_gnn_Wr", "L1_gnn_br",
         "L1_gnn_att", "L1_gnn_bias", "L1_gnn_ln_g", "L1_gnn_ln_b", "L3_gnn_W_self1", "L3_gnn_W_neigh1", "L3_gnn_b1",
         "L3_gnn_W_self2", "L3_gnn_W_neigh2", "L3_gnn_b2"]


def kernel(**inputs):
    import numpy as np
    import concourse.bacc as bacc
    from concourse.bass_utils import run_bass_kernel_spmd

    nc = bacc.Bacc("TRN2", target_bir_lowering=False, num_devices=1)
    arrays, args = {}, []
    for name in NAMES:
        a = np.ascontiguousarray(inputs[name])
        arrays[f"in_{name}"] = a
        args.append(nc.dram_tensor(f"in_{name}", a.shape, mybir.dt.from_np(a.dtype), kind="ExternalInput").ap())
    args.append(nc.dram_tensor("out", (N, C), F32, kind="ExternalOutput").ap())
    graph_layers(nc, *args)
    result = run_bass_kernel_spmd(nc, [arrays], core_ids=[0])
    return result.results[0]["out"]
```
